# Optimizing a Trainium2 kernel written in Bass

```python
import numpy as np
import jax
import jax.numpy as jnp

def _softmax(x, axis=-1):
    return jax.nn.softmax(x, axis=axis)

def _gelu(x):
    return jax.nn.gelu(x, approximate=True)

def _silu(x):
    return jax.nn.silu(x)

def _sigmoid(x):
    return jax.nn.sigmoid(x)

def _layernorm(x, axis=-1, eps=1e-05):
    m = jnp.mean(x, axis=axis, keepdims=True)
    v = jnp.var(x, axis=axis, keepdims=True)
    return (x - m) / jnp.sqrt(v + eps)

def _scatter_add(tgt, idx, src, axis=0):
    return tgt.at[idx].add(src)

def _segment_sum(src, seg, n):
    return jax.ops.segment_sum(src, seg, n)
kernel_name = 'mk_lm_tower_d1_tok_ids256_r4_54f523'

def setup_inputs(seed: int=0):
    np.random.seed(seed)
    _w = jnp.asarray

    def _rec_inputs():
        import jax
        import jax.numpy as jnp
        _rk = jax.random.key(seed)
        x = jax.random.randint(jax.random.fold_in(_rk, 1), (32, 512), 0, 127998, jnp.int32)
        return x
    x = _rec_inputs()

    def _L0_tok_setup():
        import jax, jax.numpy as jnp
        import numpy as np
        VOCAB = 32000
        HIDDEN = 512
        BATCH, SEQ = (4, 1024)
        key = jax.random.key(seed)
        k_ids, k_tab = jax.random.split(key)
        input_ids = jax.random.randint(k_ids, (BATCH, SEQ), 0, VOCAB, dtype=jnp.int32)
        ple_table = jax.random.normal(k_tab, (VOCAB, HIDDEN), dtype=jnp.float32)
        return {'input_ids': input_ids, 'ple_table': ple_table, 'layer_idx': 3, 'ple_dim': 64}
    _L0_tok_all = _L0_tok_setup()
    _L0_tok_in = {k: v for k, v in _L0_tok_all.items() if k in ('ple_table',)}
    del _L0_tok_all

    def _L0_attn_setup():
        import jax, jax.numpy as jnp
        import numpy as np

        def softcap(x, a=10.0):
            return a * jnp.tanh(x / a)
        key = jax.random.key(seed)
        B, T, D = (4, 512, 64)
        ks = jax.random.split(key, 5)
        w = lambda k, s: jax.random.normal(k, s, dtype=jnp.float32) * 0.02
        return {'x': jax.random.normal(ks[0], (B, T, D), dtype=jnp.float32), 'Wq': w(ks[1], (D, D)), 'bq': jnp.zeros((D,), jnp.float32), 'Wk': w(ks[2], (D, D)), 'bk': jnp.zeros((D,), jnp.float32), 'Wv': w(ks[3], (D, D)), 'bv': jnp.zeros((D,), jnp.float32), 'Wg': w(ks[4], (D, 3 * D)), 'bg': jnp.zeros((3 * D,), jnp.float32), 'input_bias': -jnp.ones((D,), jnp.float32), 'norm_scale': jnp.ones((D,), jnp.float32)}
    _L0_attn_all = _L0_attn_setup()
    _L0_attn_in = {k: v for k, v in _L0_attn_all.items() if k in ('Wq', 'bq', 'Wk', 'bk', 'Wv', 'bv', 'Wg', 'bg', 'input_bias', 'norm_scale')}
    del _L0_attn_all

    def _L0_ffn_setup():
        import jax, jax.numpy as jnp
        import numpy as np
        B, T, C = (64, 96, 64)
        NH, NKV = (4, 2)
        HD = C // NH
        NREP = NH // NKV
        NE, TOPK = (8, 2)
        HID = int(8 / 3 * C)
        EPS_RMS = 1e-06

        def _rope_tables(t_len):
            inv_freq = 1.0 / 10000.0 ** (np.arange(0, HD, 2, dtype=np.float32) / HD)
            t = np.arange(t_len, dtype=np.float32)
            freqs = np.outer(t, inv_freq)
            emb = np.concatenate([freqs, freqs], axis=-1)
            return (jnp.asarray(np.cos(emb)), jnp.asarray(np.sin(emb)))

        def _rotate_half(x):
            h = x.shape[-1] // 2
            return jnp.concatenate([-x[..., h:], x[..., :h]], axis=-1)

        def _rmsnorm(v, w):
            return v * jax.lax.rsqrt(jnp.mean(v * v, axis=-1, keepdims=True) + EPS_RMS) * w
        key = jax.random.key(seed)
        ks = jax.random.split(key, 10)
        s = lambda k, shape: jax.random.normal(k, shape, jnp.float32) * 0.02
        return {'x': jax.random.normal(ks[0], (B, T, C), jnp.float32), 'ln1_w': jnp.ones((C,), jnp.float32), 'ln2_w': jnp.ones((C,), jnp.float32), 'wq': s(ks[1], (NH * HD, C)), 'wk': s(ks[2], (NKV * HD, C)), 'wv': s(ks[3], (NKV * HD, C)), 'wo': s(ks[4], (C, C)), 'router_w': s(ks[5], (NE, C)), 'w1': s(ks[6], (NE, HID, C)), 'w2': s(ks[7], (NE, C, HID)), 'w3': s(ks[8], (NE, HID, C))}
    _L0_ffn_all = _L0_ffn_setup()
    _L0_ffn_in = {k: v for k, v in _L0_ffn_all.items() if k in ('ln1_w', 'ln2_w', 'wq', 'wk', 'wv', 'wo', 'router_w', 'w1', 'w2', 'w3')}
    del _L0_ffn_all
    return {'x': x, 'L0_tok_ple_table': _L0_tok_in['ple_table'], 'L0_attn_Wq': _L0_attn_in['Wq'], 'L0_attn_bq': _L0_attn_in['bq'], 'L0_attn_Wk': _L0_attn_in['Wk'], 'L0_attn_bk': _L0_attn_in['bk'], 'L0_attn_Wv': _L0_attn_in['Wv'], 'L0_attn_bv': _L0_attn_in['bv'], 'L0_attn_Wg': _L0_attn_in['Wg'], 'L0_attn_bg': _L0_attn_in['bg'], 'L0_attn_input_bias': _L0_attn_in['input_bias'], 'L0_attn_norm_scale': _L0_attn_in['norm_scale'], 'L0_ffn_ln1_w': _L0_ffn_in['ln1_w'], 'L0_ffn_ln2_w': _L0_ffn_in['ln2_w'], 'L0_ffn_wq': _L0_ffn_in['wq'], 'L0_ffn_wk': _L0_ffn_in['wk'], 'L0_ffn_wv': _L0_ffn_in['wv'], 'L0_ffn_wo': _L0_ffn_in['wo'], 'L0_ffn_router_w': _L0_ffn_in['router_w'], 'L0_ffn_w1': _L0_ffn_in['w1'], 'L0_ffn_w2': _L0_ffn_in['w2'], 'L0_ffn_w3': _L0_ffn_in['w3']}

def reference(x, L0_tok_ple_table, L0_attn_Wq, L0_attn_bq, L0_attn_Wk, L0_attn_bk, L0_attn_Wv, L0_attn_bv, L0_attn_Wg, L0_attn_bg, L0_attn_input_bias, L0_attn_norm_scale, L0_ffn_ln1_w, L0_ffn_ln2_w, L0_ffn_wq, L0_ffn_wk, L0_ffn_wv, L0_ffn_wo, L0_ffn_router_w, L0_ffn_w1, L0_ffn_w2, L0_ffn_w3):
    import jax
    import jax.numpy as jnp

    def _L0_tok_ref(input_ids, ple_table, layer_idx, ple_dim):
        import jax, jax.numpy as jnp
        import numpy as np
        VOCAB = 32000
        HIDDEN = 512
        BATCH, SEQ = (4, 1024)
        start = layer_idx * ple_dim
        layer_slice = jax.lax.dynamic_slice_in_dim(ple_table, start, ple_dim, axis=1)
        return layer_slice[input_ids].astype(jnp.float32)

    def _L0_attn_ref(x, Wq, bq, Wk, bk, Wv, bv, Wg, bg, input_bias, norm_scale):
        import jax, jax.numpy as jnp
        import numpy as np

        def softcap(x, a=10.0):
            return a * jnp.tanh(x / a)
        B, T, D = x.shape
        inv_sqrt_d = 1.0 / jnp.sqrt(jnp.asarray(D, jnp.float32))
        q = x @ Wq + bq
        k = (x @ Wk + bk) * inv_sqrt_d
        v = x @ Wv + bv
        gates = x @ Wg + bg
        i_pre, f_pre, o_pre = jnp.split(gates, 3, axis=-1)
        log_i = softcap(i_pre + input_bias)
        log_f = -jax.nn.softplus(f_pre)

        def step(carry, inp):
            M, n, m = carry
            qt, kt, vt, li, lf, op = inp
            m_next = jnp.maximum(lf + m, li)
            i_s = jnp.exp(li - m_next)
            f_s = jnp.exp(lf + m - m_next)
            M = f_s[:, :, None] * M + i_s[:, :, None] * (vt[:, :, None] * kt[:, None, :])
            n = f_s * n + i_s * kt
            h_raw = jnp.einsum('bij,bj->bi', M, qt)
            denom = jnp.maximum(jnp.abs(jnp.einsum('bi,bi->b', n, qt))[:, None], 1e-06)
            h = jax.nn.sigmoid(op) * (h_raw / denom)
            return ((M, n, m_next), h)
        M0 = jnp.zeros((B, D, D), jnp.float32)
        n0 = jnp.zeros((B, D), jnp.float32)
        m0 = jnp.zeros((B, D), jnp.float32)
        xs = tuple((jnp.swapaxes(a, 0, 1) for a in (q, k, v, log_i, log_f, o_pre)))
        _, hs = jax.lax.scan(step, (M0, n0, m0), xs)
        out = jnp.swapaxes(hs, 0, 1)
        rms = jnp.sqrt(jnp.mean(out * out, axis=-1, keepdims=True) + 1e-08)
        return out / rms * norm_scale

    def _L0_ffn_ref(x, ln1_w, ln2_w, wq, wk, wv, wo, router_w, w1, w2, w3):
        import jax, jax.numpy as jnp
        import numpy as np
        B, T, C = (64, 96, 64)
        NH, NKV = (4, 2)
        HD = C // NH
        NREP = NH // NKV
        NE, TOPK = (8, 2)
        HID = int(8 / 3 * C)
        EPS_RMS = 1e-06

        def _rope_tables(t_len):
            inv_freq = 1.0 / 10000.0 ** (np.arange(0, HD, 2, dtype=np.float32) / HD)
            t = np.arange(t_len, dtype=np.float32)
            freqs = np.outer(t, inv_freq)
            emb = np.concatenate([freqs, freqs], axis=-1)
            return (jnp.asarray(np.cos(emb)), jnp.asarray(np.sin(emb)))

        def _rotate_half(x):
            h = x.shape[-1] // 2
            return jnp.concatenate([-x[..., h:], x[..., :h]], axis=-1)

        def _rmsnorm(v, w):
            return v * jax.lax.rsqrt(jnp.mean(v * v, axis=-1, keepdims=True) + EPS_RMS) * w
        Bx, Tx, Cx = x.shape
        h = _rmsnorm(x, ln1_w)
        q = (h @ wq.T).reshape(Bx, Tx, NH, HD).transpose(0, 2, 1, 3)
        k = (h @ wk.T).reshape(Bx, Tx, NKV, HD).transpose(0, 2, 1, 3)
        v = (h @ wv.T).reshape(Bx, Tx, NKV, HD).transpose(0, 2, 1, 3)
        cos, sin = _rope_tables(Tx)
        cos, sin = (cos[None, None], sin[None, None])
        q = q * cos + _rotate_half(q) * sin
        k = k * cos + _rotate_half(k) * sin
        k = jnp.repeat(k, NREP, axis=1)
        v = jnp.repeat(v, NREP, axis=1)
        scores = jnp.einsum('bhtd,bhsd->bhts', q, k) / jnp.sqrt(jnp.float32(HD))
        causal = jnp.tril(jnp.ones((Tx, Tx), dtype=bool))
        scores = jnp.where(causal[None, None], scores, jnp.float32(-1e+30))
        att = jax.nn.softmax(scores, axis=-1)
        y = jnp.einsum('bhts,bhsd->bhtd', att, v).transpose(0, 2, 1, 3).reshape(Bx, Tx, Cx)
        x = x + y @ wo.T
        flat = _rmsnorm(x, ln2_w).reshape(-1, Cx)
        probs = jax.nn.softmax(flat @ router_w.T, axis=-1)
        tp, ti = jax.lax.top_k(probs, TOPK)
        tp = tp / (jnp.sum(tp, axis=-1, keepdims=True) + 1e-09)
        weights = jnp.sum(tp[..., None] * jax.nn.one_hot(ti, NE, dtype=flat.dtype), axis=1)
        out = jnp.zeros_like(flat)
        for e in range(NE):
            hh = jax.nn.silu(flat @ w1[e].T) * (flat @ w3[e].T)
            out = out + weights[:, e:e + 1] * (hh @ w2[e].T)
        return x + out.reshape(Bx, Tx, Cx)
    h = _L0_tok_ref(x, L0_tok_ple_table, 3, 64)
    h = h + _L0_attn_ref(_layernorm(h, axis=-1), L0_attn_Wq, L0_attn_bq, L0_attn_Wk, L0_attn_bk, L0_attn_Wv, L0_attn_bv, L0_attn_Wg, L0_attn_bg, L0_attn_input_bias, L0_attn_norm_scale)
    h = h + _L0_ffn_ref(_layernorm(h, axis=-1), L0_ffn_ln1_w, L0_ffn_ln2_w, L0_ffn_wq, L0_ffn_wk, L0_ffn_wv, L0_ffn_wo, L0_ffn_router_w, L0_ffn_w1, L0_ffn_w2, L0_ffn_w3)
    return h

_drawn_inputs = setup_inputs


def setup_inputs(seed=0):
    import zlib

    import numpy as np

    out = dict(_drawn_inputs(seed))
    spreads = {'L0_attn_bq': (0.0, 0.1),
     'L0_attn_bk': (0.0, 0.1),
     'L0_attn_bv': (0.0, 0.1),
     'L0_attn_bg': (0.0, 0.1),
     'L0_attn_input_bias': (-1.0, 0.6),
     'L0_attn_norm_scale': (1.0, 0.2),
     'L0_ffn_ln1_w': (1.0, 0.6),
     'L0_ffn_ln2_w': (1.0, 0.6)}
    factors = {'L0_ffn_wq': 8.0,
     'L0_ffn_wk': 8.0,
     'L0_ffn_wv': 4.208,
     'L0_ffn_wo': 3.803,
     'L0_ffn_router_w': 8.0,
     'L0_ffn_w1': 8.0,
     'L0_ffn_w2': 8.0,
     'L0_ffn_w3': 8.0}
    for name, (base, spread) in spreads.items():
        noise = np.random.default_rng([zlib.crc32(name.encode()), seed]).standard_normal(out[name].shape)
        drawn = base * np.exp(spread * noise) if base else spread * noise
        out[name] = jnp.asarray(drawn.astype(out[name].dtype))
    for name, factor in factors.items():
        out[name] = (out[name] * factor).astype(out[name].dtype)
    return out
```

```python
import numpy as np
import concourse.bass as bass
from concourse import mybir
from concourse.alu_op_type import AluOpType as ALU
from contextlib import ExitStack

B, T, D = 32, 512, 64
P = 128
NP = B // 2
NT = T // P
G = 2 * NT
VOCAB, HIDDEN, LAYER = 32000, 512, 3
L = 64
NC = T // L
NH, NKV, HD = 4, 2, 16
NE, HID = 8, 170
F = NE * HID
NJ = (F + P - 1) // P
NEG = -1.0e30
CASTS = 22
PIECES = 3


def tower(nc, a):
    f32, bf16, i32 = mybir.dt.float32, mybir.dt.bfloat16, mybir.dt.int32
    ACT, AX = mybir.ActivationFunctionType, mybir.AxisListType.X
    pe, act, dve, pool, sp = nc.tensor, nc.scalar, nc.vector, nc.gpsimd, nc.sync
    ctx = ExitStack()

    def sb(name, shape, dt=f32):
        return ctx.enter_context(nc.sbuf_tensor(name, shape, dt))

    def dram(name, shape, dt):
        return nc.dram_tensor(name, shape, dt, kind="Internal").ap()

    with ctx:
        ident = sb("ident", [P, P])
        identb = sb("identb", [P, P], bf16)
        maskb = sb("maskb", [P, 2 * P], bf16)
        chunkmask = sb("chunkmask", [P, P])
        batchmask = sb("batchmask", [P, P])
        restart = sb("restart", [P, T])
        onesbd = sb("onesbd", [P, 2])
        rev = sb("rev", [P, NE])
        proj = sb("proj", [P, 6, P])
        bias = sb("bias", [P, 6])
        ibias = sb("ibias", [P, 1])
        bi = sb("bi", [P, 2])
        nscale = sb("nscale", [P, D])
        ln1 = sb("ln1", [P, 1])
        ln2 = sb("ln2", [P, 1])
        wq = sb("wq", [P, 2, P])
        wk = sb("wk", [P, 2, D])
        wv = sb("wv", [P, D])
        wo = sb("wo", [P, P])
        ropeq = sb("ropeq", [P, 2, T])
        ropek = sb("ropek", [D, 2, T])
        rw = sb("rw", [P, NE])
        w13 = sb("w13", [P, 2, 3, F], bf16)
        w2 = sb("w2", [P, NJ, D])
        selg = sb("selg", [P, NJ * P], bf16)
        idx = sb("idx", [P, NP * G], i32)
        idxc = sb("idxc", [P, G], i32)

        x0 = sb("x0", [P, G, D])
        xr = sb("xr", [P, G, D])
        st = sb("st", [P, 8, G])
        xc = sb("xc", [P, G, D])
        xn = xc
        xsq = sb("xsq", [P, G, D])
        xT = sb("xT", [P, T])
        qT = sb("qT", [P, T])
        kT = sb("kT", [P, T])
        ab = sb("ab", [P, 3, T])
        mn = sb("mn", [P, 3, T])
        li = sb("li", [P, T])
        mext = sb("mext", [P, T + 1])
        gcum = sb("gcum", [P, T])
        wexp = sb("wexp", [P, T])
        eexp = sb("eexp", [P, T])
        uT = sb("uT", [P, T])
        ek = sb("ek", [P, T])
        wdec = sb("wdec", [P, T])
        nst = ek
        wqx = sb("wqx", [P, T])
        prod = wqx
        hw = sb("hw", [P, T])
        pad = sb("pad", [P, 1])
        ktok = sb("ktok", [P, NT, P])
        utok = sb("utok", [P, NT, P])
        atm = sb("atm", [P, 2, T])
        dlt = sb("dlt", [P, NC, P])
        stT = sb("stT", [P, NC - 1, P])
        hgT = sb("hgT", [P, T])
        ht = sb("ht", [P, G, D])
        mt = sb("mt", [P, 24, G])
        h1 = sb("h1", [P, G, D])
        y0 = sb("y0", [P, G, D])
        hc = sb("hc", [P, G, D])
        ho = ht
        hn = sb("hn", [P, G, D])
        y0b = sb("y0b", [P, G, D])
        hy = sb("hy", [P, G, D])
        hnT = sb("hnT", [P, T])
        t1 = sb("t1", [P, 2, T])
        t2 = sb("t2", [P, 2, T])
        qr = t2
        qp = sb("qp", [P, PIECES, T], bf16)
        kp = sb("kp", [D, PIECES, T], bf16)
        qs = sb("qs", [P, 2 * NH, T], bf16)
        ks = sb("ks", [P, 2 * NKV, T], bf16)
        va = sb("va", [P, NT, 2 * NKV, 32])
        nm = sb("nm", [P, NT, 2 * NH])
        nmr = sb("nmr", [P, NT, 2 * NH])
        mp = sb("mp", [P, NT, PIECES, 2 * NH], bf16)
        mrow = sb("mrow", [PIECES * 2 * NH, T], bf16)
        pr = sb("pr", [P, 2, NH, T])
        yT = sb("yT", [P, 2, T])
        rden = sb("rden", [P, 2, NT * NH])
        x2 = sb("x2", [P, G, D])
        bt = sb("bt", [P, 8, G])
        hx = sb("hx", [P, G, D])
        xf = sb("xf", [P, 2, T])
        xa = sb("xa", [P, 2, T], bf16)
        xb = sb("xb", [P, 2, T], bf16)
        xres = sb("xres", [D, T])
        x2p = sb("x2p", [D, T], bf16)
        lg = sb("lg", [P, 15, G, NE])
        ls = sb("ls", [P, 12, G])
        wp = sb("wp", [P, G, PIECES, NE], bf16)
        wT = sb("wT", [P, 2, T], bf16)
        sl = sb("sl", [P, 2, T])
        sgt = sl
        moT = sl[:, 0, :]
        x2sq = xsq
        fl = pr[:, 0, 0:2, :].rearrange("p a t -> p (a t)").rearrange("p (g a d) -> p g a d", a=2, d=D)
        ynT = hnT
        yn = x2[:, :, :].rearrange("p (t b) (h d) -> p t b h d", b=2, h=NH)
        hsq = atm[:, 0, :].rearrange("p (g d) -> p g d", d=D)
        hh = sb("hh", [P, 2, 2, T])
        ot = sb("ot", [P, G, D])

        wtmp = pr[:, :, :, :].rearrange("p a h t -> p (a h t)")[:, 0:2 * F].rearrange("p (m f) -> p m f", m=2)
        maskf = mn[:, 1, 0:2 * P]
        selgf = ab[:, :, :].rearrange("p a t -> p (a t)")[:, 0:NJ * P]

        banks = [ctx.enter_context(nc.psum_tensor(f"bank{i}", [P, T], f32)) for i in range(7)]
        ring, ybank, h1bank, gbank, h3bank, obank = banks[0:2], banks[2], banks[3], banks[4], banks[5], banks[6]
        misc = ctx.enter_context(nc.psum_tensor("misc", [P, T], f32))
        miscb = misc[:, :].bitcast(bf16)

        qscr = dram("qscr", [PIECES * HD, 2 * NH, T], bf16)
        kscr = dram("kscr", [PIECES * HD, 2 * NKV, T], bf16)
        mscr = dram("mscr", [PIECES, 2 * NH, T], bf16)


        SKEW = dict(g=0, m=1, b=2, c=3)
        ORDER = ("g0 c0 b0 c1 m0 c2 b1 m1 b2 c3 m2 b3 c4 m3 b4 c5 m4 b5 c6 m5 m6 b6 c7 b7 m7 c8 b8 m8 c9 b9 m9 "
                 "c10 b10 m10 c11 b11 m11 c12 b12 c13 b13 c14 c16 b14 c15 "
                 "g1 m12 g2 g3 b15 m13 g4 g5 b16 g6 m14 g7 b17 g8 g9 m15 b18 g10 m16 b19 g11 m17 b20 b21 g12 b22 b23 "
                 "b24 b25 b26 b27 b28 b29").split()
        READ = dict(g4=[("xT", 1)], g5=[("qT", 1)], g6=[("kT", 1)], g7=[("gx", 1)],
                    g8=[("gx", 2)], g9=[("gx", 3)], g12=[("uT", 1)],
                    m0=[("ktok", 1)], m1=[("utok", 1)], m2=[("atm", 1)], m3=[("atm", 2)], m4=[("dlt", 1)],
                    m5=[("dlt", 2)], m7=[("stT", 1)], m8=[("stT", 2)], m9=[("hgT", 1)], m10=[("ht", 1)],
                    m11=[("dabs", 1)],
                    b0=[("hnT", 1)], b1=[("t1", 1)], b2=[("t2", 1)], b3=[("t1", 2)], b4=[("t2", 2)], b5=[("va", 1)],
                    b14=[("mrow", 1)], b24=[("yn", 1)], b25=[("yn", 2)], b26=[("ynT", 1)], b27=[("x2", 1), ("hx", 1)],
                    c0=[("xf", 1)], c1=[("xf", 2)], c2=[("lg", 1)], c3=[("wT", 1)], c15=[("ot", 1)])
        TENANTS = [step for step in ORDER if step in READ]
        PE_OF = dict(g="pe_gate", m="pe_mem", b="pe_attn", c="pe_moe")
        NTH = {step: 1 + [t for t in TENANTS if t[0] == step[0]].index(step) for step in TENANTS}

        PER = dict(
            idxc=1, x0=16 * G, xres=1, g_sum=1, g_nm=1, xc=1, xsq=1, g_var=1, g_dve=4, g_act=2, xn=1,
            xT=1, qT=1, kT=1, gx=3, gabs=1, gexp=1, gln=1, lsi=1, lf=1, lso=1, si=1, so=1, li=1, mscan=1, lfc=1,
            gcum=1, aw=1, ae=1, wexp=1, eexp=1, uT=1, ek=1, wdec=1, nst=1, wqx=1, prod=1, hw=1,
            ktok=1, utok=1, atm=2, dlt=2, dltw=1, state=NC - 2, stT=2, hgT=1, ht=1, dabs=1, den=1, rd=1, hsq=1, hsum=1, rd2=1,
            hms=1, mh_dve=4, mh_act=2, hf=1, ho=1, hos=1, h1=1, m_sum=1, m_nm=1, hc=1, hsq2=1, m_var=1, ml_dve=4,
            ml_act=2, m_a=1, m_b=1, mr_dve=4, mr_act=2, rr=1, hn=1, y0=1,
            hy=1, y0b=1, hnT=1, t1=2, t2=2, qr=2, p1=2, r1=2, p2=2, p3=2, qk_out=32, qk_in=16 * 7, va=1, smax=4 * 2 * NH,
            mp=5, mrow=1, m_out=16, m_in=16, pexp=4 * 2 * NH, yT=2, rden=2, yn=2, ynT=1, x2=1, hx=1, x2sq=1, b_var=1,
            b_dve=4, b_act=2, fl=1,
            xf=2, cast1=4, xahi=2, cres=2, cast2=2, xblo=2, lg=1, r_dve=21, r_act=1, wp=5, wT=1,
            silu=2 * NJ, gated=2 * NJ, hh=2 * NJ, moT=1, ot=1, out=32,
            pe_gate=7, pe_mem=11, pe_attn=11, pe_moe=5, pe_s=4 * 2 * NH, pe_st=4 * 2 * NH, pe_pv=8,
            pe_h1=2 * NJ, pe_g=2 * NJ, pe_h3=2 * NJ, pe_down=NJ)
        s = {name: ctx.enter_context(nc.semaphore(name)) for name in PER}
        loaded = ctx.enter_context(nc.semaphore("loaded"))
        cleared = ctx.enter_context(nc.semaphore("cleared"))
        cast = ctx.enter_context(nc.semaphore("cast"))
        setup = ctx.enter_context(nc.semaphore("setup"))

        def upto(name, n, k=1):
            return n * PER[name] + k

        def full(name, n):
            return upto(name, n, PER[name])

        def later(n):
            return type(n) is not int or n > 0

        def active(it):
            return [c for c in SKEW if 0 <= it - SKEW[c] < NP]

        def before(step, it, stages):
            mine = [t for t in TENANTS if t[0] in stages]
            if mine.index(step) > 0:
                prev, at = mine[mine.index(step) - 1], it
            else:
                last = active(it - 1) if type(it) is int else list(SKEW)
                if not last:
                    return []
                prev, at = [t for t in TENANTS if t[0] in last][-1], it - 1
            return [(name, upto(name, at - SKEW[prev[0]], k)) for name, k in READ[prev]]

        def run(program, engine):
            for it in range(3):
                program(it, active(it))
            with engine.Fori(3, NP) as it:
                program(it, list(SKEW))
            for it in range(NP, NP + 3):
                program(it, active(it))

        def bc(t, n):
            return t.unsqueeze(2).to_broadcast([t.shape[0], t.shape[1], n])

        def rsqrt_arg(site, n, tiny, src, scale, eps):
            dve.tensor_scalar(out=tiny[0], in0=src, scalar1=scale, scalar2=eps, op0=ALU.mult,
                              op1=ALU.add).then_inc(s[site + "_dve"], 1)

        def rsqrt_table(site, n, tiny):
            act.wait_ge(s[site + "_dve"], upto(site + "_dve", n, 1))
            act.activation(tiny[1], tiny[0], ACT.Ln).then_inc(s[site + "_act"], 1)
            act.wait_ge(s[site + "_act"], upto(site + "_act", n, 1))
            act.activation(tiny[2], tiny[1], ACT.Exp, scale=-0.5).then_inc(s[site + "_act"], 1)

        def rsqrt_step(site, n, tiny):
            dve.wait_ge(s[site + "_act"], upto(site + "_act", n, 2))
            dve.tensor_tensor(out=tiny[3], in0=tiny[2], in1=tiny[2], op=ALU.mult).then_inc(s[site + "_dve"], 1)
            dve.wait_ge(s[site + "_dve"], upto(site + "_dve", n, 2))
            dve.scalar_tensor_tensor(out=tiny[4], in0=tiny[3], scalar=-0.5, in1=tiny[0], op0=ALU.mult,
                                     op1=ALU.mult).then_inc(s[site + "_dve"], 1)
            dve.wait_ge(s[site + "_dve"], upto(site + "_dve", n, 3))
            dve.scalar_tensor_tensor(out=tiny[5], in0=tiny[4], scalar=1.5, in1=tiny[2], op0=ALU.add,
                                     op1=ALU.mult).then_inc(s[site + "_dve"], 1)
            dve.wait_ge(s[site + "_dve"], upto(site + "_dve", n, 4))

        g_tiny = [st[:, r, :] for r in range(6)]
        mh_tiny = [mt[:, r, :] for r in range(0, 6)]
        ml_tiny = [mt[:, r, :] for r in range(6, 12)]
        mr_tiny = [mt[:, r, :] for r in range(12, 18)]
        b_tiny = [bt[:, r, :] for r in range(6)]
        wend = wexp[:, :].rearrange("p (c l) -> p c l", l=L)[:, :, L - 1]
        UNITS = [(b, t, h) for b in range(2) for t in range(NT) for h in range(NH)]
        block = ctx.enter_context(nc.Block())

        @block.sync
        def _(_e):
            for dst, name in ((ident, "ident"), (maskf, "maskf"), (chunkmask, "chunkmask"), (batchmask, "batchmask"),
                              (restart, "restart"), (onesbd, "onesbd"), (rev, "rev"), (proj, "proj"), (bias, "bias"),
                              (ibias, "ibias"), (nscale, "nscale"), (ln1, "ln1"), (ln2, "ln2"), (wq, "wq"),
                              (wk, "wk"), (wv, "wv"), (wo, "wo"), (ropeq, "ropeq"), (ropek, "ropek"), (rw, "rw"),
                              (w2, "w2"), (idx, "idx")):
                sp.dma_start(dst if type(dst) is bass.AP else dst[(slice(None),) * len(dst.shape)], a[name]).then_inc(loaded, 16)
            sp.dma_start(wtmp[:, 0, :], a["w1"]).then_inc(loaded, 16)
            sp.dma_start(wtmp[:, 1, :], a["w3"]).then_inc(loaded, 16)
            sp.dma_start(selgf, a["selg"]).then_inc(loaded, 16)

            def program(it, stages):
                for step in [x for x in ORDER if x[0] in stages]:
                    n = it - SKEW[step[0]]
                    if step == "b5":
                        sp.wait_ge(s["p3"], upto("p3", n, 1))
                        sp.dma_start(qscr.rearrange("(p d) g t -> (d g) p t", p=PIECES),
                                     qp[:, :, :]).then_inc(s["qk_out"], 16)
                        sp.wait_ge(s["p3"], upto("p3", n, 2))
                        sp.dma_start(kscr.rearrange("(p d) g t -> (d g) p t", p=PIECES),
                                     kp[:, :, :]).then_inc(s["qk_out"], 16)
                        sp.wait_ge(s["qk_out"], full("qk_out", n))
                        for dst, src, at, rows, frm in (
                                (qs, qscr, 0, 16, 0), (qs, qscr, 16, 16, 0), (qs, qscr, 32, 32, 0),
                                (qs, qscr, 64, 32, 16), (ks, kscr, 0, 48, 0), (ks, kscr, 48, 32, 0),
                                (ks, kscr, 80, 16, 0)):
                            sp.dma_start(dst[at:at + rows, :, :], src[frm:frm + rows, :, :]).then_inc(s["qk_in"], 16)
                    if step == "b14":
                        sp.wait_ge(s["mrow"], upto("mrow", n))
                        sp.dma_start(mscr.rearrange("p g t -> (p g) t"), mrow[:, :]).then_inc(s["m_out"], 16)
                        sp.wait_ge(s["m_out"], full("m_out", n))
                        sp.dma_start(qs[PIECES * 2 * HD:PIECES * 2 * HD + PIECES, :, :], mscr).then_inc(s["m_in"], 16)
                    if step == "c15":
                        sp.wait_ge(s["ot"], upto("ot", n))
                        for b in range(2):
                            dst = a["out"][bass.ds(n * 2 + b, 1), :, :].rearrange("o (i p) d -> p (o i) d", p=P)
                            src = ot[:, :, :].rearrange("p (i b) d -> p i b d", b=2)[:, :, b, :]
                            sp.dma_start(dst, src).then_inc(s["out"], 16)

            run(program, sp)
            sp.wait_ge(s["out"], full("out", NP - 1))

        @block.tensor
        def _(_e):
            def mm(out, lhsT, rhs, start=True, stop=True, **k):
                return pe.matmul(out, lhsT, rhs, start=start, stop=stop, **k)

            def four(step, src):
                for t in range(NT):
                    last = pe.transpose(misc[:, t * P:(t + 1) * P], src(t), ident[:, :])
                last.then_inc(s[PE_OF[step[0]]], 1)

            def done(step, last):
                last.then_inc(s[PE_OF[step[0]]], 1)

            pe.wait_ge(loaded, 16 * 25)
            pe.wait_ge(cleared, 8)
            pe.wait_ge(cast, CASTS)

            def down(n, j):
                if j == 0:
                    if later(n):
                        pe.wait_ge(s["moT"], upto("moT", n - 1))
                rows = min(P, F - j * P)
                pe.wait_ge(s["hh"], upto("hh", n, 2 * j + 2))
                for b in range(2):
                    last = mm(obank[D * b:D * b + D, :], w2[0:rows, j, :], hh[0:rows, j % 2, b, :],
                              start=j == 0, stop=j == NJ - 1)
                last.then_inc(s["pe_down"], 1)

            def pv(n, k):
                b, t = k // NT, k % NT
                pe.wait_ge(s["pexp"], upto("pexp", n, NH * (k + 1)))
                if t == 0:
                    if b or later(n):
                        pe.wait_ge(s["yT"], upto("yT", n, b))
                for h in range(NH):
                    last = mm(ybank[32 * h:32 * h + 32, t * P:T], va[:, t, b * NKV + h // 2, :],
                              pr[:, k % 2, h, 0:T - t * P], start=t == 0, stop=t == NT - 1)
                last.then_inc(s["pe_pv"], 1)

            def program(it, stages):
                for step in [x for x in ORDER if x[0] in stages]:
                    n = it - SKEW[step[0]]
                    c, k = step[0], int(step[1:])
                    if step in READ:
                        for name, value in before(step, it, stages):
                            pe.wait_ge(s[name], value)
                    if step == "g4":
                        pe.wait_ge(s["xn"], upto("xn", n))
                        four(step, lambda t: xn[:, 2 * t:2 * t + 2, :].rearrange("p b d -> p (b d)"))
                    if c == "g" and 5 <= k <= 9:
                        if k == 5:
                            pe.wait_ge(s["xT"], upto("xT", n))
                        done(step, mm(misc[:, :], proj[:, (0, 1, 3, 4, 5)[k - 5], :], xT[:, :]))
                    if step == "g12":
                        done(step, mm(misc[:, :], proj[:, 2, :], xT[:, :]))
                    if step == "m0":
                        pe.wait_ge(s["kT"], upto("kT", n))
                        four(step, lambda t: kT[:, t * P:(t + 1) * P])
                    if step == "m1":
                        pe.wait_ge(s["uT"], upto("uT", n))
                        four(step, lambda t: uT[:, t * P:(t + 1) * P])
                    if step in ("m2", "m3"):
                        b = k - 2
                        for t in range(NT):
                            last = mm(misc[:, t * P:(t + 1) * P], kT[D * b:D * b + D, t * P:(t + 1) * P],
                                      qT[D * b:D * b + D, t * P:(t + 1) * P])
                        done(step, last)
                    if step in ("m4", "m5"):
                        if step == "m4":
                            pe.wait_ge(s["ktok"], upto("ktok", n))
                            pe.wait_ge(s["utok"], upto("utok", n))
                        par = k - 4
                        for q in range(NT - par):
                            last = mm(misc[:, q * P:(q + 1) * P], utok[L * par:L * par + L, q, :],
                                      ktok[L * par:L * par + L, q, :])
                        done(step, last)
                    if step in ("m7", "m8"):
                        pe.wait_ge(s["state"], full("state", n))
                        lo, hi = ((0, 4), (4, NC - 1))[k - 7]
                        for j in range(lo, hi):
                            last = pe.transpose(misc[:, (j - lo) * P:(j - lo + 1) * P], dlt[:, j, :], ident[:, :])
                        done(step, last)
                    if step == "m9":
                        pe.wait_ge(s["stT"], full("stT", n))
                        pe.wait_ge(s["atm"], full("atm", n))
                        for j in range(1, NC):
                            mm(misc[:, j * L:(j + 1) * L], stT[:, j - 1, :], qT[:, j * L:(j + 1) * L], start=j == 1,
                               stop=False, skip_group_check=True)
                        for t in range(NT):
                            for b in range(2):
                                last = mm(misc[D * b:D * b + D, t * P:(t + 1) * P], utok[:, t, D * b:D * b + D],
                                          atm[:, b, t * P:(t + 1) * P], start=False, stop=t == NT - 1,
                                          skip_group_check=True)
                        done(step, last)
                    if step == "m10":
                        pe.wait_ge(s["hgT"], upto("hgT", n))
                        four(step, lambda t: hgT[:, t * P:(t + 1) * P])
                    if step == "m11":
                        pe.wait_ge(s["prod"], upto("prod", n))
                        for t in range(NT):
                            last = mm(misc[:, 2 * t:2 * t + 2], prod[:, t * P:(t + 1) * P], onesbd[:, :])
                        done(step, last)
                    if step == "b0":
                        pe.wait_ge(s["hn"], upto("hn", n))
                        four(step, lambda t: hn[:, 2 * t:2 * t + 2, :].rearrange("p b d -> p (b d)"))
                    if step in ("b1", "b2"):
                        if step == "b1":
                            pe.wait_ge(s["hnT"], upto("hnT", n))
                        done(step, mm(misc[:, :], wq[:, k - 1, :], hnT[:, :]))
                    if step in ("b3", "b4"):
                        done(step, mm(misc[0:D, :], wk[:, k - 3, :], hnT[:, :]))
                    if step == "b5":
                        for t in range(NT):
                            last = mm(misc[:, t * D:(t + 1) * D], hnT[:, t * P:(t + 1) * P], wv[:, :])
                        done(step, last)
                    if c == "b" and 6 <= k <= 13:
                        b, t = (k - 6) // NT, (k - 6) % NT
                        if k == 6:
                            pe.wait_ge(s["qk_in"], full("qk_in", n))
                        for h in range(NH):
                            u = (k - 6) * NH + h
                            if u >= 2:
                                pe.wait_ge(s["smax"], upto("smax", n, u - 1))
                            else:
                                if later(n):
                                    pe.wait_ge(s["pexp"], upto("pexp", n - 1, PER["pexp"] - 1 + u))
                            mm(ring[u % 2][:, 0:(t + 1) * P], qs[:, b * NH + h, t * P:(t + 1) * P],
                               ks[:, b * NKV + h // 2, 0:(t + 1) * P], stop=False)
                            mm(ring[u % 2][:, t * P:(t + 1) * P], identb[:, :], maskb[:, 0:P],
                               start=False).then_inc(s["pe_s"], 1)
                    if step == "b14":
                        pe.wait_ge(s["mp"], full("mp", n))
                        for t in range(NT):
                            last = pe.transpose(miscb[0:PIECES * 2 * NH, t * P:(t + 1) * P],
                                                mp[:, t, :, :].rearrange("p a b -> p (a b)"), identb[:, :])
                        done(step, last)
                    if c == "b" and 15 <= k <= 22:
                        b, t = (k - 15) // NT, (k - 15) % NT
                        if k == 15:
                            pe.wait_ge(s["m_in"], upto("m_in", n, 16))
                        for h in range(NH):
                            u = (k - 15) * NH + h
                            if u >= 2:
                                pe.wait_ge(s["pexp"], upto("pexp", n, u - 1))
                            else:
                                pe.wait_ge(s["smax"], upto("smax", n, PER["smax"] - 1 + u))
                            mm(ring[u % 2][:, 0:T - t * P], ks[:, b * NKV + h // 2, t * P:(t + 1) * P],
                               qs[:, b * NH + h, t * P:T], stop=False)
                            mm(ring[u % 2][:, 0:P], identb[:, :], maskb[:, P:2 * P],
                               start=False).then_inc(s["pe_st"], 1)
                        if k > 15:
                            pv(n, k - 16)
                    if step == "b23":
                        pv(n, 7)
                    if step in ("b24", "b25"):
                        pe.wait_ge(s["yT"], upto("yT", n, k - 23))
                        four(step, lambda t: yT[:, k - 24, t * P:(t + 1) * P])
                    if step == "b26":
                        pe.wait_ge(s["yn"], full("yn", n))
                        four(step, lambda t: yn[:, t, :, :, :].rearrange("p b h d -> p (b h d)"))
                    if step == "b27":
                        pe.wait_ge(s["ynT"], upto("ynT", n))
                        for t in range(NT):
                            last = mm(misc[:, t * P:(t + 1) * P], ynT[:, t * P:(t + 1) * P], wo[:, :])
                        done(step, last)
                    if step in ("c0", "c1"):
                        pe.wait_ge(s["fl"], upto("fl", n))
                        four(step, lambda t: fl[:, 2 * t + k, :, :].rearrange("p a d -> p (a d)"))
                    if step == "c2":
                        pe.wait_ge(s["xf"], full("xf", n))
                        for g in range(G):
                            last = mm(misc[:, g * NE:(g + 1) * NE], xf[:, g % 2, (g // 2) * P:(g // 2 + 1) * P],
                                      rw[:, :])
                        done(step, last)
                    if step == "c3":
                        pe.wait_ge(s["wp"], full("wp", n))
                        for g in range(G):
                            col = (g % 2) * T + (g // 2) * P
                            last = pe.transpose(miscb[0:PIECES * NE, col:col + P],
                                                wp[:, g, :, :].rearrange("p a b -> p (a b)"), identb[:, :])
                        done(step, last)
                    if c == "c" and 4 <= k <= 14:
                        j = k - 4
                        cols = slice(j * P, min(F, (j + 1) * P))
                        w = cols.stop - cols.start
                        if j == 0:
                            pe.wait_ge(s["xahi"], full("xahi", n))
                            pe.wait_ge(s["xblo"], full("xblo", n))
                            pe.wait_ge(s["wT"], upto("wT", n))
                        for b in range(2):
                            u = 2 * j + b
                            if u or later(n):
                                pe.wait_ge(s["silu"], upto("silu", n, u))
                            for p, mov in enumerate((xa, xa, xb)):
                                last = mm(h1bank[0:w, :], w13[:, 0, p, cols], mov[:, b, :], start=p == 0, stop=p == 2)
                            last.then_inc(s["pe_h1"], 1)
                            if u or later(n):
                                pe.wait_ge(s["gated"], upto("gated", n, u))
                            mm(gbank[0:w, :], selg[:, cols], wT[:, b, :]).then_inc(s["pe_g"], 1)
                            if u or later(n):
                                pe.wait_ge(s["hh"], upto("hh", n, u))
                            for p, mov in enumerate((xa, xa, xb)):
                                last = mm(h3bank[0:w, :], w13[:, 1, p, cols], mov[:, b, :], start=p == 0, stop=p == 2)
                            last.then_inc(s["pe_h3"], 1)
                        if j:
                            down(n, j - 1)
                    if step == "c15":
                        pe.wait_ge(s["moT"], upto("moT", n))
                        four(step, lambda t: moT[:, t * P:(t + 1) * P])
                    if step == "c16":
                        down(n, NJ - 1)

            run(program, pe)

        @block.scalar
        def _(_e):
            act.wait_ge(loaded, 16 * 25)

            def program(it, stages):
                for step in [x for x in ORDER if x[0] in stages]:
                    n = it - SKEW[step[0]]
                    c, k = step[0], int(step[1:])
                    if step == "g1":
                        act.wait_ge(s["xc"], upto("xc", n))
                        act.activation(xsq[:, :, :], xc[:, :, :], ACT.Square).then_inc(s["xsq"], 1)
                    if step == "g2":
                        rsqrt_table("g", n, g_tiny)
                    if step == "g4":
                        act.wait_ge(s["pe_gate"], upto("pe_gate", n, NTH[step]))
                        act.activation(xT[:, :], misc[:, :], ACT.Copy).then_inc(s["xT"], 1)
                    if step == "g5":
                        if later(n):
                            act.wait_ge(s["hgT"], upto("hgT", n - 1))
                        act.wait_ge(s["pe_gate"], upto("pe_gate", n, NTH[step]))
                        act.activation(qT[:, :], misc[:, :], ACT.Identity, bias=bias[:, 0:1]).then_inc(s["qT"], 1)
                    if c == "g" and 7 <= k <= 9:
                        q = k - 7
                        act.wait_ge(s["pe_gate"], upto("pe_gate", n, NTH[step]))
                        act.activation(mn[:, q, :], misc[:, :], ACT.Identity, scale=(0.2, -1.0, 1.0)[q],
                                       bias=(bi[:, 0:1], bi[:, 1:2], bias[:, 5:6])[q]).then_inc(s["gx"], 1)
                    if step == "g10":
                        act.wait_ge(s["gx"], full("gx", n))
                        act.activation(ab[:, :, :], mn[:, :, :], ACT.Abs).then_inc(s["gabs"], 1)
                        act.wait_ge(s["gabs"], upto("gabs", n))
                        act.activation(ab[:, :, :], ab[:, :, :], ACT.Exp, scale=-1.0).then_inc(s["gexp"], 1)
                        act.wait_ge(s["gexp"], upto("gexp", n))
                        act.activation(ab[:, :, :], ab[:, :, :], ACT.Ln, bias=1.0).then_inc(s["gln"], 1)
                        act.wait_ge(s["lsi"], upto("lsi", n))
                        act.activation(li[:, :], mn[:, 0, :], ACT.Exp).then_inc(s["si"], 1)
                        act.wait_ge(s["lso"], upto("lso", n))
                        act.activation(ab[:, 2, :], mn[:, 2, :], ACT.Exp).then_inc(s["so"], 1)
                    if step == "g11":
                        act.wait_ge(s["aw"], upto("aw", n))
                        act.activation(wexp[:, :], mn[:, 0, :], ACT.Exp).then_inc(s["wexp"], 1)
                        act.wait_ge(s["ae"], upto("ae", n))
                        act.activation(eexp[:, :], mn[:, 2, :], ACT.Exp).then_inc(s["eexp"], 1)
                    if step == "g12":
                        act.wait_ge(s["x0"], full("x0", n))
                        if later(n):
                            act.wait_ge(s["h1"], upto("h1", n - 1))
                        act.activation(xr[:, :, :], x0[:, :, :], ACT.Copy).then_inc(s["xres"], 1)
                    if step in ("m0", "m1"):
                        act.wait_ge(s["pe_mem"], upto("pe_mem", n, NTH[step]))
                        act.activation((ktok, utok)[k][:, :, :].rearrange("p a b -> p (a b)"), misc[:, :],
                                       ACT.Copy).then_inc(s[("ktok", "utok")[k]], 1)
                    if step in ("m7", "m8"):
                        lo, hi = ((0, 4), (4, NC - 1))[k - 7]
                        act.wait_ge(s["pe_mem"], upto("pe_mem", n, NTH[step]))
                        act.activation(stT[:, lo:hi, :].rearrange("p a b -> p (a b)"), misc[:, 0:(hi - lo) * P],
                                       ACT.Copy).then_inc(s["stT"], 1)
                    if step == "m10":
                        act.wait_ge(s["pe_mem"], upto("pe_mem", n, NTH[step]))
                        act.activation(ht[:, :, :].rearrange("p a b -> p (a b)"), misc[:, :],
                                       ACT.Copy).then_inc(s["ht"], 1)
                    if step == "m11":
                        act.wait_ge(s["pe_mem"], upto("pe_mem", n, NTH[step]))
                        act.activation(mt[:, 18, :], misc[:, 0:G], ACT.Abs).then_inc(s["dabs"], 1)
                    if step == "m12":
                        act.wait_ge(s["ht"], upto("ht", n))
                        act.activation(hsq[:, :, :], ht[:, :, :], ACT.Square).then_inc(s["hsq"], 1)
                        rsqrt_table("mh", n, mh_tiny)
                    if step == "m14":
                        act.wait_ge(s["hc"], upto("hc", n))
                        act.activation(hsq[:, :, :], hc[:, :, :], ACT.Square).then_inc(s["hsq2"], 1)
                    if step == "m15":
                        rsqrt_table("ml", n, ml_tiny)
                    if step == "m16":
                        rsqrt_table("mr", n, mr_tiny)
                    if step == "b0":
                        act.wait_ge(s["pe_attn"], upto("pe_attn", n, NTH[step]))
                        act.activation(hnT[:, :], misc[:, :], ACT.Copy, scale=ln1[:, 0:1]).then_inc(s["hnT"], 1)
                    if step in ("b2", "b4"):
                        x, rows, dst = (0, P, qp) if step == "b2" else (1, D, kp)
                        if later(n):
                            act.wait_ge(s["qk_out"], full("qk_out", n - 1))
                        act.wait_ge(s["qr"], upto("qr", n, x + 1))
                        act.activation(dst[0:rows, 0, :], qr[0:rows, x, :], ACT.Copy).then_inc(s["p1"], 1)
                        act.wait_ge(s["r1"], upto("r1", n, x + 1))
                        act.activation(dst[0:rows, 1, :], t1[0:rows, x, :], ACT.Copy).then_inc(s["p2"], 1)
                    if step == "b5":
                        if later(n):
                            act.wait_ge(s["pe_pv"], full("pe_pv", n - 1))
                        act.wait_ge(s["pe_attn"], upto("pe_attn", n, NTH[step]))
                        act.activation(va[:, :, :, 0:HD].rearrange("p t g d -> p (t g) d"),
                                       misc[:, 0:NT * D].rearrange("p (t d) -> p t d", d=HD),
                                       ACT.Copy).then_inc(s["va"], 1)
                    if step == "b14":
                        act.wait_ge(s["pe_attn"], upto("pe_attn", n, NTH[step]))
                        act.activation(mrow[:, :], miscb[0:PIECES * 2 * NH, 0:T], ACT.Copy).then_inc(s["mrow"], 1)
                    if c == "b" and 15 <= k <= 22:
                        q = k - 15
                        b, t = q // NT, q % NT
                        if q == NT + 1:
                            act.wait_ge(s["pe_pv"], upto("pe_pv", n, NT))
                            act.activation(yT[:, 0, :], ybank[:, :], ACT.Copy).then_inc(s["yT"], 1)
                        if q >= 2:
                            act.wait_ge(s["pe_pv"], upto("pe_pv", n, q - 1))
                        for h in range(NH):
                            act.wait_ge(s["pe_st"], upto("pe_st", n, q * NH + h + 1))
                            act.activation(pr[:, q % 2, h, 0:T - t * P], ring[h % 2][:, 0:T - t * P],
                                           ACT.Exp).then_inc(s["pexp"], 1)
                    if step == "b23":
                        act.wait_ge(s["pe_pv"], upto("pe_pv", n, 8))
                        act.activation(yT[:, 1, :], ybank[:, :], ACT.Copy).then_inc(s["yT"], 1)
                    if step == "b26":
                        act.wait_ge(s["pe_attn"], upto("pe_attn", n, NTH[step]))
                        act.activation(ynT[:, :], misc[:, :], ACT.Copy).then_inc(s["ynT"], 1)
                    if step == "b27":
                        act.wait_ge(s["x2"], upto("x2", n))
                        act.activation(x2sq[:, :, :], x2[:, :, :], ACT.Square).then_inc(s["x2sq"], 1)
                    if step == "b28":
                        rsqrt_table("b", n, b_tiny)
                    if step in ("c0", "c1"):
                        act.wait_ge(s["pe_moe"], upto("pe_moe", n, NTH[step]))
                        if k == 0:
                            if later(n):
                                act.wait_ge(s["pe_h3"], full("pe_h3", n - 1))
                        act.activation(xf[:, k, :], misc[:, :], ACT.Copy, scale=ln2[:, 0:1]).then_inc(s["xf"], 1)
                        act.wait_ge(s["xf"], upto("xf", n, k + 1))
                        act.activation(xa[0:D, k, :], xf[0:D, k, :], ACT.Copy).then_inc(s["cast1"], 1)
                        act.activation(xb[D:P, k, :], xf[D:P, k, :], ACT.Copy).then_inc(s["cast1"], 1)
                        act.wait_ge(s["cres"], upto("cres", n, k + 1))
                        act.activation(x2p[:, :], xres[:, :], ACT.Copy).then_inc(s["cast2"], 1)
                    if step == "c2":
                        act.wait_ge(s["r_dve"], upto("r_dve", n, 2))
                        act.activation(lg[:, 2, :, :], lg[:, 1, :, :], ACT.Exp).then_inc(s["r_act"], 1)
                    if step == "c3":
                        act.wait_ge(s["pe_moe"], upto("pe_moe", n, NTH[step]))
                        act.activation(wT[0:PIECES * NE, :, :].rearrange("p b t -> p (b t)"),
                                       miscb[0:PIECES * NE, :], ACT.Copy).then_inc(s["wT"], 1)
                    if c == "c" and 4 <= k <= 14:
                        j = k - 4
                        w = min(P, F - j * P)
                        for b in range(2):
                            u = 2 * j + b
                            if u >= 2:
                                act.wait_ge(s["hh"], upto("hh", n, u - 1))
                            act.wait_ge(s["pe_h1"], upto("pe_h1", n, u + 1))
                            act.activation(sl[0:w, b, :], h1bank[0:w, :], ACT.Silu).then_inc(s["silu"], 1)
                    if step == "c16":
                        act.wait_ge(s["pe_down"], upto("pe_down", n, NJ))
                        act.activation(moT[:, :], obank[:, :], ACT.Copy).then_inc(s["moT"], 1)

            run(program, act)

        @block.vector
        def _(_e):
            tt, ts, stt = dve.tensor_tensor, dve.tensor_scalar, dve.scalar_tensor_tensor
            dve.wait_ge(loaded, 16 * 25)
            casts = 0

            def link(ins):
                nonlocal casts
                casts += 1
                ins.then_inc(cast, 1)
                dve.wait_ge(cast, casts)

            for m in range(2):
                link(dve.tensor_copy(out=w13[:, m, 0, :], in_=wtmp[:, m, :]))
                link(tt(out=wtmp[:, m, :], in0=wtmp[:, m, :], in1=w13[:, m, 0, :], op=ALU.subtract))
                link(dve.tensor_copy(out=w13[:, m, 1, :], in_=wtmp[:, m, :]))
                link(dve.tensor_copy(out=w13[0:D, m, 2, :], in_=w13[0:D, m, 0, :]))
                link(tt(out=w13[D:P, m, 2, :], in0=wtmp[D:P, m, :], in1=w13[D:P, m, 1, :], op=ALU.subtract))
            link(dve.tensor_copy(out=selg[:, :], in_=selgf))
            link(dve.tensor_copy(out=identb[:, :], in_=ident[:, :]))
            link(dve.tensor_copy(out=maskb[:, :], in_=maskf))
            link(tt(out=bi[:, 0:1], in0=bias[:, 3:4], in1=ibias[:, :], op=ALU.add))
            link(ts(out=bi[:, 0:1], in0=bi[:, 0:1], scalar1=0.2, scalar2=None, op0=ALU.mult))
            link(ts(out=bi[:, 1:2], in0=bias[:, 4:5], scalar1=-1.0, scalar2=None, op0=ALU.mult))
            for lo in range(0, NP * G, NP * G):
                fx, fn = mn[:, 0, 0:NP * G], mn[:, 2, 0:NP * G]
                link(dve.tensor_copy(out=fx, in_=idx[:, :]))
                link(ts(out=fn, in0=fx, scalar1=0.0, scalar2=float(VOCAB), op0=ALU.is_lt, op1=ALU.mult))
                link(tt(out=fx, in0=fx, in1=fn, op=ALU.add))
                link(ts(out=fx, in0=fx, scalar1=0.0, scalar2=float(VOCAB - 1), op0=ALU.max, op1=ALU.min))
                link(ts(out=fx, in0=fx, scalar1=float(HIDDEN // D), scalar2=float(LAYER), op0=ALU.mult, op1=ALU.add))
                link(dve.tensor_copy(out=idx[:, :], in_=fx))
            assert casts == CASTS, casts
            dve.wait_ge(cleared, 8)

            def program(it, stages):
                for step in [x for x in ORDER if x[0] in stages]:
                    n = it - SKEW[step[0]]
                    c, k = step[0], int(step[1:])
                    if step == "g1":
                        dve.wait_ge(s["x0"], full("x0", n))
                        dve.tensor_reduce(out=st[:, 6, :], in_=x0[:, :, :], axis=AX, op=ALU.add).then_inc(s["g_sum"], 1)
                        dve.wait_ge(s["g_sum"], upto("g_sum", n))
                        ts(out=st[:, 7, :], in0=st[:, 6, :], scalar1=-1.0 / D, scalar2=None,
                           op0=ALU.mult).then_inc(s["g_nm"], 1)
                        dve.wait_ge(s["g_nm"], upto("g_nm", n))
                        tt(out=xc[:, :, :], in0=x0[:, :, :], in1=bc(st[:, 7, :], D), op=ALU.add).then_inc(s["xc"], 1)
                    if step == "g2":
                        dve.wait_ge(s["xsq"], upto("xsq", n))
                        dve.tensor_reduce(out=st[:, 6, :], in_=xsq[:, :, :], axis=AX,
                                          op=ALU.add).then_inc(s["g_var"], 1)
                        dve.wait_ge(s["g_var"], upto("g_var", n))
                        rsqrt_arg("g", n, g_tiny, st[:, 6, :], 1.0 / D, 1e-5)
                    if step == "g3":
                        rsqrt_step("g", n, g_tiny)
                        tt(out=xn[:, :, :], in0=xc[:, :, :], in1=bc(g_tiny[5], D), op=ALU.mult).then_inc(s["xn"], 1)
                    if step == "g6":
                        dve.wait_ge(s["pe_gate"], upto("pe_gate", n, NTH[step]))
                        if later(n):
                            dve.wait_ge(s["hgT"], upto("hgT", n - 1))
                        ts(out=kT[:, :], in0=misc[:, :], scalar1=bias[:, 1:2], scalar2=D ** -0.5, op0=ALU.add,
                           op1=ALU.mult).then_inc(s["kT"], 1)
                    if step == "g10":
                        dve.wait_ge(s["gln"], upto("gln", n))
                        for q, name in enumerate(("lsi", "lf", "lso")):
                            stt(out=mn[:, q, :], in0=mn[:, q, :], scalar=0.0, in1=ab[:, q, :], op0=ALU.min,
                                op1=ALU.subtract).then_inc(s[name], 1)
                    if step == "g11":
                        dve.wait_ge(s["si"], upto("si", n))
                        ts(out=li[:, :], in0=li[:, :], scalar1=20.0, scalar2=-10.0, op0=ALU.mult,
                           op1=ALU.add).then_inc(s["li"], 1)
                        dve.wait_ge(s["li"], upto("li", n))
                        dve.wait_ge(s["lf"], upto("lf", n))
                        lf = mn[:, 1, :]
                        dve.tensor_tensor_scan(out=mext[:, 1:T + 1], data0=lf, data1=li[:, :], initial=0.0, op0=ALU.add,
                                               op1=ALU.max).then_inc(s["mscan"], 1)
                        dve.wait_ge(s["mscan"], upto("mscan", n))
                        starts = lf.rearrange("p (c l) -> p c l", l=L)[:, :, 0]
                        tt(out=starts, in0=starts, in1=mext[:, 0:T].rearrange("p (c l) -> p c l", l=L)[:, :, 0],
                           op=ALU.add).then_inc(s["lfc"], 1)
                        dve.wait_ge(s["lfc"], upto("lfc", n))
                        dve.tensor_tensor_scan(out=gcum[:, :], data0=restart[:, :], data1=lf, initial=0.0,
                                               op0=ALU.mult, op1=ALU.add).then_inc(s["gcum"], 1)
                        dve.wait_ge(s["gcum"], upto("gcum", n))
                        dve.wait_ge(s["so"], upto("so", n))
                        tt(out=mn[:, 0, :], in0=gcum[:, :], in1=mext[:, 1:T + 1], op=ALU.subtract).then_inc(s["aw"], 1)
                        tt(out=mn[:, 2, :], in0=li[:, :], in1=gcum[:, :], op=ALU.subtract).then_inc(s["ae"], 1)
                    if step == "g12":
                        dve.wait_ge(s["pe_gate"], upto("pe_gate", n, NTH[step]))
                        dve.wait_ge(s["eexp"], upto("eexp", n))
                        stt(out=uT[:, :], in0=misc[:, :], scalar=bias[:, 2:3], in1=eexp[:, :], op0=ALU.add,
                            op1=ALU.mult).then_inc(s["uT"], 1)
                        dve.wait_ge(s["wexp"], upto("wexp", n))
                        wd = wdec[:, :].rearrange("p (c l) -> p c l", l=L)[:, 1:NC, 0]
                        dve.tensor_copy(out=wd, in_=wend[:, 0:NC - 1]).then_inc(s["wdec"], 1)
                        dve.wait_ge(s["wdec"], upto("wdec", n))
                        dve.wait_ge(s["ek"], upto("ek", n))
                        dve.tensor_tensor_scan(out=nst[:, :], data0=wdec[:, :], data1=ek[:, :], initial=0.0,
                                               op0=ALU.mult, op1=ALU.add).then_inc(s["nst"], 1)
                    if step in ("m2", "m3"):
                        b = k - 2
                        dve.wait_ge(s["pe_mem"], upto("pe_mem", n, NTH[step]))
                        tt(out=atm[:, b, :].rearrange("p (t q) -> p t q", q=P),
                           in0=misc[:, :].rearrange("p (t q) -> p t q", q=P),
                           in1=chunkmask[:, :].unsqueeze(1).to_broadcast([P, NT, P]), op=ALU.mult).then_inc(s["atm"], 1)
                    if step in ("m4", "m5"):
                        par = k - 4
                        q = NT - par
                        dve.wait_ge(s["pe_mem"], upto("pe_mem", n, NTH[step]))
                        tt(out=dlt[:, :, :].rearrange("p (q a) d -> p q a d", a=2)[:, 0:q, par, :],
                           in0=misc[:, 0:q * P].rearrange("p (q d) -> p q d", d=P),
                           in1=batchmask[:, :].unsqueeze(1).to_broadcast([P, q, P]), op=ALU.mult).then_inc(s["dlt"], 1)
                    if step == "m6":
                        dve.wait_ge(s["dltw"], upto("dltw", n))
                        for j in range(1, NC - 1):
                            if j > 1:
                                dve.wait_ge(s["state"], upto("state", n, j - 1))
                            stt(out=dlt[:, j, :], in0=dlt[:, j - 1, :], scalar=wend[:, j:j + 1], in1=dlt[:, j, :],
                                op0=ALU.mult, op1=ALU.add).then_inc(s["state"], 1)
                    if step == "m9":
                        dve.wait_ge(s["pe_mem"], upto("pe_mem", n, NTH[step]))
                        dve.wait_ge(s["hw"], upto("hw", n))
                        tt(out=hgT[:, :], in0=misc[:, :], in1=hw[:, :], op=ALU.mult).then_inc(s["hgT"], 1)
                    if step == "m12":
                        dve.wait_ge(s["dabs"], upto("dabs", n))
                        ts(out=mt[:, 18, :], in0=mt[:, 18, :], scalar1=1e-6, scalar2=None,
                           op0=ALU.max).then_inc(s["den"], 1)
                        dve.wait_ge(s["den"], upto("den", n))
                        dve.reciprocal(out=mt[:, 19, :], in_=mt[:, 18, :]).then_inc(s["rd"], 1)
                        dve.wait_ge(s["rd"], upto("rd", n))
                        tt(out=mt[:, 20, :], in0=mt[:, 19, :], in1=mt[:, 19, :], op=ALU.mult).then_inc(s["rd2"], 1)
                        dve.wait_ge(s["hsq"], upto("hsq", n))
                        dve.tensor_reduce(out=mt[:, 21, :], in_=hsq[:, :, :], axis=AX, op=ALU.add).then_inc(s["hsum"], 1)
                        dve.wait_ge(s["hsum"], upto("hsum", n))
                        stt(out=mt[:, 22, :], in0=mt[:, 21, :], scalar=1.0 / D, in1=mt[:, 20, :], op0=ALU.mult,
                            op1=ALU.mult).then_inc(s["hms"], 1)
                        dve.wait_ge(s["hms"], upto("hms", n))
                        rsqrt_arg("mh", n, mh_tiny, mt[:, 22, :], 1.0, 1e-8)
                    if step == "m13":
                        rsqrt_step("mh", n, mh_tiny)
                        tt(out=mt[:, 23, :], in0=mt[:, 19, :], in1=mh_tiny[5], op=ALU.mult).then_inc(s["hf"], 1)
                        dve.wait_ge(s["hf"], upto("hf", n))
                        tt(out=ho[:, :, :], in0=ht[:, :, :], in1=bc(mt[:, 23, :], D), op=ALU.mult).then_inc(s["ho"], 1)
                    if step == "m14":
                        dve.wait_ge(s["h1"], upto("h1", n))
                        dve.tensor_reduce(out=mt[:, 18, :], in_=h1[:, :, :], axis=AX, op=ALU.add).then_inc(s["m_sum"], 1)
                        dve.wait_ge(s["m_sum"], upto("m_sum", n))
                        ts(out=mt[:, 20, :], in0=mt[:, 18, :], scalar1=-1.0 / D, scalar2=None,
                           op0=ALU.mult).then_inc(s["m_nm"], 1)
                        dve.wait_ge(s["m_nm"], upto("m_nm", n))
                        tt(out=hc[:, :, :], in0=h1[:, :, :], in1=bc(mt[:, 20, :], D), op=ALU.add).then_inc(s["hc"], 1)
                    if step == "m15":
                        dve.wait_ge(s["hsq2"], upto("hsq2", n))
                        dve.tensor_reduce(out=mt[:, 21, :], in_=hsq[:, :, :], axis=AX, op=ALU.add).then_inc(s["m_var"], 1)
                        dve.wait_ge(s["m_var"], upto("m_var", n))
                        rsqrt_arg("ml", n, ml_tiny, mt[:, 21, :], 1.0 / D, 1e-5)
                    if step == "m16":
                        rsqrt_step("ml", n, ml_tiny)
                        stt(out=mt[:, 22, :], in0=mt[:, 21, :], scalar=1.0 / D, in1=ml_tiny[5], op0=ALU.mult,
                            op1=ALU.mult).then_inc(s["m_a"], 1)
                        dve.wait_ge(s["m_a"], upto("m_a", n))
                        tt(out=mt[:, 23, :], in0=mt[:, 22, :], in1=ml_tiny[5], op=ALU.mult).then_inc(s["m_b"], 1)
                        dve.wait_ge(s["m_b"], upto("m_b", n))
                        rsqrt_arg("mr", n, mr_tiny, mt[:, 23, :], 1.0, 1e-6)
                    if step == "m17":
                        rsqrt_step("mr", n, mr_tiny)
                        tt(out=mt[:, 19, :], in0=ml_tiny[5], in1=mr_tiny[5], op=ALU.mult).then_inc(s["rr"], 1)
                        dve.wait_ge(s["rr"], upto("rr", n))
                        if later(n):
                            dve.wait_ge(s["hnT"], upto("hnT", n - 1))
                        tt(out=hn[:, :, :], in0=hc[:, :, :], in1=bc(mt[:, 19, :], D), op=ALU.mult).then_inc(s["hn"], 1)
                    if c == "b" and 1 <= k <= 4:
                        x, rows, tab = (0, P, ropeq) if k < 3 else (1, D, ropek)
                        dst = t1 if k % 2 else t2
                        dve.wait_ge(s["pe_attn"], upto("pe_attn", n, NTH[step]))
                        if k in (1, 3):
                            if later(n):
                                dve.wait_ge(s["p2"], full("p2", n - 1))
                            if later(n):
                                dve.wait_ge(s["p3"], full("p3", n - 1))
                        tt(out=dst[0:rows, x, :], in0=misc[0:rows, :], in1=tab[:, (k - 1) % 2, :],
                           op=ALU.mult).then_inc(s["t1" if k % 2 else "t2"], 1)
                    if c == "b" and 6 <= k <= 13:
                        b, t = (k - 6) // NT, (k - 6) % NT
                        for h in range(NH):
                            u = (k - 6) * NH + h
                            dve.wait_ge(s["pe_s"], upto("pe_s", n, u + 1))
                            dve.tensor_reduce(out=nm[:, t, b * NH + h:b * NH + h + 1], in_=ring[u % 2][:, 0:(t + 1) * P],
                                              axis=AX, op=ALU.max, negate=True).then_inc(s["smax"], 1)
                    if step == "b14":
                        dve.wait_ge(s["smax"], full("smax", n))
                        if later(n):
                            dve.wait_ge(s["mrow"], upto("mrow", n - 1))
                        dve.tensor_copy(out=mp[:, :, 0, :], in_=nm[:, :, :]).then_inc(s["mp"], 1)
                        dve.wait_ge(s["mp"], upto("mp", n, 1))
                        tt(out=nmr[:, :, :], in0=nm[:, :, :], in1=mp[:, :, 0, :], op=ALU.subtract).then_inc(s["mp"], 1)
                        dve.wait_ge(s["mp"], upto("mp", n, 2))
                        dve.tensor_copy(out=mp[:, :, 1, :], in_=nmr[:, :, :]).then_inc(s["mp"], 1)
                        dve.wait_ge(s["mp"], upto("mp", n, 3))
                        tt(out=mp[:, :, 2, :], in0=nmr[:, :, :], in1=mp[:, :, 1, :],
                           op=ALU.subtract).then_inc(s["mp"], 2)
                    if step in ("b24", "b25"):
                        b = k - 24
                        dve.wait_ge(s["pe_attn"], upto("pe_attn", n, NTH[step]))
                        if later(n):
                            dve.wait_ge(s["ynT"], upto("ynT", n - 1))
                        y = misc[:, :].rearrange("p (g d) -> p g d", d=32)
                        dve.reciprocal(out=rden[:, b, :], in_=y[:, :, HD]).then_inc(s["rden"], 1)
                        dve.wait_ge(s["rden"], upto("rden", n, b + 1))
                        for t in range(NT):
                            r = slice(t * NH, (t + 1) * NH)
                            last = tt(out=yn[:, t, b, :, :], in0=y[:, r, 0:HD], in1=bc(rden[:, b, r], HD), op=ALU.mult)
                        last.then_inc(s["yn"], 1)
                    if step == "b27":
                        dve.wait_ge(s["pe_attn"], upto("pe_attn", n, NTH[step]))
                        y = misc[:, :].rearrange("p (g d) -> p g d", d=D)
                        dve.wait_ge(s["y0b"], upto("y0b", n))
                        tt(out=x2[:, :, :], in0=y, in1=y0b[:, :, :], op=ALU.add).then_inc(s["x2"], 1)
                        dve.wait_ge(s["hy"], upto("hy", n))
                        tt(out=hx[:, :, :], in0=y, in1=hy[:, :, :], op=ALU.add).then_inc(s["hx"], 1)
                    if step == "b28":
                        dve.wait_ge(s["x2sq"], upto("x2sq", n))
                        dve.tensor_reduce(out=bt[:, 6, :], in_=x2sq[:, :, :], axis=AX,
                                          op=ALU.add).then_inc(s["b_var"], 1)
                        dve.wait_ge(s["b_var"], upto("b_var", n))
                        rsqrt_arg("b", n, b_tiny, bt[:, 6, :], 1.0 / D, 1e-6)
                    if step == "b29":
                        rsqrt_step("b", n, b_tiny)
                        if later(n):
                            dve.wait_ge(s["xf"], full("xf", n - 1))
                        for q in range(2):
                            last = tt(out=fl[:, :, q, :], in0=x2[:, :, :], in1=bc(b_tiny[5], D), op=ALU.mult)
                        last.then_inc(s["fl"], 1)
                    if step in ("c0", "c1"):
                        dve.wait_ge(s["cast1"], upto("cast1", n, 2 * k + 2))
                        tt(out=xa[D:P, k, :], in0=xf[D:P, k, :], in1=xb[D:P, k, :],
                           op=ALU.subtract).then_inc(s["xahi"], 1)
                    if step == "c2":
                        dve.wait_ge(s["pe_moe"], upto("pe_moe", n, NTH[step]))
                        dve.tensor_copy(out=lg[:, 0, :, :].rearrange("p g e -> p (g e)"),
                                        in_=misc[:, 0:G * NE]).then_inc(s["lg"], 1)
                        dve.wait_ge(s["lg"], upto("lg", n))
                        done = 0

                        def link(ins):
                            nonlocal done
                            done += 1
                            ins.then_inc(s["r_dve"], 1)
                            dve.wait_ge(s["r_dve"], upto("r_dve", n, done))

                        x, r = [lg[:, q, :, :] for q in range(15)], [ls[:, q, :] for q in range(12)]
                        order = rev[:, :].unsqueeze(1).to_broadcast([P, G, NE])

                        def most(q, src):
                            link(dve.tensor_reduce(out=r[q], in_=src, axis=AX, op=ALU.max))

                        most(0, x[0])
                        link(tt(out=x[1], in0=x[0], in1=bc(r[0], NE), op=ALU.subtract))
                        dve.wait_ge(s["r_act"], upto("r_act", n))
                        link(dve.tensor_reduce(out=r[1], in_=x[2], axis=AX, op=ALU.add))
                        link(dve.reciprocal(out=r[2], in_=r[1]))
                        link(tt(out=x[3], in0=x[2], in1=bc(r[2], NE), op=ALU.mult))
                        most(3, x[3])
                        link(tt(out=x[4], in0=x[3], in1=bc(r[3], NE), op=ALU.is_equal))
                        link(tt(out=x[5], in0=x[4], in1=order, op=ALU.mult))
                        most(4, x[5])
                        link(tt(out=x[6], in0=x[5], in1=bc(r[4], NE), op=ALU.is_equal))
                        link(stt(out=x[7], in0=x[6], scalar=-2.0, in1=x[3], op0=ALU.mult, op1=ALU.add))
                        most(5, x[7])
                        link(tt(out=x[8], in0=x[7], in1=bc(r[5], NE), op=ALU.is_equal))
                        link(tt(out=x[9], in0=x[8], in1=order, op=ALU.mult))
                        most(6, x[9])
                        link(tt(out=x[10], in0=x[9], in1=bc(r[6], NE), op=ALU.is_equal))
                        link(tt(out=x[11], in0=x[6], in1=x[10], op=ALU.add))
                        link(tt(out=x[12], in0=x[11], in1=x[3], op=ALU.mult))
                        link(stt(out=r[7], in0=r[3], scalar=1e-9, in1=r[5], op0=ALU.add, op1=ALU.add))
                        link(dve.reciprocal(out=r[8], in_=r[7]))
                        link(tt(out=x[13], in0=x[12], in1=bc(r[8], NE), op=ALU.mult))
                        assert done == PER["r_dve"], done
                        if later(n):
                            dve.wait_ge(s["wT"], upto("wT", n - 1))
                        dve.tensor_copy(out=wp[:, :, 0, :], in_=x[13]).then_inc(s["wp"], 1)
                        dve.wait_ge(s["wp"], upto("wp", n, 1))
                        tt(out=x[14], in0=x[13], in1=wp[:, :, 0, :], op=ALU.subtract).then_inc(s["wp"], 1)
                        dve.wait_ge(s["wp"], upto("wp", n, 2))
                        dve.tensor_copy(out=wp[:, :, 1, :], in_=x[14]).then_inc(s["wp"], 1)
                        dve.wait_ge(s["wp"], upto("wp", n, 3))
                        tt(out=wp[:, :, 2, :], in0=x[14], in1=wp[:, :, 1, :], op=ALU.subtract).then_inc(s["wp"], 2)
                    if c == "c" and 4 <= k <= 14:
                        j = k - 4
                        w = min(P, F - j * P)
                        for b in range(2):
                            u = 2 * j + b
                            dve.wait_ge(s["silu"], upto("silu", n, u + 1))
                            dve.wait_ge(s["pe_g"], upto("pe_g", n, u + 1))
                            tt(out=sgt[0:w, b, :], in0=gbank[0:w, :], in1=sl[0:w, b, :], op=ALU.mult).then_inc(s["gated"], 1)
                            dve.wait_ge(s["gated"], upto("gated", n, u + 1))
                            dve.wait_ge(s["pe_h3"], upto("pe_h3", n, u + 1))
                            if j >= 2:
                                dve.wait_ge(s["pe_down"], upto("pe_down", n, j - 1))
                            tt(out=hh[0:w, j % 2, b, :], in0=h3bank[0:w, :], in1=sgt[0:w, b, :],
                               op=ALU.mult).then_inc(s["hh"], 1)
                    if step == "c15":
                        dve.wait_ge(s["pe_moe"], upto("pe_moe", n, NTH[step]))
                        if later(n):
                            dve.wait_ge(s["out"], full("out", n - 1))
                        tt(out=ot[:, :, :].rearrange("p g d -> p (g d)"), in0=misc[:, :],
                           in1=hx[:, :, :].rearrange("p g d -> p (g d)"), op=ALU.add).then_inc(s["ot"], 1)

            run(program, dve)

        @block.gpsimd
        def _(_e):
            tt = pool.tensor_tensor
            presets = 0
            for ap, v in ((qs[96:P, :, :], 0.0), (ks[96:P, :, :], 0.0), (va[:, :, :, :], 0.0), (wT[:, :, :], 0.0),
                          (wdec[:, :], 1.0), (mext[:, 0:1], 0.0),
                          (ks[96:96 + PIECES, :, :], 1.0), (va[:, :, :, HD:HD + 1], 1.0)):
                presets += 1
                pool.memset(ap, v).then_inc(cleared, 1)
                pool.wait_ge(cleared, presets)
            pool.wait_ge(cast, CASTS)

            def program(it, stages):
                for step in [x for x in ORDER if x[0] in stages]:
                    n = it - SKEW[step[0]]
                    if step == "g0":
                        if later(n):
                            pool.wait_ge(s["x0"], full("x0", n - 1))
                        pool.tensor_copy(out=idxc[:, :], in_=idx[:, bass.ds(n * G, G)]).then_inc(s["idxc"], 1)
                        pool.wait_ge(s["idxc"], upto("idxc", n))
                        if later(n):
                            pool.wait_ge(s["xres"], upto("xres", n - 1))
                        if later(n):
                            pool.wait_ge(s["xc"], upto("xc", n - 1))
                        tt(out=pad[:, 0:1], in0=nscale[:, 0:1], in1=nscale[:, 0:1], op=ALU.mult)
                        for g in range(G):
                            pool.indirect_dma_start(
                                out=x0[:, g, :], out_offset=None, in_=a["table"],
                                in_offset=bass.IndirectOffsetOnAxis(ap=idxc[:, g:g + 1], axis=0)).then_inc(s["x0"], 16)
                    if step == "g12":
                        pool.wait_ge(s["eexp"], upto("eexp", n))
                        pool.wait_ge(s["kT"], upto("kT", n))
                        tt(out=ek[:, :], in0=eexp[:, :], in1=kT[:, :], op=ALU.mult).then_inc(s["ek"], 1)
                        pool.wait_ge(s["qT"], upto("qT", n))
                        tt(out=wqx[:, :], in0=wexp[:, :], in1=qT[:, :], op=ALU.mult).then_inc(s["wqx"], 1)
                        pool.wait_ge(s["so"], upto("so", n))
                        tt(out=hw[:, :], in0=wexp[:, :], in1=ab[:, 2, :], op=ALU.mult).then_inc(s["hw"], 1)
                        pool.wait_ge(s["wqx"], upto("wqx", n))
                        pool.wait_ge(s["nst"], upto("nst", n))
                        tt(out=prod[:, :], in0=nst[:, :], in1=wqx[:, :], op=ALU.mult).then_inc(s["prod"], 1)
                    if step == "m5":
                        pool.wait_ge(s["dlt"], full("dlt", n))
                        tt(out=dlt[:, 0:NC - 1, :], in0=dlt[:, 0:NC - 1, :], in1=bc(wend[:, 0:NC - 1], P),
                           op=ALU.mult).then_inc(s["dltw"], 1)
                    if step == "m13":
                        pool.wait_ge(s["ho"], upto("ho", n))
                        tt(out=ho[:, :, :], in0=ho[:, :, :], in1=nscale[:, :].unsqueeze(1).to_broadcast([P, G, D]),
                           op=ALU.mult).then_inc(s["hos"], 1)
                        pool.wait_ge(s["hos"], upto("hos", n))
                        if later(n):
                            pool.wait_ge(s["hy"], upto("hy", n - 1))
                        tt(out=h1[:, :, :], in0=ho[:, :, :], in1=xr[:, :, :], op=ALU.add).then_inc(s["h1"], 1)
                    if step == "m17":
                        if later(n):
                            pool.wait_ge(s["y0b"], upto("y0b", n - 1))
                        pool.wait_ge(s["hn"], upto("hn", n))
                        tt(out=y0[:, :, :], in0=hc[:, :, :], in1=bc(ml_tiny[5], D), op=ALU.mult).then_inc(s["y0"], 1)
                    if step == "b0":
                        pool.wait_ge(s["y0"], upto("y0", n))
                        if later(n):
                            pool.wait_ge(s["hx"], upto("hx", n - 1))
                        tt(out=hy[:, :, :], in0=h1[:, :, :], in1=y0[:, :, :], op=ALU.add).then_inc(s["hy"], 1)
                        pool.tensor_copy(out=y0b[:, :, :], in_=y0[:, :, :]).then_inc(s["y0b"], 1)
                    if step in ("b2", "b4"):
                        x, rows, dst = (0, P, qp) if step == "b2" else (1, D, kp)
                        pool.wait_ge(s["t2"], upto("t2", n, x + 1))
                        tt(out=qr[0:rows, x, :], in0=t1[0:rows, x, :], in1=t2[0:rows, x, :],
                           op=ALU.add).then_inc(s["qr"], 1)
                        pool.wait_ge(s["p1"], upto("p1", n, x + 1))
                        tt(out=t1[0:rows, x, :], in0=qr[0:rows, x, :], in1=dst[0:rows, 0, :],
                           op=ALU.subtract).then_inc(s["r1"], 1)
                        pool.wait_ge(s["p2"], upto("p2", n, x + 1))
                        tt(out=dst[0:rows, 2, :], in0=t1[0:rows, x, :], in1=dst[0:rows, 1, :],
                           op=ALU.subtract).then_inc(s["p3"], 1)
                    if step in ("c0", "c1"):
                        k = int(step[1:])
                        if k or later(n):
                            pool.wait_ge(s["xblo"], upto("xblo", n, k))
                        pool.wait_ge(s["cast1"], upto("cast1", n, 2 * k + 1))
                        tt(out=xres[:, :], in0=xf[0:D, k, :], in1=xa[0:D, k, :], op=ALU.subtract).then_inc(s["cres"], 1)
                        pool.wait_ge(s["cast2"], upto("cast2", n, k + 1))
                        tt(out=xb[0:D, k, :], in0=xres[:, :], in1=x2p[:, :], op=ALU.subtract).then_inc(s["xblo"], 1)

            run(program, pool)
    return nc


def _host(x):
    def bd(w):
        z = np.zeros((2 * w.shape[0], 2 * w.shape[1]), np.float32)
        z[:w.shape[0], :w.shape[1]] = w
        z[w.shape[0]:, w.shape[1]:] = w
        return z

    def twice(v):
        return np.ascontiguousarray(np.tile(np.reshape(v, (-1, 1)), (2, 1)))

    h = {}
    r = np.arange(P)
    h["ident"] = np.eye(P, dtype=np.float32)
    up = np.where(r[None, :] > r[:, None], np.float32(NEG), np.float32(0))
    h["maskf"] = np.concatenate([up, up.T], 1)
    h["chunkmask"] = ((r[:, None] <= r[None, :]) & (r[:, None] // L == r[None, :] // L)).astype(np.float32)
    h["batchmask"] = (r[:, None] // D == r[None, :] // D).astype(np.float32)
    h["restart"] = np.tile((np.arange(T) % L != 0).astype(np.float32), (P, 1))
    h["onesbd"] = (r[:, None] // D == np.arange(2)[None, :]).astype(np.float32)
    h["rev"] = np.tile(NE - np.arange(NE, dtype=np.float32), (P, 1))
    Wg, bg = x["L0_attn_Wg"], x["L0_attn_bg"]
    ws = [x["L0_attn_Wq"], x["L0_attn_Wk"], x["L0_attn_Wv"], Wg[:, :D], Wg[:, D:2 * D], Wg[:, 2 * D:]]
    bs = [x["L0_attn_bq"], x["L0_attn_bk"], x["L0_attn_bv"], bg[:D], bg[D:2 * D], bg[2 * D:]]
    h["proj"] = np.stack([bd(w) for w in ws], 1)
    h["bias"] = np.concatenate([twice(b) for b in bs], 1)
    h["ibias"] = twice(x["L0_attn_input_bias"])
    h["nscale"] = np.tile(x["L0_attn_norm_scale"], (P, 1))
    h["ln1"], h["ln2"] = twice(x["L0_ffn_ln1_w"]), twice(x["L0_ffn_ln2_w"])

    swap = (np.arange(HD) + HD // 2) % HD

    def heads(w, n, order):
        w = np.transpose(np.reshape(w, (n, HD, D))[:, order, :], (2, 1, 0))
        z = np.zeros((2, D, HD, 2, n), np.float32)
        z[0, :, :, 0, :] = w
        z[1, :, :, 1, :] = w
        return np.reshape(z, (P, HD * 2 * n))

    same = np.arange(HD)
    h["wq"] = np.stack([heads(x["L0_ffn_wq"], NH, same), heads(x["L0_ffn_wq"], NH, swap)], 1)
    h["wk"] = np.stack([heads(x["L0_ffn_wk"], NKV, same), heads(x["L0_ffn_wk"], NKV, swap)], 1)
    h["wv"] = bd(np.transpose(x["L0_ffn_wv"]))
    h["wo"] = bd(np.transpose(x["L0_ffn_wo"]))
    inv = 1.0 / 10000.0 ** (np.arange(0, HD, 2, dtype=np.float32) / HD)
    ang = np.outer(np.arange(T, dtype=np.float32), inv)
    ang = np.concatenate([ang, ang], -1).T
    sign = np.where(np.arange(HD) < HD // 2, -1.0, 1.0)[:, None]
    cs = np.stack([np.cos(ang), np.sin(ang) * sign], 1).astype(np.float32)
    h["ropeq"] = np.repeat(cs * np.float32(HD ** -0.5), 2 * NH, 0)
    h["ropek"] = np.repeat(cs, 2 * NKV, 0)
    h["rw"] = np.concatenate([np.transpose(x["L0_ffn_router_w"]), np.zeros((D, NE), np.float32)], 0)
    for name in ("w1", "w3"):
        w = np.reshape(np.transpose(x["L0_ffn_" + name], (2, 0, 1)), (D, F))
        h[name] = np.concatenate([w, w], 0)
    w = np.zeros((NJ * P, D), np.float32)
    w[:F] = np.reshape(np.transpose(x["L0_ffn_w2"], (0, 2, 1)), (F, D))
    h["w2"] = np.transpose(np.reshape(w, (NJ, P, D)), (1, 0, 2))
    z = np.zeros((P, NJ * P), np.float32)
    for p in range(PIECES):
        for e in range(NE):
            z[p * NE + e, e * HID:(e + 1) * HID] = 1.0
    h["selg"] = z
    h["idx"] = np.reshape(np.transpose(np.reshape(x["x"], (NP, 2, NT, P)), (3, 0, 2, 1)), (P, NP * G))
    h["table"] = np.reshape(x["L0_tok_ple_table"], (VOCAB * HIDDEN // D, D))
    return {k: np.ascontiguousarray(v) for k, v in h.items()}


def kernel(**inputs):
    import concourse.bacc as bacc
    from concourse.bass_utils import run_bass_kernel_spmd

    arrays = _host({k: np.asarray(v) for k, v in inputs.items()})
    nc = bacc.Bacc("TRN2", target_bir_lowering=False, num_devices=1)
    a = {k: nc.dram_tensor("in_" + k, v.shape, mybir.dt.from_np(v.dtype), kind="ExternalInput").ap()
         for k, v in arrays.items()}
    a["out"] = nc.dram_tensor("out", (B, T, D), mybir.dt.float32, kind="ExternalOutput").ap()
    tower(nc, a)
    r = run_bass_kernel_spmd(nc, [{"in_" + k: v for k, v in arrays.items()}], core_ids=[0])
    return r.results[0]["out"]
```

```python
import numpy as np
import concourse.bass as bass
from concourse import mybir
from concourse.alu_op_type import AluOpType as ALU
from contextlib import ExitStack

B, T, D = 32, 512, 64
P = 128
NP = B // 2
NT = T // P
G = 2 * NT
VOCAB, HIDDEN, LAYER = 32000, 512, 3
L = 64
NC = T // L
NH, NKV, HD = 4, 2, 16
NE, HID = 8, 170
F = NE * HID
NJ = (F + P - 1) // P
NEG = -1.0e30
CASTS = 22
PIECES = 3


def tower(nc, a):
    f32, bf16, i32 = mybir.dt.float32, mybir.dt.bfloat16, mybir.dt.int32
    ACT, AX = mybir.ActivationFunctionType, mybir.AxisListType.X
    pe, act, dve, pool, sp = nc.tensor, nc.scalar, nc.vector, nc.gpsimd, nc.sync
    ctx = ExitStack()

    def sb(name, shape, dt=f32):
        return ctx.enter_context(nc.sbuf_tensor(name, shape, dt))

    def dram(name, shape, dt):
        return nc.dram_tensor(name, shape, dt, kind="Internal").ap()

    with ctx:
        ident = sb("ident", [P, P])
        identb = sb("identb", [P, P], bf16)
        maskb = sb("maskb", [P, 2 * P], bf16)
        chunkmask = sb("chunkmask", [P, P])
        batchmask = sb("batchmask", [P, P])
        restart = sb("restart", [P, T])
        onesbd = sb("onesbd", [P, 2])
        half3 = sb("half3", [P, 2 * G])
        rev = sb("rev", [P, NE])
        proj = sb("proj", [P, 6, P])
        bias = sb("bias", [P, 6])
        ibias = sb("ibias", [P, 1])
        bi = sb("bi", [P, 2])
        nscale = sb("nscale", [P, D])
        ln1 = sb("ln1", [P, 1])
        ln2 = sb("ln2", [P, 1])
        wq = sb("wq", [P, 2, P])
        wk = sb("wk", [P, 2, D])
        wv = sb("wv", [P, D])
        wo = sb("wo", [P, P])
        ropeq = sb("ropeq", [P, 2, T])
        ropek = sb("ropek", [D, 2, T])
        rw = sb("rw", [P, NE])
        w13 = sb("w13", [P, 2, 3, F], bf16)
        w2 = sb("w2", [P, NJ, D])
        selg = sb("selg", [P, NJ * P], bf16)
        idx = sb("idx", [P, NP * G], i32)
        idxc = sb("idxc", [P, G], i32)

        x0 = sb("x0", [P, G, D])
        xr = sb("xr", [P, G, D])
        st = sb("st", [P, 8, G])
        xc = sb("xc", [P, G, D])
        xn = xc
        xm = sb("xm", [P, G, D])
        xT = sb("xT", [P, T])
        qT = sb("qT", [P, T])
        kT = sb("kT", [P, T])
        ab = sb("ab", [P, 3, T])
        mn = sb("mn", [P, 3, T])
        li = sb("li", [P, T])
        mext = sb("mext", [P, T + 1])
        gcum = sb("gcum", [P, T])
        wexp = sb("wexp", [P, T])
        eexp = sb("eexp", [P, T])
        uT = sb("uT", [P, T])
        ek = sb("ek", [P, T])
        wdec = sb("wdec", [P, T])
        nst = ek
        wqx = sb("wqx", [P, T])
        prod = wqx
        hw = sb("hw", [P, T])
        pad = sb("pad", [P, 1])
        ktok = sb("ktok", [P, NT, P])
        utok = sb("utok", [P, NT, P])
        atm = sb("atm", [P, 2, T])
        dlt = sb("dlt", [P, NC, P])
        stT = sb("stT", [P, NC - 1, P])
        hgT = sb("hgT", [P, T])
        ht = sb("ht", [P, G, D])
        mt = sb("mt", [P, 24, G])
        h1 = sb("h1", [P, G, D])
        y0 = sb("y0", [P, G, D])
        hc = sb("hc", [P, G, D])
        ho = ht
        hn = sb("hn", [P, G, D])
        y0b = sb("y0b", [P, G, D])
        hy = sb("hy", [P, G, D])
        hnT = sb("hnT", [P, T])
        t1 = sb("t1", [P, 2, T])
        t2 = sb("t2", [P, 2, T])
        qr = t2
        qp = sb("qp", [P, PIECES, T], bf16)
        kp = sb("kp", [D, PIECES, T], bf16)
        qs = sb("qs", [P, 2 * NH, T], bf16)
        ks = sb("ks", [P, 2 * NKV, T], bf16)
        va = sb("va", [P, NT, 2 * NKV, 32])
        nm = sb("nm", [P, NT, 2 * NH])
        nmr = sb("nmr", [P, NT, 2 * NH])
        mp = sb("mp", [P, NT, PIECES, 2 * NH], bf16)
        mrow = sb("mrow", [PIECES * 2 * NH, T], bf16)
        pr = sb("pr", [P, 2, NH, T])
        yT = sb("yT", [P, 2, T])
        rden = sb("rden", [P, 2, NT * NH])
        x2 = sb("x2", [P, G, D])
        bt = sb("bt", [P, 7, G])
        hx = sb("hx", [P, G, D])
        xf = sb("xf", [P, 2, T])
        xa = sb("xa", [P, 2, T], bf16)
        xb = sb("xb", [P, 2, T], bf16)
        xres = sb("xres", [D, T])
        x2p = sb("x2p", [D, T], bf16)
        lg = sb("lg", [P, 15, G, NE])
        ls = sb("ls", [P, 12, G])
        wp = sb("wp", [P, G, PIECES, NE], bf16)
        wT = sb("wT", [P, 2, T], bf16)
        sl = sb("sl", [P, 2, T])
        sgt = sl
        moT = sl[:, 0, :]
        xsq, x2sq = [ab[:, q, :].rearrange("p (g d) -> p g d", d=D) for q in range(2)]
        fl = pr[:, 0, 0:2, :].rearrange("p a t -> p (a t)").rearrange("p (g a d) -> p g a d", a=2, d=D)
        ynT = hnT
        yn = x2[:, :, :].rearrange("p (t b) (h d) -> p t b h d", b=2, h=NH)
        hsq = atm[:, 0, :].rearrange("p (g d) -> p g d", d=D)
        hh = sb("hh", [P, 2, 2, T])
        ot = sb("ot", [P, G, D])

        wtmp = pr[:, :, :, :].rearrange("p a h t -> p (a h t)")[:, 0:2 * F].rearrange("p (m f) -> p m f", m=2)
        maskf = mn[:, 1, 0:2 * P]
        selgf = ab[:, :, :].rearrange("p a t -> p (a t)")[:, 0:NJ * P]

        banks = [ctx.enter_context(nc.psum_tensor(f"bank{i}", [P, T], f32)) for i in range(8)]
        ybank, h1bank, gbank, h3bank, obank = banks[2], banks[3], banks[4], banks[5], banks[7]
        sring, ering = banks[0:2], (banks[0], banks[1], banks[5])

        qscr = dram("qscr", [PIECES * HD, 2 * NH, T], bf16)
        kscr = dram("kscr", [PIECES * HD, 2 * NKV, T], bf16)
        mscr = dram("mscr", [PIECES, 2 * NH, T], bf16)


        SKEW = dict(f=0, g=1, m=2, q=2, b=3, a=4, e=4, c=5, d=5)
        SLOTS = [row.split() for row in (
            "c0 d0 m0 b38 b39",
            "c1 d1 m1 b5 g1",
            "c2 d2 b40 b41 m2 g2 a32",
            "c3 d3 m3 a33",
            "c4 d4 m4 g3",
            "c5 d5 m5",
            "c6 d6 a34 m6",
            "c7 b6 d7 b7 f0",
            "c8 b8 d8 a35 b42",
            "c9 b9 d9 b10 m7",
            "c10 b11 d10 m8 a36",
            "c11 b12 d11 b13 g4 a37",
            "c12 b14 d12 m9 a38",
            "c13 b15 d13 m11",
            "c14 b16 d14 m10",
            "c15 b17 d15 g5 m12 m13",
            "c16 b18 d16 g6",
            "c17 b19 d17 g7 m14",
            "c18 b20 d18 g8 b43",
            "c19 b21 d19 g9 m15 g17",
            "c20 d20 b22 e0 m16 g18",
            "c21 d21 e1")]
        SECOND = ("c22 g10 c23 e9 m17 g19 e2 g11 q0 b23 e10 g12 g13 q1 b24 e5 q2 e7 b25 g14 q3 e8 b26 q4 e6 "
                  "b27 g15 e11 b28 e12 b29 e3 g16 b30 e4 b31").split()
        ORDER = [step for row in SLOTS for step in row] + SECOND
        READERS, held = [], []
        for row in SLOTS:
            filler = [step for step in row if not (step[0] in "cd" or (step[0] == "b" and 6 <= int(step[1:]) <= 21))]
            READERS += [step for step in row if step not in filler] + held
            held = filler
        READERS += held + SECOND
        READ = dict(g4=[("xT", 1)], g5=[("qT", 1)], g6=[("kT", 1)], g7=[("gx", 1)], g8=[("gx", 2)], g9=[("gx", 3)],
                    g15=[("uT", 1)],
                    m0=[("ktok", 1)], m1=[("utok", 1)], m2=[("atm", 1)], m3=[("atm", 2)], m4=[("dlt", 1)],
                    m5=[("dlt", 2)], m7=[("stT", 1)], m8=[("stT", 2)], m9=[("hgT", 1)], m10=[("ht", 1)],
                    m11=[("dabs", 1)],
                    q0=[("hnT", 1)], q1=[("t1", 1)], q2=[("t2", 1)], q3=[("t1", 2)], q4=[("t2", 2)], b5=[("va", 1)],
                    b22=[("mrow", 1)], a32=[("yn", 1)], a33=[("yn", 2)], a34=[("ynT", 1)], a35=[("x2", 1), ("hx", 1)],
                    e0=[("xf", 1)], e1=[("xf", 2)], e2=[("lg", 1)], e3=[("wT", 1)], c23=[("ot", 1)])
        TENANTS = [step for step in ORDER if step in READ]
        NTH = {step: 1 + [t for t in TENANTS if t[0] == step[0]].index(step) for step in TENANTS}
        BANK, used = {}, {bank: bank for bank in range(8)}
        for step in TENANTS:
            at = ORDER.index(step)
            if at > ORDER.index("c22"):
                free = (6, 3, 4, 7)
            elif ORDER.index("b6") - 4 < at < ORDER.index("b21"):
                free = (6, 2)
            else:
                free = (6, 2, 0, 1)
            BANK[step] = min(free, key=used.get)
            used[BANK[step]] = 100 + at
        USERS = [[] for _ in range(8)]
        for step in ORDER:
            if step in BANK:
                USERS[BANK[step]].append((step, READ[step]))
            if step == "c0":
                for bank, name in ((3, "silu"), (4, "gated"), (5, "hh"), (7, "moT")):
                    USERS[bank].append((step, [(name, {"moT": 1}.get(name, 2 * NJ))]))
            if step == "b6":
                for bank in (0, 1):
                    USERS[bank].append((step, [("smax", 4 * 2 * NH)]))
            if step == "b23":
                for bank in (0, 1, 5):
                    USERS[bank].append((step, [("pexp", 4 * 2 * NH)]))
            if step == "b24":
                USERS[2].append((step, [("yT", 2)]))

        PER = dict(
            idxc=1, x0=16 * G, xm=1, xres=1, g_sum=1, g_nm=1, xc=1, xsq=1, g_var=1, g_v=1, g_bits=1, g_half=1, g_guess=1, g_newton=12, xn=1,
            xT=1, qT=1, kT=1, gx=3, gabs=1, gexp=1, gln=1, lf=1, lso=1, si=1, so=1, li=1, mscan=1, lfc=1,
            gcum=1, aw=1, ae=1, wexp=1, eexp=1, uT=1, ek=1, wdec=1, nst=1, wqx=1, prod=1, hw=1,
            ktok=1, utok=1, atm=2, dlt=2, dltw=1, state=NC - 2, stT=2, hgT=1, ht=1, dabs=1, den=1, rd=1, hsq=1, hsum=1, rd2=1,
            hms=1, mh_v=1, mh_bits=1, mh_half=1, mh_guess=1, mh_newton=12, hf=1, ho=1, hos=1, h1=1, m_sum=1, m_nm=1, hc=1, hsq2=1, m_var=1, ml_v=1, mr_v=1,
            ml_bits=1, ml_half=1, ml_guess=1, ml_newton=12, hn=1, y0=1,
            hy=1, y0b=1, hnT=1, t1=2, t2=2, qr=2, p1=2, r1=2, p2=2, p3=2, qk_out=32, qk_in=16 * 7, va=1, smax=4 * 2 * NH,
            mp=5, mrow=1, m_out=16, m_in=16, pexp=4 * 2 * NH, yT=2, rden=2, yn=2, ynT=1, x2=1, hx=1, x2sq=1, b_var=1,
            b_v=1, b_bits=1, b_half=1, b_guess=1, b_newton=12, fl=1,
            xf=2, cast1=4, xahi=2, cres=2, cast2=2, xblo=2, hxc=1, lg=1, r_dve=21, r_act=1, wp=5, wT=1,
            silu=2 * NJ, gated=2 * NJ, hh=2 * NJ, moT=1, ot=1, out=32,
            pe_gate=7, pe_mem=11, pe_qk=5, pe_attn=2, pe_tail=4, pe_prep=4, pe_moe=1, pe_s=4 * 2 * NH, pe_st=4 * 2 * NH, pe_pv=8,
            pe_h1=2 * NJ, pe_g=2 * NJ, pe_h3=2 * NJ, pe_down=NJ)
        s = {name: ctx.enter_context(nc.semaphore(name)) for name in PER}
        loaded = ctx.enter_context(nc.semaphore("loaded"))
        cleared = ctx.enter_context(nc.semaphore("cleared"))
        cast = ctx.enter_context(nc.semaphore("cast"))
        setup = ctx.enter_context(nc.semaphore("setup"))

        PE_OF = dict(g="pe_gate", m="pe_mem", q="pe_qk", b="pe_attn", a="pe_tail", e="pe_prep", c="pe_moe")

        def upto(name, n, k=1):
            return n * PER[name] + k

        def full(name, n):
            return upto(name, n, PER[name])

        def later(n):
            return type(n) is not int or n > 0

        FIRST = SKEW["c"] + 1

        def active(it):
            return [c for c in SKEW if 0 <= it - SKEW[c] < NP]

        def before(step, bank, it, stages):
            mine = [u for u in USERS[bank] if u[0][0] in stages]
            at = [u[0] for u in mine].index(step)
            if at > 0:
                prev, reads = mine[at - 1]
            else:
                last = active(it - 1) if type(it) is int else list(SKEW)
                mine = [u for u in USERS[bank] if u[0][0] in last]
                if not mine:
                    return []
                (prev, reads), it = mine[-1], it - 1
            return [(name, upto(name, it - SKEW[prev[0]], k)) for name, k in reads]

        def run(program, engine):
            for it in range(FIRST):
                program(it, active(it))
            with engine.Fori(FIRST, NP) as it:
                program(it, list(SKEW))
            for it in range(NP, NP + SKEW["c"]):
                program(it, active(it))

        def bc(t, n):
            return t.unsqueeze(2).to_broadcast([t.shape[0], t.shape[1], n])

        def rsqrt_guess(site, n, tiny):
            dve.tensor_scalar(out=tiny[2].bitcast(i32), in0=tiny[0].bitcast(i32), scalar1=1, scalar2=None,
                              op0=ALU.arith_shift_right).then_inc(s[site + "_bits"], 1)
            dve.tensor_scalar(out=tiny[1], in0=tiny[0], scalar1=-0.5, scalar2=None,
                              op0=ALU.mult).then_inc(s[site + "_half"], 1)
            dve.wait_ge(s[site + "_bits"], upto(site + "_bits", n))
            dve.tensor_scalar(out=tiny[4].bitcast(i32), in0=tiny[2].bitcast(i32), scalar1=-1.0,
                              scalar2=float(0x5F3759DF), op0=ALU.mult, op1=ALU.add).then_inc(s[site + "_guess"], 1)

        def newton(site, n, tiny):
            name = site + "_newton"
            pool.wait_ge(s[site + "_half"], upto(site + "_half", n))
            pool.wait_ge(s[site + "_guess"], upto(site + "_guess", n))
            for r in range(3):
                if r:
                    pool.wait_ge(s[name], upto(name, n, 4 * r))
                pool.tensor_tensor(out=tiny[2], in0=tiny[4], in1=tiny[4], op=ALU.mult).then_inc(s[name], 1)
                pool.wait_ge(s[name], upto(name, n, 4 * r + 1))
                pool.tensor_tensor(out=tiny[3], in0=tiny[2], in1=tiny[1], op=ALU.mult).then_inc(s[name], 1)
                pool.wait_ge(s[name], upto(name, n, 4 * r + 2))
                pool.tensor_tensor(out=tiny[2], in0=tiny[3], in1=half3[:, 0:tiny[3].shape[1]],
                                   op=ALU.add).then_inc(s[name], 1)
                pool.wait_ge(s[name], upto(name, n, 4 * r + 3))
                pool.tensor_tensor(out=tiny[4], in0=tiny[4], in1=tiny[2], op=ALU.mult).then_inc(s[name], 1)

        g_tiny = [st[:, r, :] for r in range(5)]
        mh_tiny = [mt[:, r, :] for r in range(5)]
        ml_tiny = [mt[:, 5 + 2 * r:7 + 2 * r, :].rearrange("p a g -> p (a g)") for r in range(5)]
        b_tiny = [bt[:, r, :] for r in range(5)]
        wend = wexp[:, :].rearrange("p (c l) -> p c l", l=L)[:, :, L - 1]
        UNITS = [(b, t, h) for b in range(2) for t in range(NT) for h in range(NH)]
        block = ctx.enter_context(nc.Block())

        @block.sync
        def _(_e):
            for dst, name in ((ident, "ident"), (maskf, "maskf"), (chunkmask, "chunkmask"), (batchmask, "batchmask"),
                              (restart, "restart"), (onesbd, "onesbd"), (rev, "rev"), (proj, "proj"), (bias, "bias"),
                              (ibias, "ibias"), (nscale, "nscale"), (ln1, "ln1"), (ln2, "ln2"), (wq, "wq"),
                              (wk, "wk"), (wv, "wv"), (wo, "wo"), (ropeq, "ropeq"), (ropek, "ropek"), (rw, "rw"),
                              (w2, "w2"), (idx, "idx")):
                sp.dma_start(dst if type(dst) is bass.AP else dst[(slice(None),) * len(dst.shape)], a[name]).then_inc(loaded, 16)
            sp.dma_start(wtmp[:, 0, :], a["w1"]).then_inc(loaded, 16)
            sp.dma_start(wtmp[:, 1, :], a["w3"]).then_inc(loaded, 16)
            sp.dma_start(selgf, a["selg"]).then_inc(loaded, 16)

            def program(it, stages):
                for step in [x for x in ORDER if x[0] in stages]:
                    n = it - SKEW[step[0]]
                    misc = banks[BANK[step]] if step in BANK else None
                    if step == "b41":
                        sp.wait_ge(s["p3"], upto("p3", n, 1))
                        sp.dma_start(qscr.rearrange("(p d) g t -> (d g) p t", p=PIECES),
                                     qp[:, :, :]).then_inc(s["qk_out"], 16)
                        sp.wait_ge(s["p3"], upto("p3", n, 2))
                        sp.dma_start(kscr.rearrange("(p d) g t -> (d g) p t", p=PIECES),
                                     kp[:, :, :]).then_inc(s["qk_out"], 16)
                        sp.wait_ge(s["qk_out"], full("qk_out", n))
                        if later(n):
                            sp.wait_ge(s["pe_st"], full("pe_st", n - 1))
                        for dst, src, at, rows, frm in (
                                (qs, qscr, 0, 16, 0), (qs, qscr, 16, 16, 0), (qs, qscr, 32, 32, 0),
                                (qs, qscr, 64, 32, 16), (ks, kscr, 0, 48, 0), (ks, kscr, 48, 32, 0),
                                (ks, kscr, 80, 16, 0)):
                            sp.dma_start(dst[at:at + rows, :, :], src[frm:frm + rows, :, :]).then_inc(s["qk_in"], 16)
                    if step == "b22":
                        sp.wait_ge(s["mrow"], upto("mrow", n))
                        sp.dma_start(mscr.rearrange("p g t -> (p g) t"), mrow[:, :]).then_inc(s["m_out"], 16)
                        sp.wait_ge(s["m_out"], full("m_out", n))
                        sp.dma_start(qs[PIECES * 2 * HD:PIECES * 2 * HD + PIECES, :, :], mscr).then_inc(s["m_in"], 16)
                    if step == "c23":
                        sp.wait_ge(s["ot"], upto("ot", n))
                        for b in range(2):
                            dst = a["out"][bass.ds(n * 2 + b, 1), :, :].rearrange("o (i p) d -> p (o i) d", p=P)
                            src = ot[:, :, :].rearrange("p (i b) d -> p i b d", b=2)[:, :, b, :]
                            sp.dma_start(dst, src).then_inc(s["out"], 16)

            run(program, sp)
            sp.wait_ge(s["out"], full("out", NP - 1))

        @block.tensor
        def _(_e):
            def mm(out, lhsT, rhs, start=True, stop=True, **k):
                return pe.matmul(out, lhsT, rhs, start=start, stop=stop, **k)

            def four(step, src):
                misc = banks[BANK[step]]
                for t in range(NT):
                    last = pe.transpose(misc[:, t * P:(t + 1) * P], src(t), ident[:, :])
                last.then_inc(s[PE_OF[step[0]]], 1)

            def done(step, last):
                last.then_inc(s[PE_OF[step[0]]], 1)

            pe.wait_ge(loaded, 16 * 25)
            pe.wait_ge(cleared, 9)
            pe.wait_ge(cast, CASTS)

            def down(n, j):
                rows = min(P, F - j * P)
                pe.wait_ge(s["hh"], upto("hh", n, 2 * j + 2))
                for b in range(2):
                    last = mm(obank[D * b:D * b + D, :], w2[0:rows, j, :], hh[0:rows, j % 2, b, :],
                              start=j == 0, stop=j == NJ - 1)
                last.then_inc(s["pe_down"], 1)

            def up(n, u):
                b = u % 2
                cols = slice(u // 2 * P, min(F, (u // 2 + 1) * P))
                w = cols.stop - cols.start
                if u:
                    pe.wait_ge(s["silu"], upto("silu", n, u))
                for p, mov in enumerate((xa, xa, xb)):
                    last = mm(h1bank[0:w, :], w13[:, 0, p, cols], mov[:, b, :], start=p == 0, stop=p == 2)
                last.then_inc(s["pe_h1"], 1)
                if u:
                    pe.wait_ge(s["gated"], upto("gated", n, u))
                mm(gbank[0:w, :], selg[:, cols], wT[:, b, :]).then_inc(s["pe_g"], 1)

            def pv(n, k):
                b, t = k // NT, k % NT
                pe.wait_ge(s["pexp"], upto("pexp", n, NH * (k + 1)))
                if t == 0:
                    if b:
                        pe.wait_ge(s["yT"], upto("yT", n, 1))
                for h in range(NH):
                    last = mm(ybank[32 * h:32 * h + 32, t * P:T], va[:, t, b * NKV + h // 2, :],
                              pr[:, k % 2, h, 0:T - t * P], start=t == 0, stop=t == NT - 1)
                last.then_inc(s["pe_pv"], 1)

            def program(it, stages):
                for step in [x for x in ORDER if x[0] in stages]:
                    n = it - SKEW[step[0]]
                    misc = banks[BANK[step]] if step in BANK else None
                    c, k = step[0], int(step[1:])
                    if step in BANK:
                        for name, value in before(step, BANK[step], it, stages):
                            pe.wait_ge(s[name], value)
                    if step == "g4":
                        pe.wait_ge(s["xn"], upto("xn", n))
                        four(step, lambda t: xn[:, 2 * t:2 * t + 2, :].rearrange("p b d -> p (b d)"))
                    if c == "g" and 5 <= k <= 9:
                        if k == 5:
                            pe.wait_ge(s["xT"], upto("xT", n))
                        done(step, mm(misc[:, :], proj[:, (0, 1, 3, 4, 5)[k - 5], :], xT[:, :]))
                    if step == "g15":
                        done(step, mm(misc[:, :], proj[:, 2, :], xT[:, :]))
                    if step == "m0":
                        pe.wait_ge(s["kT"], upto("kT", n))
                        four(step, lambda t: kT[:, t * P:(t + 1) * P])
                    if step == "m1":
                        pe.wait_ge(s["uT"], upto("uT", n))
                        four(step, lambda t: uT[:, t * P:(t + 1) * P])
                    if step in ("m2", "m3"):
                        b = k - 2
                        for t in range(NT):
                            last = mm(misc[:, t * P:(t + 1) * P], kT[D * b:D * b + D, t * P:(t + 1) * P],
                                      qT[D * b:D * b + D, t * P:(t + 1) * P])
                        done(step, last)
                    if step in ("m4", "m5"):
                        if step == "m4":
                            pe.wait_ge(s["ktok"], upto("ktok", n))
                            pe.wait_ge(s["utok"], upto("utok", n))
                        par = k - 4
                        for q in range(NT - par):
                            last = mm(misc[:, q * P:(q + 1) * P], utok[L * par:L * par + L, q, :],
                                      ktok[L * par:L * par + L, q, :])
                        done(step, last)
                    if step in ("m7", "m8"):
                        pe.wait_ge(s["state"], full("state", n))
                        lo, hi = ((0, 4), (4, NC - 1))[k - 7]
                        for j in range(lo, hi):
                            last = pe.transpose(misc[:, (j - lo) * P:(j - lo + 1) * P], dlt[:, j, :], ident[:, :])
                        done(step, last)
                    if step == "m9":
                        pe.wait_ge(s["stT"], full("stT", n))
                        pe.wait_ge(s["atm"], full("atm", n))
                        for j in range(1, NC):
                            mm(misc[:, j * L:(j + 1) * L], stT[:, j - 1, :], qT[:, j * L:(j + 1) * L], start=j == 1,
                               stop=False, skip_group_check=True)
                        for t in range(NT):
                            for b in range(2):
                                last = mm(misc[D * b:D * b + D, t * P:(t + 1) * P], utok[:, t, D * b:D * b + D],
                                          atm[:, b, t * P:(t + 1) * P], start=False, stop=t == NT - 1,
                                          skip_group_check=True)
                        done(step, last)
                    if step == "m10":
                        pe.wait_ge(s["hgT"], upto("hgT", n))
                        four(step, lambda t: hgT[:, t * P:(t + 1) * P])
                    if step == "m11":
                        pe.wait_ge(s["prod"], upto("prod", n))
                        for t in range(NT):
                            last = mm(misc[:, 2 * t:2 * t + 2], prod[:, t * P:(t + 1) * P], onesbd[:, :])
                        done(step, last)
                    if step == "q0":
                        pe.wait_ge(s["hn"], upto("hn", n))
                        four(step, lambda t: hn[:, 2 * t:2 * t + 2, :].rearrange("p b d -> p (b d)"))
                    if step in ("q1", "q2"):
                        if step == "q1":
                            pe.wait_ge(s["hnT"], upto("hnT", n))
                        done(step, mm(misc[:, :], wq[:, k - 1, :], hnT[:, :]))
                    if step in ("q3", "q4"):
                        done(step, mm(misc[0:D, :], wk[:, k - 3, :], hnT[:, :]))
                    if step == "b5":
                        for t in range(NT):
                            last = mm(misc[:, t * D:(t + 1) * D], hnT[:, t * P:(t + 1) * P], wv[:, :])
                        done(step, last)
                    if c == "b" and 6 <= k <= 21:
                        b, t = (k - 6) // 2 // NT, (k - 6) // 2 % NT
                        if k == 6:
                            pe.wait_ge(s["qk_in"], full("qk_in", n))
                            for bank in (0, 1):
                                for name, value in before(step, bank, it, stages):
                                    pe.wait_ge(s[name], value)
                        for u in range((k - 6) * 2, (k - 6) * 2 + 2):
                            h = u % NH
                            if u >= 2:
                                pe.wait_ge(s["smax"], upto("smax", n, u - 1))
                            mm(sring[u % 2][:, 0:(t + 1) * P], qs[:, b * NH + h, t * P:(t + 1) * P],
                               ks[:, b * NKV + h // 2, 0:(t + 1) * P], stop=False)
                            mm(sring[u % 2][:, t * P:(t + 1) * P], identb[:, :], maskb[:, 0:P],
                               start=False).then_inc(s["pe_s"], 1)
                    if step == "b22":
                        pe.wait_ge(s["mp"], full("mp", n))
                        for t in range(NT):
                            last = pe.transpose(misc[:, :].bitcast(bf16)[0:PIECES * 2 * NH, t * P:(t + 1) * P],
                                                mp[:, t, :, :].rearrange("p a b -> p (a b)"), identb[:, :])
                        done(step, last)
                    if c == "b" and 23 <= k <= 30:
                        b, t = (k - 23) // NT, (k - 23) % NT
                        if k == 23:
                            pe.wait_ge(s["m_in"], upto("m_in", n, 16))
                            for bank in (0, 1, 5):
                                for name, value in before(step, bank, it, stages):
                                    pe.wait_ge(s[name], value)
                        if k == 24:
                            for name, value in before(step, 2, it, stages):
                                pe.wait_ge(s[name], value)
                        for h in range(NH):
                            u = (k - 23) * NH + h
                            if u >= 3:
                                pe.wait_ge(s["pexp"], upto("pexp", n, u - 2))
                            mm(ering[u % 3][:, 0:T - t * P], ks[:, b * NKV + h // 2, t * P:(t + 1) * P],
                               qs[:, b * NH + h, t * P:T], stop=False)
                            mm(ering[u % 3][:, 0:P], identb[:, :], maskb[:, P:2 * P],
                               start=False).then_inc(s["pe_st"], 1)
                        if k > 23:
                            pv(n, k - 24)
                    if step == "b31":
                        pv(n, 7)
                    if step in ("a32", "a33"):
                        pe.wait_ge(s["yT"], upto("yT", n, k - 31))
                        four(step, lambda t: yT[:, k - 32, t * P:(t + 1) * P])
                    if step == "a34":
                        pe.wait_ge(s["yn"], full("yn", n))
                        four(step, lambda t: yn[:, t, :, :, :].rearrange("p b h d -> p (b h d)"))
                    if step == "a35":
                        pe.wait_ge(s["ynT"], upto("ynT", n))
                        for t in range(NT):
                            last = mm(misc[:, t * P:(t + 1) * P], ynT[:, t * P:(t + 1) * P], wo[:, :])
                        done(step, last)
                    if step in ("e0", "e1"):
                        pe.wait_ge(s["fl"], upto("fl", n))
                        four(step, lambda t: fl[:, 2 * t + k, :, :].rearrange("p a d -> p (a d)"))
                    if step == "e2":
                        pe.wait_ge(s["xf"], full("xf", n))
                        for g in range(G):
                            last = mm(misc[:, g * NE:(g + 1) * NE], xf[:, g % 2, (g // 2) * P:(g // 2 + 1) * P],
                                      rw[:, :])
                        done(step, last)
                    if step == "e3":
                        pe.wait_ge(s["wp"], full("wp", n))
                        for g in range(G):
                            col = (g % 2) * T + (g // 2) * P
                            last = pe.transpose(misc[:, :].bitcast(bf16)[0:PIECES * NE, col:col + P],
                                                wp[:, g, :, :].rearrange("p a b -> p (a b)"), identb[:, :])
                        done(step, last)
                    if c == "c" and k < 2 * NJ:
                        j, b, u = k // 2, k % 2, k
                        cols = slice(j * P, min(F, (j + 1) * P))
                        w = cols.stop - cols.start
                        if u == 0:
                            pe.wait_ge(s["xahi"], full("xahi", n))
                            pe.wait_ge(s["xblo"], full("xblo", n))
                            pe.wait_ge(s["wT"], upto("wT", n))
                            for bank in (3, 4, 5, 7):
                                for name, value in before(step, bank, it, stages):
                                    pe.wait_ge(s[name], value)
                            up(n, 0)
                        if u:
                            pe.wait_ge(s["hh"], upto("hh", n, u))
                        for p, mov in enumerate((xa, xa, xb)):
                            last = mm(h3bank[0:w, :], w13[:, 1, p, cols], mov[:, b, :], start=p == 0, stop=p == 2)
                        last.then_inc(s["pe_h3"], 1)
                    if c == "d":
                        if k + 1 < 2 * NJ:
                            up(n, k + 1)
                        if k % 2 and k > 1:
                            down(n, k // 2 - 1)
                    if step == "c23":
                        pe.wait_ge(s["moT"], upto("moT", n))
                        four(step, lambda t: moT[:, t * P:(t + 1) * P])
                    if step == "c22":
                        down(n, NJ - 1)

            run(program, pe)

        @block.scalar
        def _(_e):
            act.wait_ge(loaded, 16 * 25)

            def program(it, stages):
                for step in [x for x in READERS if x[0] in stages]:
                    n = it - SKEW[step[0]]
                    misc = banks[BANK[step]] if step in BANK else None
                    c, k = step[0], int(step[1:])
                    if step == "g1":
                        act.wait_ge(s["xc"], upto("xc", n))
                        act.activation(xsq[:, :, :], xc[:, :, :], ACT.Square).then_inc(s["xsq"], 1)
                        act.wait_ge(s["x0"], full("x0", n))
                        act.activation(xm[:, :, :], x0[:, :, :], ACT.Copy).then_inc(s["xm"], 1)
                    if step == "g4":
                        act.wait_ge(s["pe_gate"], upto("pe_gate", n, NTH[step]))
                        act.activation(xT[:, :], misc[:, :], ACT.Copy).then_inc(s["xT"], 1)
                    if step == "g5":
                        if later(n):
                            act.wait_ge(s["hgT"], upto("hgT", n - 1))
                        act.wait_ge(s["pe_gate"], upto("pe_gate", n, NTH[step]))
                        act.activation(qT[:, :], misc[:, :], ACT.Identity, bias=bias[:, 0:1]).then_inc(s["qT"], 1)
                    if c == "g" and 7 <= k <= 9:
                        q = k - 7
                        act.wait_ge(s["pe_gate"], upto("pe_gate", n, NTH[step]))
                        act.activation(mn[:, q, :], misc[:, :], ACT.Identity, scale=(0.1, -1.0, 1.0)[q],
                                       bias=(bi[:, 0:1], bi[:, 1:2], bias[:, 5:6])[q]).then_inc(s["gx"], 1)
                    if step == "g18":
                        act.wait_ge(s["gx"], full("gx", n))
                        act.activation(ab[:, 1:3, :], mn[:, 1:3, :], ACT.Abs).then_inc(s["gabs"], 1)
                    if step == "g10":
                        act.wait_ge(s["gabs"], upto("gabs", n))
                        act.activation(ab[:, 1:3, :], ab[:, 1:3, :], ACT.Exp, scale=-1.0).then_inc(s["gexp"], 1)
                        act.activation(li[:, :], mn[:, 0, :], ACT.Tanh).then_inc(s["si"], 1)
                    if step == "g19":
                        act.wait_ge(s["gexp"], upto("gexp", n))
                        act.activation(ab[:, 1:3, :], ab[:, 1:3, :], ACT.Ln, bias=1.0).then_inc(s["gln"], 1)
                    if step == "g12":
                        act.wait_ge(s["lso"], upto("lso", n))
                        act.activation(ab[:, 2, :], mn[:, 2, :], ACT.Exp).then_inc(s["so"], 1)
                    if step == "g14":
                        act.wait_ge(s["aw"], upto("aw", n))
                        act.activation(wexp[:, :], mn[:, 0, :], ACT.Exp).then_inc(s["wexp"], 1)
                        act.wait_ge(s["ae"], upto("ae", n))
                        act.activation(eexp[:, :], mn[:, 2, :], ACT.Exp).then_inc(s["eexp"], 1)
                    if step == "g17":
                        act.wait_ge(s["xm"], upto("xm", n))
                        if later(n):
                            act.wait_ge(s["h1"], upto("h1", n - 1))
                        act.activation(xr[:, :, :], xm[:, :, :], ACT.Copy).then_inc(s["xres"], 1)
                    if step in ("m0", "m1"):
                        act.wait_ge(s["pe_mem"], upto("pe_mem", n, NTH[step]))
                        act.activation((ktok, utok)[k][:, :, :].rearrange("p a b -> p (a b)"), misc[:, :],
                                       ACT.Copy).then_inc(s[("ktok", "utok")[k]], 1)
                    if step in ("m7", "m8"):
                        lo, hi = ((0, 4), (4, NC - 1))[k - 7]
                        act.wait_ge(s["pe_mem"], upto("pe_mem", n, NTH[step]))
                        act.activation(stT[:, lo:hi, :].rearrange("p a b -> p (a b)"), misc[:, 0:(hi - lo) * P],
                                       ACT.Copy).then_inc(s["stT"], 1)
                    if step == "m10":
                        act.wait_ge(s["pe_mem"], upto("pe_mem", n, NTH[step]))
                        act.activation(ht[:, :, :].rearrange("p a b -> p (a b)"), misc[:, :],
                                       ACT.Copy).then_inc(s["ht"], 1)
                    if step == "m11":
                        act.wait_ge(s["pe_mem"], upto("pe_mem", n, NTH[step]))
                        act.activation(mt[:, 18, :], misc[:, 0:G], ACT.Abs).then_inc(s["dabs"], 1)
                    if step == "m12":
                        act.wait_ge(s["ht"], upto("ht", n))
                        act.activation(hsq[:, :, :], ht[:, :, :], ACT.Square).then_inc(s["hsq"], 1)
                    if step == "m15":
                        act.wait_ge(s["hc"], upto("hc", n))
                        act.activation(hsq[:, :, :], hc[:, :, :], ACT.Square).then_inc(s["hsq2"], 1)
                    if step == "q0":
                        act.wait_ge(s["pe_qk"], upto("pe_qk", n, NTH[step]))
                        act.activation(hnT[:, :], misc[:, :], ACT.Copy, scale=ln1[:, 0:1]).then_inc(s["hnT"], 1)
                    if step in ("b38", "b39"):
                        x, rows, dst = (0, P, qp) if step == "b38" else (1, D, kp)
                        if later(n):
                            act.wait_ge(s["qk_out"], full("qk_out", n - 1))
                        act.wait_ge(s["qr"], upto("qr", n, x + 1))
                        act.activation(dst[0:rows, 0, :], qr[0:rows, x, :], ACT.Copy).then_inc(s["p1"], 1)
                    if step in ("b40", "b41"):
                        x, rows, dst = (0, P, qp) if step == "b40" else (1, D, kp)
                        act.wait_ge(s["r1"], upto("r1", n, x + 1))
                        act.activation(dst[0:rows, 1, :], t1[0:rows, x, :], ACT.Copy).then_inc(s["p2"], 1)
                    if step == "b5":
                        if later(n):
                            act.wait_ge(s["pe_pv"], full("pe_pv", n - 1))
                        act.wait_ge(s["pe_attn"], upto("pe_attn", n, NTH[step]))
                        act.activation(va[:, :, :, 0:HD].rearrange("p t g d -> p (t g) d"),
                                       misc[:, 0:NT * D].rearrange("p (t d) -> p t d", d=HD),
                                       ACT.Copy).then_inc(s["va"], 1)
                    if step == "b22":
                        act.wait_ge(s["pe_attn"], upto("pe_attn", n, NTH[step]))
                        act.activation(mrow[:, :], misc[:, :].bitcast(bf16)[0:PIECES * 2 * NH, 0:T], ACT.Copy).then_inc(s["mrow"], 1)
                    if c == "b" and 23 <= k <= 30:
                        q = k - 23
                        b, t = q // NT, q % NT
                        if q == NT + 1:
                            act.wait_ge(s["pe_pv"], upto("pe_pv", n, NT))
                            act.activation(yT[:, 0, :], ybank[:, :], ACT.Copy).then_inc(s["yT"], 1)
                        if q >= 2:
                            act.wait_ge(s["pe_pv"], upto("pe_pv", n, q - 1))
                        for h in range(NH):
                            act.wait_ge(s["pe_st"], upto("pe_st", n, q * NH + h + 1))
                            act.activation(pr[:, q % 2, h, 0:T - t * P], ering[(q * NH + h) % 3][:, 0:T - t * P],
                                           ACT.Exp).then_inc(s["pexp"], 1)
                    if step == "b31":
                        act.wait_ge(s["pe_pv"], upto("pe_pv", n, 8))
                        act.activation(yT[:, 1, :], ybank[:, :], ACT.Copy).then_inc(s["yT"], 1)
                    if step == "a34":
                        act.wait_ge(s["pe_tail"], upto("pe_tail", n, NTH[step]))
                        act.activation(ynT[:, :], misc[:, :], ACT.Copy).then_inc(s["ynT"], 1)
                    if step == "a36":
                        act.wait_ge(s["x2"], upto("x2", n))
                        act.activation(x2sq[:, :, :], x2[:, :, :], ACT.Square).then_inc(s["x2sq"], 1)
                    if step in ("e0", "e1"):
                        act.wait_ge(s["pe_prep"], upto("pe_prep", n, NTH[step]))
                        act.activation(xf[:, k, :], misc[:, :], ACT.Copy, scale=ln2[:, 0:1]).then_inc(s["xf"], 1)
                    if step in ("e5", "e6"):
                        k = k - 5
                        act.wait_ge(s["cres"], upto("cres", n, k + 1))
                        act.activation(x2p[:, :], xres[:, :], ACT.Copy).then_inc(s["cast2"], 1)
                    if step == "e7":
                        act.wait_ge(s["r_dve"], upto("r_dve", n, 2))
                        act.activation(lg[:, 2, :, :], lg[:, 1, :, :], ACT.Exp).then_inc(s["r_act"], 1)
                    if step == "e3":
                        act.wait_ge(s["pe_prep"], upto("pe_prep", n, NTH[step]))
                        act.activation(wT[0:PIECES * NE, :, :].rearrange("p b t -> p (b t)"),
                                       misc[:, :].bitcast(bf16)[0:PIECES * NE, :], ACT.Copy).then_inc(s["wT"], 1)
                    if step == "c0" or (c == "d" and k < 2 * NJ - 1):
                        for u in ((0,) if c == "c" else (k + 1,)):
                            w = min(P, F - (u // 2) * P)
                            if u >= 2:
                                act.wait_ge(s["hh"], upto("hh", n, u - 1))
                            act.wait_ge(s["pe_h1"], upto("pe_h1", n, u + 1))
                            act.activation(sl[0:w, u % 2, :], h1bank[0:w, :], ACT.Silu).then_inc(s["silu"], 1)
                    if step == "c22":
                        act.wait_ge(s["pe_down"], upto("pe_down", n, NJ))
                        act.activation(moT[:, :], obank[:, :], ACT.Copy).then_inc(s["moT"], 1)

            run(program, act)

        @block.vector
        def _(_e):
            tt, ts, stt = dve.tensor_tensor, dve.tensor_scalar, dve.scalar_tensor_tensor
            dve.wait_ge(loaded, 16 * 25)
            casts = 0

            def link(ins):
                nonlocal casts
                casts += 1
                ins.then_inc(cast, 1)
                dve.wait_ge(cast, casts)

            for m in range(2):
                link(dve.tensor_copy(out=w13[:, m, 0, :], in_=wtmp[:, m, :]))
                link(tt(out=wtmp[:, m, :], in0=wtmp[:, m, :], in1=w13[:, m, 0, :], op=ALU.subtract))
                link(dve.tensor_copy(out=w13[:, m, 1, :], in_=wtmp[:, m, :]))
                link(dve.tensor_copy(out=w13[0:D, m, 2, :], in_=w13[0:D, m, 0, :]))
                link(tt(out=w13[D:P, m, 2, :], in0=wtmp[D:P, m, :], in1=w13[D:P, m, 1, :], op=ALU.subtract))
            link(dve.tensor_copy(out=selg[:, :], in_=selgf))
            link(dve.tensor_copy(out=identb[:, :], in_=ident[:, :]))
            link(dve.tensor_copy(out=maskb[:, :], in_=maskf))
            link(tt(out=bi[:, 0:1], in0=bias[:, 3:4], in1=ibias[:, :], op=ALU.add))
            link(ts(out=bi[:, 0:1], in0=bi[:, 0:1], scalar1=0.1, scalar2=None, op0=ALU.mult))
            link(ts(out=bi[:, 1:2], in0=bias[:, 4:5], scalar1=-1.0, scalar2=None, op0=ALU.mult))
            for lo in range(0, NP * G, NP * G):
                fx, fn = mn[:, 0, 0:NP * G], mn[:, 2, 0:NP * G]
                link(dve.tensor_copy(out=fx, in_=idx[:, :]))
                link(ts(out=fn, in0=fx, scalar1=0.0, scalar2=float(VOCAB), op0=ALU.is_lt, op1=ALU.mult))
                link(tt(out=fx, in0=fx, in1=fn, op=ALU.add))
                link(ts(out=fx, in0=fx, scalar1=0.0, scalar2=float(VOCAB - 1), op0=ALU.max, op1=ALU.min))
                link(ts(out=fx, in0=fx, scalar1=float(HIDDEN // D), scalar2=float(LAYER), op0=ALU.mult, op1=ALU.add))
                link(dve.tensor_copy(out=idx[:, :], in_=fx))
            assert casts == CASTS, casts
            dve.wait_ge(cleared, 9)

            def program(it, stages):
                for step in [x for x in READERS if x[0] in stages]:
                    n = it - SKEW[step[0]]
                    misc = banks[BANK[step]] if step in BANK else None
                    c, k = step[0], int(step[1:])
                    if step == "g1":
                        dve.wait_ge(s["x0"], full("x0", n))
                        dve.tensor_reduce(out=st[:, 6, :], in_=x0[:, :, :], axis=AX, op=ALU.add).then_inc(s["g_sum"], 1)
                        dve.wait_ge(s["g_sum"], upto("g_sum", n))
                        ts(out=st[:, 7, :], in0=st[:, 6, :], scalar1=-1.0 / D, scalar2=None,
                           op0=ALU.mult).then_inc(s["g_nm"], 1)
                        dve.wait_ge(s["g_nm"], upto("g_nm", n))
                        tt(out=xc[:, :, :], in0=x0[:, :, :], in1=bc(st[:, 7, :], D), op=ALU.add).then_inc(s["xc"], 1)
                    if step == "g2":
                        dve.wait_ge(s["xsq"], upto("xsq", n))
                        dve.tensor_reduce(out=st[:, 6, :], in_=xsq[:, :, :], axis=AX,
                                          op=ALU.add).then_inc(s["g_var"], 1)
                        dve.wait_ge(s["g_var"], upto("g_var", n))
                        ts(out=g_tiny[0], in0=st[:, 6, :], scalar1=1.0 / D, scalar2=1e-5, op0=ALU.mult,
                           op1=ALU.add).then_inc(s["g_v"], 1)
                        dve.wait_ge(s["g_v"], upto("g_v", n))
                        rsqrt_guess("g", n, g_tiny)
                    if step == "g6":
                        dve.wait_ge(s["pe_gate"], upto("pe_gate", n, NTH[step]))
                        if later(n):
                            dve.wait_ge(s["hgT"], upto("hgT", n - 1))
                        ts(out=kT[:, :], in0=misc[:, :], scalar1=bias[:, 1:2], scalar2=D ** -0.5, op0=ALU.add,
                           op1=ALU.mult).then_inc(s["kT"], 1)
                    if step == "g11":
                        dve.wait_ge(s["gln"], upto("gln", n))
                        for q, name in ((1, "lf"), (2, "lso")):
                            stt(out=mn[:, q, :], in0=mn[:, q, :], scalar=0.0, in1=ab[:, q, :], op0=ALU.min,
                                op1=ALU.subtract).then_inc(s[name], 1)
                    if step == "g13":
                        dve.wait_ge(s["si"], upto("si", n))
                        ts(out=li[:, :], in0=li[:, :], scalar1=10.0, scalar2=None,
                           op0=ALU.mult).then_inc(s["li"], 1)
                        dve.wait_ge(s["li"], upto("li", n))
                        dve.wait_ge(s["lf"], upto("lf", n))
                        lf = mn[:, 1, :]
                        dve.tensor_tensor_scan(out=mext[:, 1:T + 1], data0=lf, data1=li[:, :], initial=0.0, op0=ALU.add,
                                               op1=ALU.max).then_inc(s["mscan"], 1)
                        dve.wait_ge(s["mscan"], upto("mscan", n))
                        starts = lf.rearrange("p (c l) -> p c l", l=L)[:, :, 0]
                        tt(out=starts, in0=starts, in1=mext[:, 0:T].rearrange("p (c l) -> p c l", l=L)[:, :, 0],
                           op=ALU.add).then_inc(s["lfc"], 1)
                        dve.wait_ge(s["lfc"], upto("lfc", n))
                        dve.tensor_tensor_scan(out=gcum[:, :], data0=restart[:, :], data1=lf, initial=0.0,
                                               op0=ALU.mult, op1=ALU.add).then_inc(s["gcum"], 1)
                        dve.wait_ge(s["gcum"], upto("gcum", n))
                        dve.wait_ge(s["so"], upto("so", n))
                        tt(out=mn[:, 0, :], in0=gcum[:, :], in1=mext[:, 1:T + 1], op=ALU.subtract).then_inc(s["aw"], 1)
                        tt(out=mn[:, 2, :], in0=li[:, :], in1=gcum[:, :], op=ALU.subtract).then_inc(s["ae"], 1)
                    if step == "g15":
                        dve.wait_ge(s["pe_gate"], upto("pe_gate", n, NTH[step]))
                        dve.wait_ge(s["eexp"], upto("eexp", n))
                        stt(out=uT[:, :], in0=misc[:, :], scalar=bias[:, 2:3], in1=eexp[:, :], op0=ALU.add,
                            op1=ALU.mult).then_inc(s["uT"], 1)
                        dve.wait_ge(s["wexp"], upto("wexp", n))
                        wd = wdec[:, :].rearrange("p (c l) -> p c l", l=L)[:, 1:NC, 0]
                        dve.tensor_copy(out=wd, in_=wend[:, 0:NC - 1]).then_inc(s["wdec"], 1)
                    if step == "g16":
                        dve.wait_ge(s["wdec"], upto("wdec", n))
                        dve.wait_ge(s["ek"], upto("ek", n))
                        dve.tensor_tensor_scan(out=nst[:, :], data0=wdec[:, :], data1=ek[:, :], initial=0.0,
                                               op0=ALU.mult, op1=ALU.add).then_inc(s["nst"], 1)
                    if step in ("m2", "m3"):
                        b = k - 2
                        dve.wait_ge(s["pe_mem"], upto("pe_mem", n, NTH[step]))
                        tt(out=atm[:, b, :].rearrange("p (t q) -> p t q", q=P),
                           in0=misc[:, :].rearrange("p (t q) -> p t q", q=P),
                           in1=chunkmask[:, :].unsqueeze(1).to_broadcast([P, NT, P]), op=ALU.mult).then_inc(s["atm"], 1)
                    if step in ("m4", "m5"):
                        par = k - 4
                        q = NT - par
                        dve.wait_ge(s["pe_mem"], upto("pe_mem", n, NTH[step]))
                        tt(out=dlt[:, :, :].rearrange("p (q a) d -> p q a d", a=2)[:, 0:q, par, :],
                           in0=misc[:, 0:q * P].rearrange("p (q d) -> p q d", d=P),
                           in1=batchmask[:, :].unsqueeze(1).to_broadcast([P, q, P]), op=ALU.mult).then_inc(s["dlt"], 1)
                    if step == "m6":
                        dve.wait_ge(s["dltw"], upto("dltw", n))
                        for j in range(1, NC - 1):
                            if j > 1:
                                dve.wait_ge(s["state"], upto("state", n, j - 1))
                            stt(out=dlt[:, j, :], in0=dlt[:, j - 1, :], scalar=wend[:, j:j + 1], in1=dlt[:, j, :],
                                op0=ALU.mult, op1=ALU.add).then_inc(s["state"], 1)
                    if step == "m9":
                        dve.wait_ge(s["pe_mem"], upto("pe_mem", n, NTH[step]))
                        dve.wait_ge(s["hw"], upto("hw", n))
                        tt(out=hgT[:, :], in0=misc[:, :], in1=hw[:, :], op=ALU.mult).then_inc(s["hgT"], 1)
                    if step == "m12":
                        dve.wait_ge(s["dabs"], upto("dabs", n))
                        ts(out=mt[:, 18, :], in0=mt[:, 18, :], scalar1=1e-6, scalar2=None,
                           op0=ALU.max).then_inc(s["den"], 1)
                        dve.wait_ge(s["den"], upto("den", n))
                        dve.reciprocal(out=mt[:, 19, :], in_=mt[:, 18, :]).then_inc(s["rd"], 1)
                        dve.wait_ge(s["rd"], upto("rd", n))
                        tt(out=mt[:, 20, :], in0=mt[:, 19, :], in1=mt[:, 19, :], op=ALU.mult).then_inc(s["rd2"], 1)
                    if step == "m13":
                        dve.wait_ge(s["rd2"], upto("rd2", n))
                        dve.wait_ge(s["hsq"], upto("hsq", n))
                        dve.tensor_reduce(out=mt[:, 21, :], in_=hsq[:, :, :], axis=AX, op=ALU.add).then_inc(s["hsum"], 1)
                        dve.wait_ge(s["hsum"], upto("hsum", n))
                        stt(out=mt[:, 22, :], in0=mt[:, 21, :], scalar=1.0 / D, in1=mt[:, 20, :], op0=ALU.mult,
                            op1=ALU.mult).then_inc(s["hms"], 1)
                        dve.wait_ge(s["hms"], upto("hms", n))
                        ts(out=mh_tiny[0], in0=mt[:, 22, :], scalar1=1e-8, scalar2=None,
                           op0=ALU.add).then_inc(s["mh_v"], 1)
                        dve.wait_ge(s["mh_v"], upto("mh_v", n))
                        rsqrt_guess("mh", n, mh_tiny)
                    if step == "m14":
                        dve.wait_ge(s["mh_newton"], full("mh_newton", n))
                        tt(out=mt[:, 23, :], in0=mt[:, 19, :], in1=mh_tiny[4], op=ALU.mult).then_inc(s["hf"], 1)
                    if step == "m15":
                        dve.wait_ge(s["h1"], upto("h1", n))
                        dve.tensor_reduce(out=mt[:, 18, :], in_=h1[:, :, :], axis=AX, op=ALU.add).then_inc(s["m_sum"], 1)
                        dve.wait_ge(s["m_sum"], upto("m_sum", n))
                        ts(out=mt[:, 20, :], in0=mt[:, 18, :], scalar1=-1.0 / D, scalar2=None,
                           op0=ALU.mult).then_inc(s["m_nm"], 1)
                        dve.wait_ge(s["m_nm"], upto("m_nm", n))
                        tt(out=hc[:, :, :], in0=h1[:, :, :], in1=bc(mt[:, 20, :], D), op=ALU.add).then_inc(s["hc"], 1)
                    if step == "m16":
                        dve.wait_ge(s["hsq2"], upto("hsq2", n))
                        dve.tensor_reduce(out=mt[:, 21, :], in_=hsq[:, :, :], axis=AX, op=ALU.add).then_inc(s["m_var"], 1)
                        dve.wait_ge(s["m_var"], upto("m_var", n))
                        ts(out=ml_tiny[0][:, 0:G], in0=mt[:, 21, :], scalar1=1.0 / D, scalar2=1e-5, op0=ALU.mult,
                           op1=ALU.add).then_inc(s["ml_v"], 1)
                        ts(out=ml_tiny[0][:, G:2 * G], in0=mt[:, 21, :], scalar1=(1.0 + 1e-6) / D, scalar2=1e-11,
                           op0=ALU.mult, op1=ALU.add).then_inc(s["mr_v"], 1)
                        dve.wait_ge(s["ml_v"], upto("ml_v", n))
                        dve.wait_ge(s["mr_v"], upto("mr_v", n))
                        rsqrt_guess("ml", n, ml_tiny)
                    if step == "m17":
                        dve.wait_ge(s["ml_newton"], full("ml_newton", n))
                        if later(n):
                            dve.wait_ge(s["hnT"], upto("hnT", n - 1))
                        tt(out=hn[:, :, :], in0=hc[:, :, :], in1=bc(ml_tiny[4][:, G:2 * G], D),
                           op=ALU.mult).then_inc(s["hn"], 1)
                    if c == "q" and 1 <= k <= 4:
                        x, rows, tab = (0, P, ropeq) if k < 3 else (1, D, ropek)
                        dst = t1 if k % 2 else t2
                        dve.wait_ge(s["pe_qk"], upto("pe_qk", n, NTH[step]))
                        if k in (1, 3):
                            if later(n):
                                dve.wait_ge(s["p2"], full("p2", n - 1))
                            if later(n):
                                dve.wait_ge(s["p3"], full("p3", n - 1))
                        tt(out=dst[0:rows, x, :], in0=misc[0:rows, :], in1=tab[:, (k - 1) % 2, :],
                           op=ALU.mult).then_inc(s["t1" if k % 2 else "t2"], 1)
                    if c == "b" and 6 <= k <= 21:
                        b, t = (k - 6) // 2 // NT, (k - 6) // 2 % NT
                        for u in range((k - 6) * 2, (k - 6) * 2 + 2):
                            h = u % NH
                            dve.wait_ge(s["pe_s"], upto("pe_s", n, u + 1))
                            dve.tensor_reduce(out=nm[:, t, b * NH + h:b * NH + h + 1], in_=sring[u % 2][:, 0:(t + 1) * P],
                                              axis=AX, op=ALU.max, negate=True).then_inc(s["smax"], 1)
                    if step == "b43":
                        dve.wait_ge(s["smax"], full("smax", n))
                        if later(n):
                            dve.wait_ge(s["mrow"], upto("mrow", n - 1))
                        dve.tensor_copy(out=mp[:, :, 0, :], in_=nm[:, :, :]).then_inc(s["mp"], 1)
                        dve.wait_ge(s["mp"], upto("mp", n, 1))
                        tt(out=nmr[:, :, :], in0=nm[:, :, :], in1=mp[:, :, 0, :], op=ALU.subtract).then_inc(s["mp"], 1)
                        dve.wait_ge(s["mp"], upto("mp", n, 2))
                        dve.tensor_copy(out=mp[:, :, 1, :], in_=nmr[:, :, :]).then_inc(s["mp"], 1)
                        dve.wait_ge(s["mp"], upto("mp", n, 3))
                        tt(out=mp[:, :, 2, :], in0=nmr[:, :, :], in1=mp[:, :, 1, :],
                           op=ALU.subtract).then_inc(s["mp"], 2)
                    if step in ("a32", "a33"):
                        b = k - 32
                        dve.wait_ge(s["pe_tail"], upto("pe_tail", n, NTH[step]))
                        if later(n):
                            dve.wait_ge(s["ynT"], upto("ynT", n - 1))
                        y = misc[:, :].rearrange("p (g d) -> p g d", d=32)
                        dve.reciprocal(out=rden[:, b, :], in_=y[:, :, HD]).then_inc(s["rden"], 1)
                        dve.wait_ge(s["rden"], upto("rden", n, b + 1))
                        for t in range(NT):
                            r = slice(t * NH, (t + 1) * NH)
                            last = tt(out=yn[:, t, b, :, :], in0=y[:, r, 0:HD], in1=bc(rden[:, b, r], HD), op=ALU.mult)
                        last.then_inc(s["yn"], 1)
                    if step == "a35":
                        dve.wait_ge(s["pe_tail"], upto("pe_tail", n, NTH[step]))
                        y = misc[:, :].rearrange("p (g d) -> p g d", d=D)
                        dve.wait_ge(s["y0b"], upto("y0b", n))
                        tt(out=x2[:, :, :], in0=y, in1=y0b[:, :, :], op=ALU.add).then_inc(s["x2"], 1)
                        dve.wait_ge(s["hy"], upto("hy", n))
                        if later(n):
                            dve.wait_ge(s["hxc"], upto("hxc", n - 1))
                        tt(out=hx[:, :, :], in0=y, in1=hy[:, :, :], op=ALU.add).then_inc(s["hx"], 1)
                    if step == "a37":
                        dve.wait_ge(s["x2sq"], upto("x2sq", n))
                        dve.tensor_reduce(out=bt[:, 5, :], in_=x2sq[:, :, :], axis=AX,
                                          op=ALU.add).then_inc(s["b_var"], 1)
                        dve.wait_ge(s["b_var"], upto("b_var", n))
                        ts(out=b_tiny[0], in0=bt[:, 5, :], scalar1=1.0 / D, scalar2=1e-6, op0=ALU.mult,
                           op1=ALU.add).then_inc(s["b_v"], 1)
                        dve.wait_ge(s["b_v"], upto("b_v", n))
                        rsqrt_guess("b", n, b_tiny)
                    if step == "e4":
                        dve.wait_ge(s["hx"], upto("hx", n))
                        if later(n):
                            dve.wait_ge(s["out"], full("out", n - 1))
                        dve.tensor_copy(out=ot[:, :, :], in_=hx[:, :, :]).then_inc(s["hxc"], 1)
                    if step in ("e9", "e10"):
                        k = k - 9
                        dve.wait_ge(s["xf"], upto("xf", n, k + 1))
                        if k == 0 and later(n):
                            dve.wait_ge(s["pe_h3"], full("pe_h3", n - 1))
                        dve.tensor_copy(out=xa[0:D, k, :], in_=xf[0:D, k, :]).then_inc(s["cast1"], 1)
                        dve.tensor_copy(out=xb[D:P, k, :], in_=xf[D:P, k, :]).then_inc(s["cast1"], 1)
                        dve.wait_ge(s["cast1"], upto("cast1", n, 2 * k + 2))
                        tt(out=xa[D:P, k, :], in0=xf[D:P, k, :], in1=xb[D:P, k, :],
                           op=ALU.subtract).then_inc(s["xahi"], 1)
                    if step == "e2":
                        dve.wait_ge(s["pe_prep"], upto("pe_prep", n, NTH[step]))
                        dve.tensor_copy(out=lg[:, 0, :, :].rearrange("p g e -> p (g e)"),
                                        in_=misc[:, 0:G * NE]).then_inc(s["lg"], 1)
                        dve.wait_ge(s["lg"], upto("lg", n))
                    if step in ("e2", "e8", "e11", "e12"):
                        done = {"e2": 0, "e8": 2, "e11": 11, "e12": 17}[step]

                        def link(ins):
                            nonlocal done
                            done += 1
                            ins.then_inc(s["r_dve"], 1)
                            dve.wait_ge(s["r_dve"], upto("r_dve", n, done))

                        def most(q, src):
                            link(dve.tensor_reduce(out=r[q], in_=src, axis=AX, op=ALU.max))

                        x, r = [lg[:, q, :, :] for q in range(15)], [ls[:, q, :] for q in range(12)]
                        order = rev[:, :].unsqueeze(1).to_broadcast([P, G, NE])
                    if step == "e2":
                        most(0, x[0])
                        link(tt(out=x[1], in0=x[0], in1=bc(r[0], NE), op=ALU.subtract))
                    if step == "e8":
                        dve.wait_ge(s["r_act"], upto("r_act", n))
                        link(dve.tensor_reduce(out=r[1], in_=x[2], axis=AX, op=ALU.add))
                        link(dve.reciprocal(out=r[2], in_=r[1]))
                        link(tt(out=x[3], in0=x[2], in1=bc(r[2], NE), op=ALU.mult))
                        most(3, x[3])
                        link(tt(out=x[4], in0=x[3], in1=bc(r[3], NE), op=ALU.is_equal))
                        link(tt(out=x[5], in0=x[4], in1=order, op=ALU.mult))
                        most(4, x[5])
                        link(tt(out=x[6], in0=x[5], in1=bc(r[4], NE), op=ALU.is_equal))
                        link(stt(out=x[7], in0=x[6], scalar=-2.0, in1=x[3], op0=ALU.mult, op1=ALU.add))
                    if step == "e11":
                        most(5, x[7])
                        link(tt(out=x[8], in0=x[7], in1=bc(r[5], NE), op=ALU.is_equal))
                        link(tt(out=x[9], in0=x[8], in1=order, op=ALU.mult))
                        most(6, x[9])
                        link(tt(out=x[10], in0=x[9], in1=bc(r[6], NE), op=ALU.is_equal))
                        link(tt(out=x[11], in0=x[6], in1=x[10], op=ALU.add))
                    if step == "e12":
                        link(tt(out=x[12], in0=x[11], in1=x[3], op=ALU.mult))
                        link(stt(out=r[7], in0=r[3], scalar=1e-9, in1=r[5], op0=ALU.add, op1=ALU.add))
                        link(dve.reciprocal(out=r[8], in_=r[7]))
                        link(tt(out=x[13], in0=x[12], in1=bc(r[8], NE), op=ALU.mult))
                        assert done == PER["r_dve"], done
                        if later(n):
                            dve.wait_ge(s["wT"], upto("wT", n - 1))
                        dve.tensor_copy(out=wp[:, :, 0, :], in_=x[13]).then_inc(s["wp"], 1)
                        dve.wait_ge(s["wp"], upto("wp", n, 1))
                        tt(out=x[14], in0=x[13], in1=wp[:, :, 0, :], op=ALU.subtract).then_inc(s["wp"], 1)
                        dve.wait_ge(s["wp"], upto("wp", n, 2))
                        dve.tensor_copy(out=wp[:, :, 1, :], in_=x[14]).then_inc(s["wp"], 1)
                        dve.wait_ge(s["wp"], upto("wp", n, 3))
                        tt(out=wp[:, :, 2, :], in0=x[14], in1=wp[:, :, 1, :], op=ALU.subtract).then_inc(s["wp"], 2)
                    if c == "c" and k < 2 * NJ:
                        j, b, u = k // 2, k % 2, k
                        w = min(P, F - j * P)
                        dve.wait_ge(s["silu"], upto("silu", n, u + 1))
                        dve.wait_ge(s["pe_g"], upto("pe_g", n, u + 1))
                        tt(out=sgt[0:w, b, :], in0=gbank[0:w, :], in1=sl[0:w, b, :], op=ALU.mult).then_inc(s["gated"], 1)
                        dve.wait_ge(s["gated"], upto("gated", n, u + 1))
                        dve.wait_ge(s["pe_h3"], upto("pe_h3", n, u + 1))
                        if j >= 2:
                            dve.wait_ge(s["pe_down"], upto("pe_down", n, j - 1))
                        tt(out=hh[0:w, j % 2, b, :], in0=h3bank[0:w, :], in1=sgt[0:w, b, :],
                           op=ALU.mult).then_inc(s["hh"], 1)
                    if step == "c23":
                        dve.wait_ge(s["pe_moe"], upto("pe_moe", n, NTH[step]))
                        dve.wait_ge(s["hxc"], upto("hxc", n))
                        tt(out=ot[:, :, :].rearrange("p g d -> p (g d)"), in0=misc[:, :],
                           in1=ot[:, :, :].rearrange("p g d -> p (g d)"), op=ALU.add).then_inc(s["ot"], 1)

            run(program, dve)

        @block.gpsimd
        def _(_e):
            tt = pool.tensor_tensor
            presets = 0
            for ap, v in ((qs[96:P, :, :], 0.0), (ks[96:P, :, :], 0.0), (va[:, :, :, :], 0.0), (wT[:, :, :], 0.0),
                          (wdec[:, :], 1.0), (mext[:, 0:1], 0.0), (half3[:, :], 1.5),
                          (ks[96:96 + PIECES, :, :], 1.0), (va[:, :, :, HD:HD + 1], 1.0)):
                presets += 1
                pool.memset(ap, v).then_inc(cleared, 1)
                pool.wait_ge(cleared, presets)
            pool.wait_ge(cast, CASTS)

            def program(it, stages):
                for step in [x for x in READERS if x[0] in stages]:
                    n = it - SKEW[step[0]]
                    misc = banks[BANK[step]] if step in BANK else None
                    if step == "f0":
                        if later(n):
                            pool.wait_ge(s["x0"], full("x0", n - 1))
                        pool.tensor_copy(out=idxc[:, :], in_=idx[:, bass.ds(n * G, G)]).then_inc(s["idxc"], 1)
                        pool.wait_ge(s["idxc"], upto("idxc", n))
                        if later(n):
                            pool.wait_ge(s["xm"], upto("xm", n - 1))
                        if later(n):
                            pool.wait_ge(s["xc"], upto("xc", n - 1))
                        tt(out=pad[:, 0:1], in0=nscale[:, 0:1], in1=nscale[:, 0:1], op=ALU.mult)
                        for g in range(G):
                            pool.indirect_dma_start(
                                out=x0[:, g, :], out_offset=None, in_=a["table"],
                                in_offset=bass.IndirectOffsetOnAxis(ap=idxc[:, g:g + 1], axis=0)).then_inc(s["x0"], 16)
                    if step == "g2":
                        newton("g", n, g_tiny)
                    if step == "g15":
                        pool.wait_ge(s["eexp"], upto("eexp", n))
                        pool.wait_ge(s["kT"], upto("kT", n))
                        tt(out=ek[:, :], in0=eexp[:, :], in1=kT[:, :], op=ALU.mult).then_inc(s["ek"], 1)
                        pool.wait_ge(s["qT"], upto("qT", n))
                        tt(out=wqx[:, :], in0=wexp[:, :], in1=qT[:, :], op=ALU.mult).then_inc(s["wqx"], 1)
                        pool.wait_ge(s["so"], upto("so", n))
                        tt(out=hw[:, :], in0=wexp[:, :], in1=ab[:, 2, :], op=ALU.mult).then_inc(s["hw"], 1)
                    if step == "g16":
                        pool.wait_ge(s["wqx"], upto("wqx", n))
                        pool.wait_ge(s["nst"], upto("nst", n))
                        tt(out=prod[:, :], in0=nst[:, :], in1=wqx[:, :], op=ALU.mult).then_inc(s["prod"], 1)
                    if step == "g3":
                        pool.wait_ge(s["g_newton"], full("g_newton", n))
                        pool.wait_ge(s["xsq"], upto("xsq", n))
                        tt(out=xn[:, :, :], in0=xc[:, :, :], in1=bc(g_tiny[4], D), op=ALU.mult).then_inc(s["xn"], 1)
                    if step == "m5":
                        pool.wait_ge(s["dlt"], full("dlt", n))
                        tt(out=dlt[:, 0:NC - 1, :], in0=dlt[:, 0:NC - 1, :], in1=bc(wend[:, 0:NC - 1], P),
                           op=ALU.mult).then_inc(s["dltw"], 1)
                    if step == "m13":
                        newton("mh", n, mh_tiny)
                    if step == "m16":
                        newton("ml", n, ml_tiny)
                    if step == "a38":
                        pool.wait_ge(s["b_newton"], full("b_newton", n))
                        pool.wait_ge(s["x2"], upto("x2", n))
                        if later(n):
                            pool.wait_ge(s["xf"], full("xf", n - 1))
                        for q in range(2):
                            last = tt(out=fl[:, :, q, :], in0=x2[:, :, :], in1=bc(b_tiny[4], D), op=ALU.mult)
                        last.then_inc(s["fl"], 1)
                    if step == "a37":
                        newton("b", n, b_tiny)
                    if step == "m14":
                        pool.wait_ge(s["hf"], upto("hf", n))
                        pool.wait_ge(s["hsq"], upto("hsq", n))
                        tt(out=ho[:, :, :], in0=ht[:, :, :], in1=bc(mt[:, 23, :], D), op=ALU.mult).then_inc(s["ho"], 1)
                        pool.wait_ge(s["ho"], upto("ho", n))
                        tt(out=ho[:, :, :], in0=ho[:, :, :], in1=nscale[:, :].unsqueeze(1).to_broadcast([P, G, D]),
                           op=ALU.mult).then_inc(s["hos"], 1)
                        pool.wait_ge(s["hos"], upto("hos", n))
                        if later(n):
                            pool.wait_ge(s["hy"], upto("hy", n - 1))
                        tt(out=h1[:, :, :], in0=ho[:, :, :], in1=xr[:, :, :], op=ALU.add).then_inc(s["h1"], 1)
                    if step == "m17":
                        if later(n):
                            pool.wait_ge(s["y0b"], upto("y0b", n - 1))
                        pool.wait_ge(s["hc"], upto("hc", n))
                        pool.wait_ge(s["ml_newton"], full("ml_newton", n))
                        tt(out=y0[:, :, :], in0=hc[:, :, :], in1=bc(ml_tiny[4][:, 0:G], D), op=ALU.mult).then_inc(s["y0"], 1)
                    if step == "b42":
                        pool.wait_ge(s["y0"], upto("y0", n))
                        if later(n):
                            pool.wait_ge(s["hx"], upto("hx", n - 1))
                        tt(out=hy[:, :, :], in0=h1[:, :, :], in1=y0[:, :, :], op=ALU.add).then_inc(s["hy"], 1)
                        pool.tensor_copy(out=y0b[:, :, :], in_=y0[:, :, :]).then_inc(s["y0b"], 1)
                    if step in ("q2", "q4"):
                        x, rows = (0, P) if step == "q2" else (1, D)
                        pool.wait_ge(s["t2"], upto("t2", n, x + 1))
                        tt(out=qr[0:rows, x, :], in0=t1[0:rows, x, :], in1=t2[0:rows, x, :],
                           op=ALU.add).then_inc(s["qr"], 1)
                    if step in ("b38", "b39"):
                        x, rows, dst = (0, P, qp) if step == "b38" else (1, D, kp)
                        pool.wait_ge(s["p1"], upto("p1", n, x + 1))
                        tt(out=t1[0:rows, x, :], in0=qr[0:rows, x, :], in1=dst[0:rows, 0, :],
                           op=ALU.subtract).then_inc(s["r1"], 1)
                    if step in ("b40", "b41"):
                        x, rows, dst = (0, P, qp) if step == "b40" else (1, D, kp)
                        pool.wait_ge(s["p2"], upto("p2", n, x + 1))
                        tt(out=dst[0:rows, 2, :], in0=t1[0:rows, x, :], in1=dst[0:rows, 1, :],
                           op=ALU.subtract).then_inc(s["p3"], 1)
                    if step == "e9":
                        if later(n):
                            pool.wait_ge(s["xblo"], full("xblo", n - 1))
                        pool.wait_ge(s["cast1"], upto("cast1", n, 1))
                        tt(out=xres[:, :], in0=xf[0:D, 0, :], in1=xa[0:D, 0, :], op=ALU.subtract).then_inc(s["cres"], 1)
                    if step in ("e5", "e6"):
                        k = int(step[1:]) - 5
                        pool.wait_ge(s["cast2"], upto("cast2", n, k + 1))
                        tt(out=xb[0:D, k, :], in0=xres[:, :], in1=x2p[:, :], op=ALU.subtract).then_inc(s["xblo"], 1)
                        if k == 0:
                            pool.wait_ge(s["xblo"], upto("xblo", n, 1))
                            pool.wait_ge(s["cast1"], upto("cast1", n, 3))
                            tt(out=xres[:, :], in0=xf[0:D, 1, :], in1=xa[0:D, 1, :],
                               op=ALU.subtract).then_inc(s["cres"], 1)

            run(program, pool)
    return nc


def _host(x):
    def bd(w):
        z = np.zeros((2 * w.shape[0], 2 * w.shape[1]), np.float32)
        z[:w.shape[0], :w.shape[1]] = w
        z[w.shape[0]:, w.shape[1]:] = w
        return z

    def twice(v):
        return np.ascontiguousarray(np.tile(np.reshape(v, (-1, 1)), (2, 1)))

    h = {}
    r = np.arange(P)
    h["ident"] = np.eye(P, dtype=np.float32)
    up = np.where(r[None, :] > r[:, None], np.float32(NEG), np.float32(0))
    h["maskf"] = np.concatenate([up, up.T], 1)
    h["chunkmask"] = ((r[:, None] <= r[None, :]) & (r[:, None] // L == r[None, :] // L)).astype(np.float32)
    h["batchmask"] = (r[:, None] // D == r[None, :] // D).astype(np.float32)
    h["restart"] = np.tile((np.arange(T) % L != 0).astype(np.float32), (P, 1))
    h["onesbd"] = (r[:, None] // D == np.arange(2)[None, :]).astype(np.float32)
    h["rev"] = np.tile(NE - np.arange(NE, dtype=np.float32), (P, 1))
    Wg, bg = x["L0_attn_Wg"], x["L0_attn_bg"]
    ws = [x["L0_attn_Wq"], x["L0_attn_Wk"], x["L0_attn_Wv"], Wg[:, :D], Wg[:, D:2 * D], Wg[:, 2 * D:]]
    bs = [x["L0_attn_bq"], x["L0_attn_bk"], x["L0_attn_bv"], bg[:D], bg[D:2 * D], bg[2 * D:]]
    h["proj"] = np.stack([bd(w) for w in ws], 1)
    h["bias"] = np.concatenate([twice(b) for b in bs], 1)
    h["ibias"] = twice(x["L0_attn_input_bias"])
    h["nscale"] = np.tile(x["L0_attn_norm_scale"], (P, 1))
    h["ln1"], h["ln2"] = twice(x["L0_ffn_ln1_w"]), twice(x["L0_ffn_ln2_w"])

    swap = (np.arange(HD) + HD // 2) % HD

    def heads(w, n, order):
        w = np.transpose(np.reshape(w, (n, HD, D))[:, order, :], (2, 1, 0))
        z = np.zeros((2, D, HD, 2, n), np.float32)
        z[0, :, :, 0, :] = w
        z[1, :, :, 1, :] = w
        return np.reshape(z, (P, HD * 2 * n))

    same = np.arange(HD)
    h["wq"] = np.stack([heads(x["L0_ffn_wq"], NH, same), heads(x["L0_ffn_wq"], NH, swap)], 1)
    h["wk"] = np.stack([heads(x["L0_ffn_wk"], NKV, same), heads(x["L0_ffn_wk"], NKV, swap)], 1)
    h["wv"] = bd(np.transpose(x["L0_ffn_wv"]))
    h["wo"] = bd(np.transpose(x["L0_ffn_wo"]))
    inv = 1.0 / 10000.0 ** (np.arange(0, HD, 2, dtype=np.float32) / HD)
    ang = np.outer(np.arange(T, dtype=np.float32), inv)
    ang = np.concatenate([ang, ang], -1).T
    sign = np.where(np.arange(HD) < HD // 2, -1.0, 1.0)[:, None]
    cs = np.stack([np.cos(ang), np.sin(ang) * sign], 1).astype(np.float32)
    h["ropeq"] = np.repeat(cs * np.float32(HD ** -0.5), 2 * NH, 0)
    h["ropek"] = np.repeat(cs, 2 * NKV, 0)
    h["rw"] = np.concatenate([np.transpose(x["L0_ffn_router_w"]), np.zeros((D, NE), np.float32)], 0)
    for name in ("w1", "w3"):
        w = np.reshape(np.transpose(x["L0_ffn_" + name], (2, 0, 1)), (D, F))
        h[name] = np.concatenate([w, w], 0)
    w = np.zeros((NJ * P, D), np.float32)
    w[:F] = np.reshape(np.transpose(x["L0_ffn_w2"], (0, 2, 1)), (F, D))
    h["w2"] = np.transpose(np.reshape(w, (NJ, P, D)), (1, 0, 2))
    z = np.zeros((P, NJ * P), np.float32)
    for p in range(PIECES):
        for e in range(NE):
            z[p * NE + e, e * HID:(e + 1) * HID] = 1.0
    h["selg"] = z
    h["idx"] = np.reshape(np.transpose(np.reshape(x["x"], (NP, 2, NT, P)), (3, 0, 2, 1)), (P, NP * G))
    h["table"] = np.reshape(x["L0_tok_ple_table"], (VOCAB * HIDDEN // D, D))
    return {k: np.ascontiguousarray(v) for k, v in h.items()}


def kernel(**inputs):
    import concourse.bacc as bacc
    from concourse.bass_utils import run_bass_kernel_spmd

    arrays = _host({k: np.asarray(v) for k, v in inputs.items()})
    nc = bacc.Bacc("TRN2", target_bir_lowering=False, num_devices=1)
    a = {k: nc.dram_tensor("in_" + k, v.shape, mybir.dt.from_np(v.dtype), kind="ExternalInput").ap()
         for k, v in arrays.items()}
    a["out"] = nc.dram_tensor("out", (B, T, D), mybir.dt.float32, kind="ExternalOutput").ap()
    tower(nc, a)
    r = run_bass_kernel_spmd(nc, [{"in_" + k: v for k, v in arrays.items()}], core_ids=[0])
    return r.results[0]["out"]
```

```python
import numpy as np
import concourse.bass as bass
from concourse import mybir
from concourse.alu_op_type import AluOpType as ALU
from contextlib import ExitStack

B, T, D = 32, 512, 64
P = 128
NP = B // 2
NT = T // P
G = 2 * NT
VOCAB, HIDDEN, LAYER = 32000, 512, 3
L = 64
NC = T // L
NH, NKV, HD = 4, 2, 16
NE, HID = 8, 170
F = NE * HID
NJ = (F + P - 1) // P
NEG = -1.0e30
LOADS = 22
CASTS = 16
ROW_STEPS = 6
PIECES = 3


def tower(nc, a):
    f32, bf16, i32 = mybir.dt.float32, mybir.dt.bfloat16, mybir.dt.int32
    ACT, AX = mybir.ActivationFunctionType, mybir.AxisListType.X
    pe, act, dve, pool, sp = nc.tensor, nc.scalar, nc.vector, nc.gpsimd, nc.sync
    ctx = ExitStack()

    def sb(name, shape, dt=f32):
        return ctx.enter_context(nc.sbuf_tensor(name, shape, dt))

    def dram(name, shape, dt):
        return nc.dram_tensor(name, shape, dt, kind="Internal").ap()

    with ctx:
        ident = sb("ident", [P, P])
        identb = sb("identb", [P, P], bf16)
        maskb = sb("maskb", [P, 2 * P], bf16)
        chunkmask = sb("chunkmask", [P, P])
        batchmask = sb("batchmask", [P, P])
        restart = sb("restart", [P, T])
        onesbd = sb("onesbd", [P, 2])
        half3 = sb("half3", [P, 2 * G])
        rev = sb("rev", [P, NE])
        proj = sb("proj", [P, 6, P])
        bias = sb("bias", [P, 6])
        ibias = sb("ibias", [P, 1])
        bi = sb("bi", [P, 2])
        nscale = sb("nscale", [P, D])
        ln1 = sb("ln1", [P, 1])
        ln2 = sb("ln2", [P, 1])
        wq = sb("wq", [P, 2, P])
        wk = sb("wk", [P, P])
        wv = sb("wv", [P, D])
        wo = sb("wo", [P, P])
        ropeq = sb("ropeq", [P, 2, T])
        ropek = sb("ropek", [P, T])
        rw = sb("rw", [P, NE])
        w13 = sb("w13", [P, 2, 3, F], bf16)
        w2 = sb("w2", [P, NJ, D])
        selg = sb("selg", [P, NJ * P], bf16)
        idx = sb("idx", [P, NP * G], i32)
        idxc = sb("idxc", [P, G], i32)

        x0 = sb("x0", [P, G, D])
        xr = sb("xr", [P, G, D])
        st = sb("st", [P, 8, G])
        xc = sb("xc", [P, G, D])
        xn = xc
        xm = sb("xm", [P, G, D])
        xT = sb("xT", [P, T])
        qT = sb("qT", [P, T])
        kT = sb("kT", [P, T])
        ab = sb("ab", [P, 3, T])
        mn = sb("mn", [P, 3, T])
        li = sb("li", [P, T])
        mext = sb("mext", [P, T + 1])
        gcum = sb("gcum", [P, T])
        wexp = sb("wexp", [P, T])
        eexp = sb("eexp", [P, T])
        uT = sb("uT", [P, T])
        ek = sb("ek", [P, T])
        wdec = sb("wdec", [P, T])
        nst = ek
        wqx = sb("wqx", [P, T])
        prod = wqx
        hw = sb("hw", [P, T])
        pad = sb("pad", [P, 1])
        ktok = sb("ktok", [P, NT, P])
        utok = sb("utok", [P, NT, P])
        atm = sb("atm", [P, 2, T])
        dlt = sb("dlt", [P, NC, P])
        stT = sb("stT", [P, NC - 1, P])
        hgT = sb("hgT", [P, T])
        ht = sb("ht", [P, G, D])
        mt = sb("mt", [P, 24, G])
        h1 = sb("h1", [P, G, D])
        y0 = sb("y0", [P, G, D])
        hc = sb("hc", [P, G, D])
        ho = ht
        hn = sb("hn", [P, G, D])
        y0b = sb("y0b", [P, G, D])
        hy = sb("hy", [P, G, D])
        hnT = sb("hnT", [P, T])
        t1 = sb("t1", [P, 2, T])
        t2 = sb("t2", [P, 2, T])
        qr = t2
        qp = sb("qp", [P, PIECES, T], bf16)
        kp = sb("kp", [D, PIECES, T], bf16)
        qs = sb("qs", [P, 2 * NH, T], bf16)
        ks = sb("ks", [P, 2 * NKV, T], bf16)
        va = sb("va", [P, NT, 2 * NKV, 32])
        nm = sb("nm", [P, NT, 2 * NH])
        nmr = sb("nmr", [P, NT, 2 * NH])
        mp = sb("mp", [P, NT, PIECES, 2 * NH], bf16)
        mrow = sb("mrow", [PIECES * 2 * NH, T], bf16)
        pr = sb("pr", [P, 2, NH, T])
        yT = sb("yT", [P, 2, T])
        rden = sb("rden", [P, 2, NT * NH])
        x2 = sb("x2", [P, G, D])
        bt = sb("bt", [P, 7, G])
        hx = sb("hx", [P, G, D])
        xf = sb("xf", [P, 2, T])
        xa = sb("xa", [P, 2, T], bf16)
        xb = sb("xb", [P, 2, T], bf16)
        xres = sb("xres", [D, T])
        x2p = sb("x2p", [D, T], bf16)
        lg = sb("lg", [P, 15, G, NE])
        ls = sb("ls", [P, 12, G])
        wp = sb("wp", [P, G, PIECES, NE], bf16)
        wT = sb("wT", [P, 2, T], bf16)
        sl = sb("sl", [P, 2, T])
        sgt = sl
        moT = sl[:, 0, :]
        xsq, x2sq = [ab[:, q, :].rearrange("p (g d) -> p g d", d=D) for q in range(2)]
        fl = pr[:, 0, 0:2, :].rearrange("p a t -> p (a t)").rearrange("p (g a d) -> p g a d", a=2, d=D)
        ynT = hnT
        yn = x2[:, :, :].rearrange("p (t b) (h d) -> p t b h d", b=2, h=NH)
        hsq = atm[:, 0, :].rearrange("p (g d) -> p g d", d=D)
        hh = sb("hh", [P, 2, 2, T])
        ot = sb("ot", [P, G, D])

        wtmp = pr[:, :, :, :].rearrange("p a h t -> p (a h t)")[:, 0:2 * F].rearrange("p (m f) -> p m f", m=2)
        maskf = mn[:, 1, 0:2 * P]
        selgf = ab[:, :, :].rearrange("p a t -> p (a t)")[:, 0:NJ * P]

        banks = [ctx.enter_context(nc.psum_tensor(f"bank{i}", [P, T], f32)) for i in range(8)]
        ybank, h1bank, gbank, h3bank, obank = banks[2], banks[3], banks[4], banks[5], banks[7]
        sring, ering = banks[0:2], (banks[0], banks[1], banks[5])

        qscr = dram("qscr", [PIECES * HD, 2 * NH, T], bf16)
        kscr = dram("kscr", [PIECES * HD, 2 * NKV, T], bf16)
        mscr = dram("mscr", [PIECES, 2 * NH, T], bf16)


        SKEW = dict(f=0, g=1, m=2, q=2, b=3, a=4, e=4, h=4, c=5, d=5)
        SLOTS = [row.split() for row in (
            "c0 d0 m0 b38 b39",
            "c1 d1 b5 g1",
            "c2 d2 b40 b41 m1 m2 g2 a32",
            "c3 d3 m3 a33",
            "c4 d4 m4",
            "c5 d5 m5",
            "c6 d6 a34 m6",
            "c7 b6 d7 b7 g3 g4 m18 f0",
            "c8 b8 d8 m19 a35 a36",
            "c9 b9 d9 b10 g7",
            "c10 b11 d10 b42 m7 a37",
            "c11 b12 d11 b13 m8",
            "c12 b14 d12 b15 m11 a38",
            "c13 d13 m9",
            "c14 d14 g8",
            "c15 b16 b17 d15 m10 m12 m13",
            "c16 b18 d16 g9",
            "c17 b19 d17 g5 m14 g18",
            "c18 b20 d18 e0 b43",
            "c19 b21 d19 m15 g17",
            "c20 d20 b22 m16",
            "c21 d21 g6")]
        SECOND = ("e1 c22 g10 e9 e2 g19 c23 e7 m17 g11 b23 e8 q0 b24 g12 g13 e10 e5 b25 q1 e11 g14 q2 b26 b27 "
                  "e6 e12 g15 q3 q4 b28 e3 g16 b29 b30 h0 e4 b31").split()
        ORDER = [step for row in SLOTS for step in row] + SECOND
        READERS, held = [], []
        for row in SLOTS:
            filler = [step for step in row if not (step[0] in "cd" or (step[0] == "b" and 6 <= int(step[1:]) <= 21))]
            READERS += [step for step in row if step not in filler] + held
            held = filler
        READERS += held + SECOND
        MAXIMA = [(f"b{6 + 8 * b + 2 * t + x}", b, t, h, m) for b in range(2) for t in range(NT) for x in range(2)
                  for m in [2 if t < 2 else 1] for h in range(2 * x, 2 * x + 2, m)]
        EXPS = [(f"b{23 + NT * b + t}", b, t, h, m) for b in range(2) for t in range(NT)
                for m in [(1, 1, 2, 4)[t]] for h in range(0, NH, m)]

        READ = dict(g4=[("xT", 1)], g5=[("qT", 1)], g6=[("kT", 1)], g7=[("si", 1)], g8=[("gx", 1)], g9=[("gx", 2)],
                    g15=[("uT", 1)],
                    m0=[("ktok", 1)], m1=[("utok", 1)], m2=[("atm", 1)], m3=[("atm", 2)], m4=[("dlt", 1)],
                    m5=[("dlt", 2)], m7=[("stT", 1)], m8=[("stT", 2)], m9=[("hgT", 1)], m10=[("ht", 1)],
                    m11=[("dabs", 1)],
                    q0=[("hnT", 1)], q1=[("t1", 1)], q2=[("t2", 1)], q3=[("t1", 2), ("t2", 2)], b5=[("va", 1)],
                    b22=[("mrow", 1)], a32=[("yn", 1)], a33=[("yn", 2)], a34=[("ynT", 1)], a35=[("x2", 1), ("hx", 1)],
                    e0=[("xf", 1)], e1=[("xf", 2)], e2=[("lg", 1)], e3=[("wT", 1)], c23=[("ot", 1)])
        TENANTS = [step for step in ORDER if step in READ]
        NTH = {step: 1 + [t for t in TENANTS if t[0] == step[0]].index(step) for step in TENANTS}
        BANK, used = {}, {bank: bank for bank in range(8)}
        for step in TENANTS:
            at = ORDER.index(step)
            if at > ORDER.index("c22"):
                free = (6, 3, 4, 7)
            elif ORDER.index("c4") < at < ORDER.index("b21"):
                free = (6, 2)
            else:
                free = (6, 2, 0, 1)
            BANK[step] = min(free, key=used.get)
            used[BANK[step]] = 100 + at
        USERS = [[] for _ in range(8)]
        for step in ORDER:
            if step in BANK:
                USERS[BANK[step]].append((step, READ[step]))
            if step in ("h0", "c0"):
                for bank, name in {"h0": ((3, "silu"), (4, "gated")), "c0": ((5, "hh"), (7, "moT"))}[step]:
                    USERS[bank].append((step, [(name, {"moT": 1}.get(name, 2 * NJ))]))
            if step == "b6":
                for bank in (0, 1):
                    USERS[bank].append((step, [("smax", len(MAXIMA))]))
            if step == "b23":
                for bank in (0, 1, 5):
                    USERS[bank].append((step, [("pexp", len(EXPS))]))
            if step == "b24":
                USERS[2].append((step, [("yT", 2)]))

        PER = dict(
            idxc=1, x0=16 * G, xm=1, xres=1, g_sum=1, g_nm=1, xc=1, xsq=1, g_var=1, g_v=1, g_bits=1, g_half=1,
            g_guess=1, g_newton=12, xn=1,
            xT=1, qT=1, kT=1, gx=2, gabs=1, gexp=1, gln=1, lf=1, lso=1, si=1, so=1, li=1, mscan=1, lfc=1,
            gcum=1, aw=1, ae=1, wexp=1, eexp=1, uT=1, ek=1, wdec=1, nst=1, wqx=1, prod=1, hw=1,
            ktok=1, utok=1, atm=2, dlt=2, dltw=1, state=NC - 2, stT=2, hgT=1, ht=1, dabs=1, den=1, rd=1, hsq=1,
            hsum=1, rd2=1,
            hms=1, mh_v=1, mh_bits=1, mh_half=1, mh_guess=1, mh_newton=12, hf=1, ho=1, hos=1, h1=1, m_sum=1, m_nm=1,
            hc=1, hsq2=1, m_var=1, ml_v=1, mr_v=1,
            ml_bits=1, ml_half=1, ml_guess=1, ml_newton=12, hn=1, y0=1,
            hy=1, y0b=1, hnT=1, t1=2, t2=2, qr=2, p1=2, r1=2, p2=2, p3=2, qk_out=32, qk_in=16 * 7, va=1,
            smax=len(MAXIMA),
            mp=5, mrow=1, m_out=16, m_in=16, pexp=len(EXPS), yT=2, rden=2, yn=2, ynT=1, x2=1, hx=1, x2sq=1, b_var=1,
            b_v=1, b_bits=1, b_half=1, b_guess=1, b_newton=12, fl=1,
            xf=2, cast1=4, xahi=2, cres=2, cast2=2, xblo=2, hxc=1, lg=1, r_dve=21, r_act=1, wp=5, wT=1,
            silu=2 * NJ, gated=2 * NJ, hh=2 * NJ, moT=1, ot=1, out=32,
            pe_gate=7, pe_mem=11, pe_qk=4, pe_attn=2, pe_tail=4, pe_prep=4, pe_moe=1, pe_s=len(MAXIMA),
            pe_st=len(EXPS), pe_pv=8,
            pe_h1=2 * NJ, pe_g=2 * NJ, pe_h3=2 * NJ, pe_down=NJ)
        s = {name: ctx.enter_context(nc.semaphore(name)) for name in PER}
        loaded = ctx.enter_context(nc.semaphore("loaded"))
        idx_in = ctx.enter_context(nc.semaphore("idx_in"))
        w13_in = ctx.enter_context(nc.semaphore("w13_in"))
        rows = ctx.enter_context(nc.semaphore("rows"))
        cleared = ctx.enter_context(nc.semaphore("cleared"))
        cast = ctx.enter_context(nc.semaphore("cast"))
        setup = ctx.enter_context(nc.semaphore("setup"))

        PE_OF = dict(g="pe_gate", m="pe_mem", q="pe_qk", b="pe_attn", a="pe_tail", e="pe_prep", c="pe_moe")

        def upto(name, n, k=1):
            return n * PER[name] + k

        def full(name, n):
            return upto(name, n, PER[name])

        def later(n):
            return type(n) is not int or n > 0

        FIRST = SKEW["c"] + 1

        def active(it):
            return [c for c in SKEW if 0 <= it - SKEW[c] < NP]

        def before(step, bank, it, stages):
            mine = [u for u in USERS[bank] if u[0][0] in stages]
            at = [u[0] for u in mine].index(step)
            if at > 0:
                prev, reads = mine[at - 1]
            else:
                last = active(it - 1) if type(it) is int else list(SKEW)
                mine = [u for u in USERS[bank] if u[0][0] in last]
                if not mine:
                    return []
                (prev, reads), it = mine[-1], it - 1
            return [(name, upto(name, it - SKEW[prev[0]], k)) for name, k in reads]

        def run(program, engine):
            for it in range(FIRST):
                program(it, active(it))
            with engine.Fori(FIRST, NP) as it:
                program(it, list(SKEW))
            for it in range(NP, NP + SKEW["c"]):
                program(it, active(it))

        def bc(t, n):
            return t.unsqueeze(2).to_broadcast([t.shape[0], t.shape[1], n])

        def rsqrt_guess(site, n, tiny):
            dve.tensor_scalar(out=tiny[2].bitcast(i32), in0=tiny[0].bitcast(i32), scalar1=1, scalar2=None,
                              op0=ALU.arith_shift_right).then_inc(s[site + "_bits"], 1)
            dve.tensor_scalar(out=tiny[1], in0=tiny[0], scalar1=-0.5, scalar2=None,
                              op0=ALU.mult).then_inc(s[site + "_half"], 1)
            dve.wait_ge(s[site + "_bits"], upto(site + "_bits", n))
            dve.tensor_scalar(out=tiny[4].bitcast(i32), in0=tiny[2].bitcast(i32), scalar1=-1.0,
                              scalar2=float(0x5F3759DF), op0=ALU.mult, op1=ALU.add).then_inc(s[site + "_guess"], 1)

        def newton(site, n, tiny):
            name = site + "_newton"
            pool.wait_ge(s[site + "_half"], upto(site + "_half", n))
            pool.wait_ge(s[site + "_guess"], upto(site + "_guess", n))
            for r in range(3):
                if r:
                    pool.wait_ge(s[name], upto(name, n, 4 * r))
                pool.tensor_tensor(out=tiny[2], in0=tiny[4], in1=tiny[4], op=ALU.mult).then_inc(s[name], 1)
                pool.wait_ge(s[name], upto(name, n, 4 * r + 1))
                pool.tensor_tensor(out=tiny[3], in0=tiny[2], in1=tiny[1], op=ALU.mult).then_inc(s[name], 1)
                pool.wait_ge(s[name], upto(name, n, 4 * r + 2))
                pool.tensor_tensor(out=tiny[2], in0=tiny[3], in1=half3[:, 0:tiny[3].shape[1]],
                                   op=ALU.add).then_inc(s[name], 1)
                pool.wait_ge(s[name], upto(name, n, 4 * r + 3))
                pool.tensor_tensor(out=tiny[4], in0=tiny[4], in1=tiny[2], op=ALU.mult).then_inc(s[name], 1)

        g_tiny = [st[:, r, :] for r in range(5)]
        mh_tiny = [mt[:, r, :] for r in range(5)]
        ml_tiny = [mt[:, 5 + 2 * r:7 + 2 * r, :].rearrange("p a g -> p (a g)") for r in range(5)]
        b_tiny = [bt[:, r, :] for r in range(5)]
        wend = wexp[:, :].rearrange("p (c l) -> p c l", l=L)[:, :, L - 1]
        block = ctx.enter_context(nc.Block())

        @block.sync
        def _(_e):
            sp.dma_start(idx[:, :], a["idx"]).then_inc(idx_in, 16)
            sp.dma_start(wtmp[:, 0, :], a["w1"]).then_inc(w13_in, 16)
            sp.dma_start(wtmp[:, 1, :], a["w3"]).then_inc(w13_in, 16)
            for dst, name in ((ident, "ident"), (maskf, "maskf"), (chunkmask, "chunkmask"), (batchmask, "batchmask"),
                              (restart, "restart"), (onesbd, "onesbd"), (rev, "rev"), (proj, "proj"), (bias, "bias"),
                              (ibias, "ibias"), (nscale, "nscale"), (ln1, "ln1"), (ln2, "ln2"), (wq, "wq"),
                              (wk, "wk"), (wv, "wv"), (wo, "wo"), (ropeq, "ropeq"), (ropek, "ropek"), (rw, "rw"),
                              (w2, "w2")):
                sp.dma_start(dst if type(dst) is bass.AP else dst[(slice(None),) * len(dst.shape)],
                             a[name]).then_inc(loaded, 16)
            sp.dma_start(selgf, a["selg"]).then_inc(loaded, 16)

            def program(it, stages):
                for step in [x for x in ORDER if x[0] in stages]:
                    n = it - SKEW[step[0]]
                    misc = banks[BANK[step]] if step in BANK else None
                    if step == "b41":
                        sp.wait_ge(s["p3"], upto("p3", n, 1))
                        sp.dma_start(qscr.rearrange("(p d) g t -> (d g) p t", p=PIECES),
                                     qp[:, :, :]).then_inc(s["qk_out"], 16)
                        sp.wait_ge(s["p3"], upto("p3", n, 2))
                        sp.dma_start(kscr.rearrange("(p d) g t -> (d g) p t", p=PIECES),
                                     kp[:, :, :]).then_inc(s["qk_out"], 16)
                        sp.wait_ge(s["qk_out"], full("qk_out", n))
                        if later(n):
                            sp.wait_ge(s["pe_st"], full("pe_st", n - 1))
                        for dst, src, at, rows, frm in (
                                (qs, qscr, 0, 16, 0), (qs, qscr, 16, 16, 0), (qs, qscr, 32, 32, 0),
                                (qs, qscr, 64, 32, 16), (ks, kscr, 0, 48, 0), (ks, kscr, 48, 32, 0),
                                (ks, kscr, 80, 16, 0)):
                            sp.dma_start(dst[at:at + rows, :, :], src[frm:frm + rows, :, :]).then_inc(s["qk_in"], 16)
                    if step == "b22":
                        sp.wait_ge(s["mrow"], upto("mrow", n))
                        sp.dma_start(mscr.rearrange("p g t -> (p g) t"), mrow[:, :]).then_inc(s["m_out"], 16)
                        sp.wait_ge(s["m_out"], full("m_out", n))
                        sp.dma_start(qs[PIECES * 2 * HD:PIECES * 2 * HD + PIECES, :, :], mscr).then_inc(s["m_in"], 16)
                    if step == "c23":
                        sp.wait_ge(s["ot"], upto("ot", n))
                        for b in range(2):
                            dst = a["out"][bass.ds(n * 2 + b, 1), :, :].rearrange("o (i p) d -> p (o i) d", p=P)
                            src = ot[:, :, :].rearrange("p (i b) d -> p i b d", b=2)[:, :, b, :]
                            sp.dma_start(dst, src).then_inc(s["out"], 16)

            run(program, sp)
            sp.wait_ge(s["out"], full("out", NP - 1))

        @block.tensor
        def _(_e):
            def mm(out, lhsT, rhs, start=True, stop=True, **k):
                return pe.matmul(out, lhsT, rhs, start=start, stop=stop, **k)

            def four(step, src):
                misc = banks[BANK[step]]
                for t in range(NT):
                    last = pe.transpose(misc[:, t * P:(t + 1) * P], src(t), ident[:, :])
                last.then_inc(s[PE_OF[step[0]]], 1)

            def done(step, last):
                last.then_inc(s[PE_OF[step[0]]], 1)

            pe.wait_ge(loaded, 16 * LOADS)
            pe.wait_ge(cleared, 9)
            pe.wait_ge(cast, CASTS)

            def down(n, j):
                rows = min(P, F - j * P)
                pe.wait_ge(s["hh"], upto("hh", n, 2 * j + 2))
                for b in range(2):
                    last = mm(obank[D * b:D * b + D, :], w2[0:rows, j, :], hh[0:rows, j % 2, b, :],
                              start=j == 0, stop=j == NJ - 1)
                last.then_inc(s["pe_down"], 1)

            def up(n, u):
                b = u % 2
                cols = slice(u // 2 * P, min(F, (u // 2 + 1) * P))
                w = cols.stop - cols.start
                if u:
                    pe.wait_ge(s["silu"], upto("silu", n, u))
                for p, mov in enumerate((xa, xa, xb)):
                    last = mm(h1bank[0:w, :], w13[:, 0, p, cols], mov[:, b, :], start=p == 0, stop=p == 2)
                last.then_inc(s["pe_h1"], 1)
                if u:
                    pe.wait_ge(s["gated"], upto("gated", n, u))
                mm(gbank[0:w, :], selg[:, cols], wT[:, b, :]).then_inc(s["pe_g"], 1)

            def pv(n, k):
                b, t = k // NT, k % NT
                pe.wait_ge(s["pexp"], upto("pexp", n, len([x for x in EXPS if (x[1], x[2]) <= (b, t)])))
                if t == 0 and b:
                    pe.wait_ge(s["yT"], upto("yT", n, 1))
                for h in range(NH):
                    last = mm(ybank[32 * h:32 * h + 32, t * P:T], va[:, t, b * NKV + h // 2, :],
                              pr[:, k % 2, h, 0:T - t * P], start=t == 0, stop=t == NT - 1)
                last.then_inc(s["pe_pv"], 1)

            def program(it, stages):
                for step in [x for x in ORDER if x[0] in stages]:
                    n = it - SKEW[step[0]]
                    misc = banks[BANK[step]] if step in BANK else None
                    c, k = step[0], int(step[1:])
                    if step in BANK:
                        for name, value in before(step, BANK[step], it, stages):
                            pe.wait_ge(s[name], value)
                    if step == "g4":
                        pe.wait_ge(s["xn"], upto("xn", n))
                        four(step, lambda t: xn[:, 2 * t:2 * t + 2, :].rearrange("p b d -> p (b d)"))
                    if c == "g" and 5 <= k <= 9:
                        pe.wait_ge(s["xT"], upto("xT", n))
                        done(step, mm(misc[:, :], proj[:, (0, 1, 3, 4, 5)[k - 5], :], xT[:, :]))
                    if step == "g15":
                        done(step, mm(misc[:, :], proj[:, 2, :], xT[:, :]))
                    if step == "m0":
                        pe.wait_ge(s["kT"], upto("kT", n))
                        four(step, lambda t: kT[:, t * P:(t + 1) * P])
                    if step == "m1":
                        pe.wait_ge(s["uT"], upto("uT", n))
                        four(step, lambda t: uT[:, t * P:(t + 1) * P])
                    if step in ("m2", "m3"):
                        b = k - 2
                        for t in range(NT):
                            last = mm(misc[:, t * P:(t + 1) * P], kT[D * b:D * b + D, t * P:(t + 1) * P],
                                      qT[D * b:D * b + D, t * P:(t + 1) * P])
                        done(step, last)
                    if step in ("m4", "m5"):
                        if step == "m4":
                            pe.wait_ge(s["ktok"], upto("ktok", n))
                            pe.wait_ge(s["utok"], upto("utok", n))
                        par = k - 4
                        for q in range(NT - par):
                            last = mm(misc[:, q * P:(q + 1) * P], utok[L * par:L * par + L, q, :],
                                      ktok[L * par:L * par + L, q, :])
                        done(step, last)
                    if step in ("m7", "m8"):
                        pe.wait_ge(s["state"], full("state", n))
                        lo, hi = ((0, 4), (4, NC - 1))[k - 7]
                        for j in range(lo, hi):
                            last = pe.transpose(misc[:, (j - lo) * P:(j - lo + 1) * P], dlt[:, j, :], ident[:, :])
                        done(step, last)
                    if step == "m9":
                        pe.wait_ge(s["stT"], full("stT", n))
                        pe.wait_ge(s["atm"], full("atm", n))
                        for j in range(1, NC):
                            mm(misc[:, j * L:(j + 1) * L], stT[:, j - 1, :], qT[:, j * L:(j + 1) * L], start=j == 1,
                               stop=False, skip_group_check=True)
                        for t in range(NT):
                            for b in range(2):
                                last = mm(misc[D * b:D * b + D, t * P:(t + 1) * P], utok[:, t, D * b:D * b + D],
                                          atm[:, b, t * P:(t + 1) * P], start=False, stop=t == NT - 1,
                                          skip_group_check=True)
                        done(step, last)
                    if step == "m10":
                        pe.wait_ge(s["hgT"], upto("hgT", n))
                        four(step, lambda t: hgT[:, t * P:(t + 1) * P])
                    if step == "m11":
                        pe.wait_ge(s["prod"], upto("prod", n))
                        for t in range(NT):
                            last = mm(misc[:, 2 * t:2 * t + 2], prod[:, t * P:(t + 1) * P], onesbd[:, :])
                        done(step, last)
                    if step == "q0":
                        pe.wait_ge(s["hn"], upto("hn", n))
                        four(step, lambda t: hn[:, 2 * t:2 * t + 2, :].rearrange("p b d -> p (b d)"))
                    if step in ("q1", "q2"):
                        if step == "q1":
                            pe.wait_ge(s["hnT"], upto("hnT", n))
                        done(step, mm(misc[:, :], wq[:, k - 1, :], hnT[:, :]))
                    if step == "q3":
                        done(step, mm(misc[:, :], wk[:, :], hnT[:, :]))
                    if step == "b5":
                        for t in range(NT):
                            last = mm(misc[:, t * D:(t + 1) * D], hnT[:, t * P:(t + 1) * P], wv[:, :])
                        done(step, last)
                    if c == "b" and 6 <= k <= 21:
                        if k == 6:
                            pe.wait_ge(s["qk_in"], full("qk_in", n))
                            for bank in (0, 1):
                                for name, value in before(step, bank, it, stages):
                                    pe.wait_ge(s[name], value)
                        for u, (_, b, t, h, m) in [x for x in enumerate(MAXIMA) if x[1][0] == step]:
                            if u >= 2:
                                pe.wait_ge(s["smax"], upto("smax", n, u - 1))
                            w = (t + 1) * P
                            for x in range(m):
                                mm(sring[u % 2][:, x * w:(x + 1) * w], qs[:, b * NH + h + x, t * P:(t + 1) * P],
                                   ks[:, b * NKV + (h + x) // 2, 0:w], stop=False)
                                last = mm(sring[u % 2][:, x * w + t * P:(x + 1) * w], identb[:, :], maskb[:, 0:P],
                                          start=False)
                            last.then_inc(s["pe_s"], 1)
                    if step == "b22":
                        pe.wait_ge(s["mp"], full("mp", n))
                        for t in range(NT):
                            last = pe.transpose(misc[:, :].bitcast(bf16)[0:PIECES * 2 * NH, t * P:(t + 1) * P],
                                                mp[:, t, :, :].rearrange("p a b -> p (a b)"), identb[:, :])
                        done(step, last)
                    if c == "b" and 23 <= k <= 30:
                        if k == 23:
                            pe.wait_ge(s["m_in"], upto("m_in", n, 16))
                            for bank in (0, 1, 5):
                                for name, value in before(step, bank, it, stages):
                                    pe.wait_ge(s[name], value)
                        if k == 24:
                            for name, value in before(step, 2, it, stages):
                                pe.wait_ge(s[name], value)
                        for u, (_, b, t, h, m) in [x for x in enumerate(EXPS) if x[1][0] == step]:
                            if u >= 3:
                                pe.wait_ge(s["pexp"], upto("pexp", n, u - 2))
                            w = T - t * P
                            for x in range(m):
                                mm(ering[u % 3][:, x * w:(x + 1) * w], ks[:, b * NKV + (h + x) // 2, t * P:(t + 1) * P],
                                   qs[:, b * NH + h + x, t * P:T], stop=False)
                                last = mm(ering[u % 3][:, x * w:x * w + P], identb[:, :], maskb[:, P:2 * P],
                                          start=False)
                            last.then_inc(s["pe_st"], 1)
                        if k > 23:
                            pv(n, k - 24)
                    if step == "b31":
                        pv(n, 7)
                    if step in ("a32", "a33"):
                        pe.wait_ge(s["yT"], upto("yT", n, k - 31))
                        four(step, lambda t: yT[:, k - 32, t * P:(t + 1) * P])
                    if step == "a34":
                        pe.wait_ge(s["yn"], full("yn", n))
                        four(step, lambda t: yn[:, t, :, :, :].rearrange("p b h d -> p (b h d)"))
                    if step == "a35":
                        pe.wait_ge(s["ynT"], upto("ynT", n))
                        for t in range(NT):
                            last = mm(misc[:, t * P:(t + 1) * P], ynT[:, t * P:(t + 1) * P], wo[:, :])
                        done(step, last)
                    if step in ("e0", "e1"):
                        pe.wait_ge(s["fl"], upto("fl", n))
                        four(step, lambda t: fl[:, 2 * t + k, :, :].rearrange("p a d -> p (a d)"))
                    if step == "e2":
                        pe.wait_ge(s["xf"], full("xf", n))
                        for g in range(G):
                            last = mm(misc[:, g * NE:(g + 1) * NE], xf[:, g % 2, (g // 2) * P:(g // 2 + 1) * P],
                                      rw[:, :])
                        done(step, last)
                    if step == "e3":
                        pe.wait_ge(s["wp"], full("wp", n))
                        for g in range(G):
                            col = (g % 2) * T + (g // 2) * P
                            last = pe.transpose(misc[:, :].bitcast(bf16)[0:PIECES * NE, col:col + P],
                                                wp[:, g, :, :].rearrange("p a b -> p (a b)"), identb[:, :])
                        done(step, last)
                    if c == "c" and k < 2 * NJ:
                        j, b, u = k // 2, k % 2, k
                        cols = slice(j * P, min(F, (j + 1) * P))
                        w = cols.stop - cols.start
                        if u == 0:
                            for bank in (5, 7):
                                for name, value in before(step, bank, it, stages):
                                    pe.wait_ge(s[name], value)
                        if u:
                            pe.wait_ge(s["hh"], upto("hh", n, u))
                        for p, mov in enumerate((xa, xa, xb)):
                            last = mm(h3bank[0:w, :], w13[:, 1, p, cols], mov[:, b, :], start=p == 0, stop=p == 2)
                        last.then_inc(s["pe_h3"], 1)
                    if step == "h0":
                        pe.wait_ge(s["xahi"], full("xahi", n))
                        pe.wait_ge(s["xblo"], full("xblo", n))
                        pe.wait_ge(s["wT"], upto("wT", n))
                        for bank in (3, 4):
                            for name, value in before(step, bank, it, stages):
                                pe.wait_ge(s[name], value)
                        up(n, 0)
                    if c == "d":
                        if k + 1 < 2 * NJ:
                            up(n, k + 1)
                        if k % 2 and k > 1:
                            down(n, k // 2 - 1)
                    if step == "c23":
                        pe.wait_ge(s["moT"], upto("moT", n))
                        four(step, lambda t: moT[:, t * P:(t + 1) * P])
                    if step == "c22":
                        down(n, NJ - 1)

            run(program, pe)

        @block.scalar
        def _(_e):
            act.wait_ge(loaded, 16 * LOADS)

            def program(it, stages):
                for step in [x for x in READERS if x[0] in stages]:
                    n = it - SKEW[step[0]]
                    misc = banks[BANK[step]] if step in BANK else None
                    c, k = step[0], int(step[1:])
                    if step == "g1":
                        act.wait_ge(s["xc"], upto("xc", n))
                        act.activation(xsq[:, :, :], xc[:, :, :], ACT.Square).then_inc(s["xsq"], 1)
                        act.wait_ge(s["x0"], full("x0", n))
                        act.activation(xm[:, :, :], x0[:, :, :], ACT.Copy).then_inc(s["xm"], 1)
                    if step == "g4":
                        act.wait_ge(s["pe_gate"], upto("pe_gate", n, NTH[step]))
                        act.activation(xT[:, :], misc[:, :], ACT.Copy).then_inc(s["xT"], 1)
                    if step == "g5":
                        if later(n):
                            act.wait_ge(s["hgT"], upto("hgT", n - 1))
                        act.wait_ge(s["pe_gate"], upto("pe_gate", n, NTH[step]))
                        act.activation(qT[:, :], misc[:, :], ACT.Identity, bias=bias[:, 0:1]).then_inc(s["qT"], 1)
                    if step == "g7":
                        act.wait_ge(s["pe_gate"], upto("pe_gate", n, NTH[step]))
                        act.activation(li[:, :], misc[:, :], ACT.Tanh, scale=0.1, bias=bi[:, 0:1]).then_inc(s["si"], 1)
                    if step in ("g8", "g9"):
                        q = k - 7
                        act.wait_ge(s["pe_gate"], upto("pe_gate", n, NTH[step]))
                        act.activation(mn[:, q, :], misc[:, :], ACT.Identity, scale=(-1.0, 1.0)[q - 1],
                                       bias=(bi[:, 1:2], bias[:, 5:6])[q - 1]).then_inc(s["gx"], 1)
                    if step == "g18":
                        act.wait_ge(s["gx"], full("gx", n))
                        act.activation(ab[:, 1:3, :], mn[:, 1:3, :], ACT.Abs).then_inc(s["gabs"], 1)
                    if step == "g10":
                        act.preload_act_table_set("natural_log_exp_and_others")
                        act.wait_ge(s["gabs"], upto("gabs", n))
                        act.activation(ab[:, 1:3, :], ab[:, 1:3, :], ACT.Exp, scale=-1.0).then_inc(s["gexp"], 1)
                    if step == "g19":
                        act.wait_ge(s["gexp"], upto("gexp", n))
                        act.activation(ab[:, 1:3, :], ab[:, 1:3, :], ACT.Ln, bias=1.0).then_inc(s["gln"], 1)
                    if step == "g12":
                        act.wait_ge(s["lso"], upto("lso", n))
                        act.activation(ab[:, 2, :], mn[:, 2, :], ACT.Exp).then_inc(s["so"], 1)
                    if step == "g14":
                        act.wait_ge(s["aw"], upto("aw", n))
                        act.activation(wexp[:, :], mn[:, 0, :], ACT.Exp).then_inc(s["wexp"], 1)
                        act.wait_ge(s["ae"], upto("ae", n))
                        act.activation(eexp[:, :], mn[:, 2, :], ACT.Exp).then_inc(s["eexp"], 1)
                    if step == "g17":
                        act.wait_ge(s["xm"], upto("xm", n))
                        if later(n):
                            act.wait_ge(s["h1"], upto("h1", n - 1))
                        act.activation(xr[:, :, :], xm[:, :, :], ACT.Copy).then_inc(s["xres"], 1)
                    if step in ("m0", "m1"):
                        act.wait_ge(s["pe_mem"], upto("pe_mem", n, NTH[step]))
                        act.activation((ktok, utok)[k][:, :, :].rearrange("p a b -> p (a b)"), misc[:, :],
                                       ACT.Copy).then_inc(s[("ktok", "utok")[k]], 1)
                    if step in ("m7", "m8"):
                        lo, hi = ((0, 4), (4, NC - 1))[k - 7]
                        act.wait_ge(s["pe_mem"], upto("pe_mem", n, NTH[step]))
                        act.activation(stT[:, lo:hi, :].rearrange("p a b -> p (a b)"), misc[:, 0:(hi - lo) * P],
                                       ACT.Copy).then_inc(s["stT"], 1)
                    if step == "m10":
                        act.wait_ge(s["pe_mem"], upto("pe_mem", n, NTH[step]))
                        act.activation(ht[:, :, :].rearrange("p a b -> p (a b)"), misc[:, :],
                                       ACT.Copy).then_inc(s["ht"], 1)
                    if step == "m11":
                        act.wait_ge(s["pe_mem"], upto("pe_mem", n, NTH[step]))
                        act.activation(mt[:, 18, :], misc[:, 0:G], ACT.Abs).then_inc(s["dabs"], 1)
                    if step == "m12":
                        act.wait_ge(s["ht"], upto("ht", n))
                        act.activation(hsq[:, :, :], ht[:, :, :], ACT.Square).then_inc(s["hsq"], 1)
                    if step == "m15":
                        act.wait_ge(s["hc"], upto("hc", n))
                        act.activation(hsq[:, :, :], hc[:, :, :], ACT.Square).then_inc(s["hsq2"], 1)
                    if step == "q0":
                        act.wait_ge(s["pe_qk"], upto("pe_qk", n, NTH[step]))
                        act.activation(hnT[:, :], misc[:, :], ACT.Copy, scale=ln1[:, 0:1]).then_inc(s["hnT"], 1)
                    if step in ("b38", "b39"):
                        x, rows, dst = (0, P, qp) if step == "b38" else (1, D, kp)
                        if later(n):
                            act.wait_ge(s["qk_out"], full("qk_out", n - 1))
                        act.wait_ge(s["qr"], upto("qr", n, x + 1))
                        act.activation(dst[0:rows, 0, :], qr[0:rows, x, :], ACT.Copy).then_inc(s["p1"], 1)
                    if step in ("b40", "b41"):
                        x, rows, dst = (0, P, qp) if step == "b40" else (1, D, kp)
                        act.wait_ge(s["r1"], upto("r1", n, x + 1))
                        act.activation(dst[0:rows, 1, :], t1[0:rows, x, :], ACT.Copy).then_inc(s["p2"], 1)
                    if step == "b5":
                        if later(n):
                            act.wait_ge(s["pe_pv"], full("pe_pv", n - 1))
                        act.wait_ge(s["pe_attn"], upto("pe_attn", n, NTH[step]))
                        act.activation(va[:, :, :, 0:HD].rearrange("p t g d -> p (t g) d"),
                                       misc[:, 0:NT * D].rearrange("p (t d) -> p t d", d=HD),
                                       ACT.Copy).then_inc(s["va"], 1)
                    if step == "b22":
                        act.wait_ge(s["pe_attn"], upto("pe_attn", n, NTH[step]))
                        act.activation(mrow[:, :], misc[:, :].bitcast(bf16)[0:PIECES * 2 * NH, 0:T],
                                       ACT.Copy).then_inc(s["mrow"], 1)
                    if c == "b" and 23 <= k <= 30:
                        q = k - 23
                        b, t = q // NT, q % NT
                        if q == NT + 1:
                            act.wait_ge(s["pe_pv"], upto("pe_pv", n, NT))
                            act.activation(yT[:, 0, :], ybank[:, :], ACT.Copy).then_inc(s["yT"], 1)
                        if q >= 2:
                            act.wait_ge(s["pe_pv"], upto("pe_pv", n, q - 1))
                        for u, (_, b, t, h, m) in [x for x in enumerate(EXPS) if x[1][0] == step]:
                            w = T - t * P
                            act.wait_ge(s["pe_st"], upto("pe_st", n, u + 1))
                            act.activation(pr[:, q % 2, h:h + m, 0:w],
                                           ering[u % 3][:, 0:m * w].rearrange("p (h w) -> p h w", w=w),
                                           ACT.Exp).then_inc(s["pexp"], 1)
                    if step == "b31":
                        act.wait_ge(s["pe_pv"], upto("pe_pv", n, 8))
                        act.activation(yT[:, 1, :], ybank[:, :], ACT.Copy).then_inc(s["yT"], 1)
                    if step == "a34":
                        act.wait_ge(s["pe_tail"], upto("pe_tail", n, NTH[step]))
                        act.activation(ynT[:, :], misc[:, :], ACT.Copy).then_inc(s["ynT"], 1)
                    if step == "a36":
                        act.wait_ge(s["x2"], upto("x2", n))
                        act.activation(x2sq[:, :, :], x2[:, :, :], ACT.Square).then_inc(s["x2sq"], 1)
                    if step in ("e0", "e1"):
                        act.wait_ge(s["pe_prep"], upto("pe_prep", n, NTH[step]))
                        act.activation(xf[:, k, :], misc[:, :], ACT.Copy, scale=ln2[:, 0:1]).then_inc(s["xf"], 1)
                    if step in ("e5", "e6"):
                        k = k - 5
                        act.wait_ge(s["cres"], upto("cres", n, k + 1))
                        act.activation(x2p[:, :], xres[:, :], ACT.Copy).then_inc(s["cast2"], 1)
                    if step == "e7":
                        act.wait_ge(s["r_dve"], upto("r_dve", n, 2))
                        act.activation(lg[:, 2, :, :], lg[:, 1, :, :], ACT.Exp).then_inc(s["r_act"], 1)
                    if step == "e3":
                        act.wait_ge(s["pe_prep"], upto("pe_prep", n, NTH[step]))
                        act.activation(wT[0:PIECES * NE, :, :].rearrange("p b t -> p (b t)"),
                                       misc[:, :].bitcast(bf16)[0:PIECES * NE, :], ACT.Copy).then_inc(s["wT"], 1)
                    if step == "h0" or (c == "d" and k < 2 * NJ - 1):
                        for u in ((0,) if c == "h" else (k + 1,)):
                            w = min(P, F - (u // 2) * P)
                            if u >= 2:
                                act.wait_ge(s["hh"], upto("hh", n, u - 1))
                            act.wait_ge(s["pe_h1"], upto("pe_h1", n, u + 1))
                            act.activation(sl[0:w, u % 2, :], h1bank[0:w, :], ACT.Silu).then_inc(s["silu"], 1)
                    if step == "c22":
                        act.wait_ge(s["pe_down"], upto("pe_down", n, NJ))
                        act.activation(moT[:, :], obank[:, :], ACT.Copy).then_inc(s["moT"], 1)

            run(program, act)

        @block.vector
        def _(_e):
            tt, ts, stt = dve.tensor_tensor, dve.tensor_scalar, dve.scalar_tensor_tensor
            steps = 0

            def row(ins):
                nonlocal steps
                steps += 1
                ins.then_inc(rows, 1)
                dve.wait_ge(rows, steps)

            dve.wait_ge(idx_in, 16)
            fx, fn = kT[:, 0:NP * G], qT[:, 0:NP * G]
            row(dve.tensor_copy(out=fx, in_=idx[:, :]))
            row(ts(out=fn, in0=fx, scalar1=0.0, scalar2=float(VOCAB), op0=ALU.is_lt, op1=ALU.mult))
            row(tt(out=fx, in0=fx, in1=fn, op=ALU.add))
            row(ts(out=fx, in0=fx, scalar1=0.0, scalar2=float(VOCAB - 1), op0=ALU.max, op1=ALU.min))
            row(ts(out=fx, in0=fx, scalar1=float(HIDDEN // D), scalar2=float(LAYER), op0=ALU.mult, op1=ALU.add))
            row(dve.tensor_copy(out=idx[:, :], in_=fx))
            assert steps == ROW_STEPS, steps
            dve.wait_ge(w13_in, 32)
            casts = 0

            def link(ins):
                nonlocal casts
                casts += 1
                ins.then_inc(cast, 1)
                dve.wait_ge(cast, casts)

            for m in range(2):
                link(dve.tensor_copy(out=w13[:, m, 0, :], in_=wtmp[:, m, :]))
                link(tt(out=wtmp[:, m, :], in0=wtmp[:, m, :], in1=w13[:, m, 0, :], op=ALU.subtract))
                link(dve.tensor_copy(out=w13[:, m, 1, :], in_=wtmp[:, m, :]))
                link(dve.tensor_copy(out=w13[0:D, m, 2, :], in_=w13[0:D, m, 0, :]))
                link(tt(out=w13[D:P, m, 2, :], in0=wtmp[D:P, m, :], in1=w13[D:P, m, 1, :], op=ALU.subtract))
            dve.wait_ge(loaded, 16 * LOADS)
            link(dve.tensor_copy(out=selg[:, :], in_=selgf))
            link(dve.tensor_copy(out=identb[:, :], in_=ident[:, :]))
            link(dve.tensor_copy(out=maskb[:, :], in_=maskf))
            link(tt(out=bi[:, 0:1], in0=bias[:, 3:4], in1=ibias[:, :], op=ALU.add))
            link(ts(out=bi[:, 0:1], in0=bi[:, 0:1], scalar1=0.1, scalar2=None, op0=ALU.mult))
            link(ts(out=bi[:, 1:2], in0=bias[:, 4:5], scalar1=-1.0, scalar2=None, op0=ALU.mult))
            assert casts == CASTS, casts
            dve.wait_ge(cleared, 9)

            def program(it, stages):
                for step in [x for x in READERS if x[0] in stages]:
                    n = it - SKEW[step[0]]
                    misc = banks[BANK[step]] if step in BANK else None
                    c, k = step[0], int(step[1:])
                    if step == "g1":
                        dve.wait_ge(s["x0"], full("x0", n))
                        dve.tensor_reduce(out=st[:, 6, :], in_=x0[:, :, :], axis=AX, op=ALU.add).then_inc(s["g_sum"], 1)
                        dve.wait_ge(s["g_sum"], upto("g_sum", n))
                        ts(out=st[:, 7, :], in0=st[:, 6, :], scalar1=-1.0 / D, scalar2=None,
                           op0=ALU.mult).then_inc(s["g_nm"], 1)
                        dve.wait_ge(s["g_nm"], upto("g_nm", n))
                        tt(out=xc[:, :, :], in0=x0[:, :, :], in1=bc(st[:, 7, :], D), op=ALU.add).then_inc(s["xc"], 1)
                    if step == "g2":
                        dve.wait_ge(s["xsq"], upto("xsq", n))
                        dve.tensor_reduce(out=st[:, 6, :], in_=xsq[:, :, :], axis=AX,
                                          op=ALU.add).then_inc(s["g_var"], 1)
                        dve.wait_ge(s["g_var"], upto("g_var", n))
                        ts(out=g_tiny[0], in0=st[:, 6, :], scalar1=1.0 / D, scalar2=1e-5, op0=ALU.mult,
                           op1=ALU.add).then_inc(s["g_v"], 1)
                        dve.wait_ge(s["g_v"], upto("g_v", n))
                        rsqrt_guess("g", n, g_tiny)
                    if step == "g6":
                        dve.wait_ge(s["pe_gate"], upto("pe_gate", n, NTH[step]))
                        if later(n):
                            dve.wait_ge(s["hgT"], upto("hgT", n - 1))
                        ts(out=kT[:, :], in0=misc[:, :], scalar1=bias[:, 1:2], scalar2=D ** -0.5, op0=ALU.add,
                           op1=ALU.mult).then_inc(s["kT"], 1)
                    if step == "g11":
                        dve.wait_ge(s["gln"], upto("gln", n))
                        for q, name in ((1, "lf"), (2, "lso")):
                            stt(out=mn[:, q, :], in0=mn[:, q, :], scalar=0.0, in1=ab[:, q, :], op0=ALU.min,
                                op1=ALU.subtract).then_inc(s[name], 1)
                    if step == "g13":
                        dve.wait_ge(s["si"], upto("si", n))
                        ts(out=li[:, :], in0=li[:, :], scalar1=10.0, scalar2=None,
                           op0=ALU.mult).then_inc(s["li"], 1)
                        dve.wait_ge(s["li"], upto("li", n))
                        dve.wait_ge(s["lf"], upto("lf", n))
                        lf = mn[:, 1, :]
                        dve.tensor_tensor_scan(out=mext[:, 1:T + 1], data0=lf, data1=li[:, :], initial=0.0, op0=ALU.add,
                                               op1=ALU.max).then_inc(s["mscan"], 1)
                        dve.wait_ge(s["mscan"], upto("mscan", n))
                        starts = lf.rearrange("p (c l) -> p c l", l=L)[:, :, 0]
                        tt(out=starts, in0=starts, in1=mext[:, 0:T].rearrange("p (c l) -> p c l", l=L)[:, :, 0],
                           op=ALU.add).then_inc(s["lfc"], 1)
                        dve.wait_ge(s["lfc"], upto("lfc", n))
                        dve.tensor_tensor_scan(out=gcum[:, :], data0=restart[:, :], data1=lf, initial=0.0,
                                               op0=ALU.mult, op1=ALU.add).then_inc(s["gcum"], 1)
                        dve.wait_ge(s["gcum"], upto("gcum", n))
                        dve.wait_ge(s["so"], upto("so", n))
                        tt(out=mn[:, 0, :], in0=gcum[:, :], in1=mext[:, 1:T + 1], op=ALU.subtract).then_inc(s["aw"], 1)
                        tt(out=mn[:, 2, :], in0=li[:, :], in1=gcum[:, :], op=ALU.subtract).then_inc(s["ae"], 1)
                    if step == "g15":
                        dve.wait_ge(s["pe_gate"], upto("pe_gate", n, NTH[step]))
                        dve.wait_ge(s["eexp"], upto("eexp", n))
                        stt(out=uT[:, :], in0=misc[:, :], scalar=bias[:, 2:3], in1=eexp[:, :], op0=ALU.add,
                            op1=ALU.mult).then_inc(s["uT"], 1)
                        dve.wait_ge(s["wexp"], upto("wexp", n))
                        wd = wdec[:, :].rearrange("p (c l) -> p c l", l=L)[:, 1:NC, 0]
                        dve.tensor_copy(out=wd, in_=wend[:, 0:NC - 1]).then_inc(s["wdec"], 1)
                    if step == "g16":
                        dve.wait_ge(s["wdec"], upto("wdec", n))
                        dve.wait_ge(s["ek"], upto("ek", n))
                        dve.tensor_tensor_scan(out=nst[:, :], data0=wdec[:, :], data1=ek[:, :], initial=0.0,
                                               op0=ALU.mult, op1=ALU.add).then_inc(s["nst"], 1)
                    if step in ("m2", "m3"):
                        b = k - 2
                        dve.wait_ge(s["pe_mem"], upto("pe_mem", n, NTH[step]))
                        tt(out=atm[:, b, :].rearrange("p (t q) -> p t q", q=P),
                           in0=misc[:, :].rearrange("p (t q) -> p t q", q=P),
                           in1=chunkmask[:, :].unsqueeze(1).to_broadcast([P, NT, P]), op=ALU.mult).then_inc(s["atm"], 1)
                    if step in ("m4", "m5"):
                        par = k - 4
                        q = NT - par
                        dve.wait_ge(s["pe_mem"], upto("pe_mem", n, NTH[step]))
                        tt(out=dlt[:, :, :].rearrange("p (q a) d -> p q a d", a=2)[:, 0:q, par, :],
                           in0=misc[:, 0:q * P].rearrange("p (q d) -> p q d", d=P),
                           in1=batchmask[:, :].unsqueeze(1).to_broadcast([P, q, P]), op=ALU.mult).then_inc(s["dlt"], 1)
                    if step in ("m6", "m18", "m19"):
                        dve.wait_ge(s["dltw"], upto("dltw", n))
                        part = ("m6", "m18", "m19").index(step)
                        for j in range(2 * part + 1, 2 * part + 3):
                            if j > 1:
                                dve.wait_ge(s["state"], upto("state", n, j - 1))
                            stt(out=dlt[:, j, :], in0=dlt[:, j - 1, :], scalar=wend[:, j:j + 1], in1=dlt[:, j, :],
                                op0=ALU.mult, op1=ALU.add).then_inc(s["state"], 1)
                    if step == "m9":
                        dve.wait_ge(s["pe_mem"], upto("pe_mem", n, NTH[step]))
                        dve.wait_ge(s["hw"], upto("hw", n))
                        tt(out=hgT[:, :], in0=misc[:, :], in1=hw[:, :], op=ALU.mult).then_inc(s["hgT"], 1)
                    if step == "m12":
                        dve.wait_ge(s["dabs"], upto("dabs", n))
                        ts(out=mt[:, 18, :], in0=mt[:, 18, :], scalar1=1e-6, scalar2=None,
                           op0=ALU.max).then_inc(s["den"], 1)
                        dve.wait_ge(s["den"], upto("den", n))
                        dve.reciprocal(out=mt[:, 19, :], in_=mt[:, 18, :]).then_inc(s["rd"], 1)
                        dve.wait_ge(s["rd"], upto("rd", n))
                        tt(out=mt[:, 20, :], in0=mt[:, 19, :], in1=mt[:, 19, :], op=ALU.mult).then_inc(s["rd2"], 1)
                    if step == "m13":
                        dve.wait_ge(s["rd2"], upto("rd2", n))
                        dve.wait_ge(s["hsq"], upto("hsq", n))
                        dve.tensor_reduce(out=mt[:, 21, :], in_=hsq[:, :, :], axis=AX,
                                          op=ALU.add).then_inc(s["hsum"], 1)
                        dve.wait_ge(s["hsum"], upto("hsum", n))
                        stt(out=mt[:, 22, :], in0=mt[:, 21, :], scalar=1.0 / D, in1=mt[:, 20, :], op0=ALU.mult,
                            op1=ALU.mult).then_inc(s["hms"], 1)
                        dve.wait_ge(s["hms"], upto("hms", n))
                        ts(out=mh_tiny[0], in0=mt[:, 22, :], scalar1=1e-8, scalar2=None,
                           op0=ALU.add).then_inc(s["mh_v"], 1)
                        dve.wait_ge(s["mh_v"], upto("mh_v", n))
                        rsqrt_guess("mh", n, mh_tiny)
                    if step == "m14":
                        dve.wait_ge(s["mh_newton"], full("mh_newton", n))
                        tt(out=mt[:, 23, :], in0=mt[:, 19, :], in1=mh_tiny[4], op=ALU.mult).then_inc(s["hf"], 1)
                    if step == "m15":
                        dve.wait_ge(s["h1"], upto("h1", n))
                        dve.tensor_reduce(out=mt[:, 18, :], in_=h1[:, :, :], axis=AX,
                                          op=ALU.add).then_inc(s["m_sum"], 1)
                        dve.wait_ge(s["m_sum"], upto("m_sum", n))
                        ts(out=mt[:, 20, :], in0=mt[:, 18, :], scalar1=-1.0 / D, scalar2=None,
                           op0=ALU.mult).then_inc(s["m_nm"], 1)
                        dve.wait_ge(s["m_nm"], upto("m_nm", n))
                        tt(out=hc[:, :, :], in0=h1[:, :, :], in1=bc(mt[:, 20, :], D), op=ALU.add).then_inc(s["hc"], 1)
                    if step == "m16":
                        dve.wait_ge(s["hsq2"], upto("hsq2", n))
                        dve.tensor_reduce(out=mt[:, 21, :], in_=hsq[:, :, :], axis=AX,
                                          op=ALU.add).then_inc(s["m_var"], 1)
                        dve.wait_ge(s["m_var"], upto("m_var", n))
                        ts(out=ml_tiny[0][:, 0:G], in0=mt[:, 21, :], scalar1=1.0 / D, scalar2=1e-5, op0=ALU.mult,
                           op1=ALU.add).then_inc(s["ml_v"], 1)
                        ts(out=ml_tiny[0][:, G:2 * G], in0=mt[:, 21, :], scalar1=(1.0 + 1e-6) / D, scalar2=1e-11,
                           op0=ALU.mult, op1=ALU.add).then_inc(s["mr_v"], 1)
                        dve.wait_ge(s["ml_v"], upto("ml_v", n))
                        dve.wait_ge(s["mr_v"], upto("mr_v", n))
                        rsqrt_guess("ml", n, ml_tiny)
                    if step == "m17":
                        dve.wait_ge(s["ml_newton"], full("ml_newton", n))
                        if later(n):
                            dve.wait_ge(s["hnT"], upto("hnT", n - 1))
                        tt(out=hn[:, :, :], in0=hc[:, :, :], in1=bc(ml_tiny[4][:, G:2 * G], D),
                           op=ALU.mult).then_inc(s["hn"], 1)
                    if step in ("q1", "q2", "q3"):
                        dve.wait_ge(s["pe_qk"], upto("pe_qk", n, NTH[step]))
                        if k in (1, 3) and later(n):
                            dve.wait_ge(s["p2"], full("p2", n - 1))
                            dve.wait_ge(s["p3"], full("p3", n - 1))
                        if k == 1:
                            tt(out=t1[:, 0, :], in0=misc[:, :], in1=ropeq[:, 0, :], op=ALU.mult).then_inc(s["t1"], 1)
                        if k == 2:
                            tt(out=t2[:, 0, :], in0=misc[:, :], in1=ropeq[:, 1, :], op=ALU.mult).then_inc(s["t2"], 1)
                        if k == 3:
                            tt(out=t1[0:D, 1, :], in0=misc[0:D, :], in1=ropek[0:D, :], op=ALU.mult).then_inc(s["t1"], 1)
                            tt(out=t2[0:D, 1, :], in0=misc[D:P, :], in1=ropek[D:P, :], op=ALU.mult).then_inc(s["t2"], 1)
                    if c == "b" and 6 <= k <= 21:
                        for u, (_, b, t, h, m) in [x for x in enumerate(MAXIMA) if x[1][0] == step]:
                            w = (t + 1) * P
                            dve.wait_ge(s["pe_s"], upto("pe_s", n, u + 1))
                            dve.tensor_reduce(out=nm[:, t, b * NH + h:b * NH + h + m],
                                              in_=sring[u % 2][:, 0:m * w].rearrange("p (h w) -> p h w", w=w),
                                              axis=AX, op=ALU.max, negate=True).then_inc(s["smax"], 1)
                    if step == "b43":
                        dve.wait_ge(s["smax"], full("smax", n))
                        if later(n):
                            dve.wait_ge(s["mrow"], upto("mrow", n - 1))
                        dve.tensor_copy(out=mp[:, :, 0, :], in_=nm[:, :, :]).then_inc(s["mp"], 1)
                        dve.wait_ge(s["mp"], upto("mp", n, 1))
                        tt(out=nmr[:, :, :], in0=nm[:, :, :], in1=mp[:, :, 0, :], op=ALU.subtract).then_inc(s["mp"], 1)
                        dve.wait_ge(s["mp"], upto("mp", n, 2))
                        dve.tensor_copy(out=mp[:, :, 1, :], in_=nmr[:, :, :]).then_inc(s["mp"], 1)
                        dve.wait_ge(s["mp"], upto("mp", n, 3))
                        tt(out=mp[:, :, 2, :], in0=nmr[:, :, :], in1=mp[:, :, 1, :],
                           op=ALU.subtract).then_inc(s["mp"], 2)
                    if step in ("a32", "a33"):
                        b = k - 32
                        dve.wait_ge(s["pe_tail"], upto("pe_tail", n, NTH[step]))
                        if later(n):
                            dve.wait_ge(s["ynT"], upto("ynT", n - 1))
                        y = misc[:, :].rearrange("p (g d) -> p g d", d=32)
                        dve.reciprocal(out=rden[:, b, :], in_=y[:, :, HD]).then_inc(s["rden"], 1)
                        dve.wait_ge(s["rden"], upto("rden", n, b + 1))
                        for t in range(NT):
                            r = slice(t * NH, (t + 1) * NH)
                            last = tt(out=yn[:, t, b, :, :], in0=y[:, r, 0:HD], in1=bc(rden[:, b, r], HD), op=ALU.mult)
                        last.then_inc(s["yn"], 1)
                    if step == "a35":
                        dve.wait_ge(s["pe_tail"], upto("pe_tail", n, NTH[step]))
                        y = misc[:, :].rearrange("p (g d) -> p g d", d=D)
                        dve.wait_ge(s["y0b"], upto("y0b", n))
                        tt(out=x2[:, :, :], in0=y, in1=y0b[:, :, :], op=ALU.add).then_inc(s["x2"], 1)
                        dve.wait_ge(s["hy"], upto("hy", n))
                        if later(n):
                            dve.wait_ge(s["hxc"], upto("hxc", n - 1))
                        tt(out=hx[:, :, :], in0=y, in1=hy[:, :, :], op=ALU.add).then_inc(s["hx"], 1)
                    if step == "a37":
                        dve.wait_ge(s["x2sq"], upto("x2sq", n))
                        dve.tensor_reduce(out=bt[:, 5, :], in_=x2sq[:, :, :], axis=AX,
                                          op=ALU.add).then_inc(s["b_var"], 1)
                        dve.wait_ge(s["b_var"], upto("b_var", n))
                        ts(out=b_tiny[0], in0=bt[:, 5, :], scalar1=1.0 / D, scalar2=1e-6, op0=ALU.mult,
                           op1=ALU.add).then_inc(s["b_v"], 1)
                        dve.wait_ge(s["b_v"], upto("b_v", n))
                        rsqrt_guess("b", n, b_tiny)
                    if step == "e4":
                        dve.wait_ge(s["hx"], upto("hx", n))
                        if later(n):
                            dve.wait_ge(s["out"], full("out", n - 1))
                        dve.tensor_copy(out=ot[:, :, :], in_=hx[:, :, :]).then_inc(s["hxc"], 1)
                    if step in ("e9", "e10"):
                        k = k - 9
                        dve.wait_ge(s["xf"], upto("xf", n, k + 1))
                        if k == 0 and later(n):
                            dve.wait_ge(s["pe_h3"], full("pe_h3", n - 1))
                        dve.tensor_copy(out=xa[0:D, k, :], in_=xf[0:D, k, :]).then_inc(s["cast1"], 1)
                        dve.tensor_copy(out=xb[D:P, k, :], in_=xf[D:P, k, :]).then_inc(s["cast1"], 1)
                        dve.wait_ge(s["cast1"], upto("cast1", n, 2 * k + 2))
                        tt(out=xa[D:P, k, :], in0=xf[D:P, k, :], in1=xb[D:P, k, :],
                           op=ALU.subtract).then_inc(s["xahi"], 1)
                    if step == "e2":
                        dve.wait_ge(s["pe_prep"], upto("pe_prep", n, NTH[step]))
                        dve.tensor_copy(out=lg[:, 0, :, :].rearrange("p g e -> p (g e)"),
                                        in_=misc[:, 0:G * NE]).then_inc(s["lg"], 1)
                        dve.wait_ge(s["lg"], upto("lg", n))
                    if step in ("e2", "e8", "e11", "e12"):
                        done = {"e2": 0, "e8": 2, "e11": 11, "e12": 17}[step]

                        def link(ins):
                            nonlocal done
                            done += 1
                            ins.then_inc(s["r_dve"], 1)
                            dve.wait_ge(s["r_dve"], upto("r_dve", n, done))

                        def most(q, src):
                            link(dve.tensor_reduce(out=r[q], in_=src, axis=AX, op=ALU.max))

                        x, r = [lg[:, q, :, :] for q in range(15)], [ls[:, q, :] for q in range(12)]
                        order = rev[:, :].unsqueeze(1).to_broadcast([P, G, NE])
                    if step == "e2":
                        most(0, x[0])
                        link(tt(out=x[1], in0=x[0], in1=bc(r[0], NE), op=ALU.subtract))
                    if step == "e8":
                        dve.wait_ge(s["r_act"], upto("r_act", n))
                        link(dve.tensor_reduce(out=r[1], in_=x[2], axis=AX, op=ALU.add))
                        link(dve.reciprocal(out=r[2], in_=r[1]))
                        link(tt(out=x[3], in0=x[2], in1=bc(r[2], NE), op=ALU.mult))
                        most(3, x[3])
                        link(tt(out=x[4], in0=x[3], in1=bc(r[3], NE), op=ALU.is_equal))
                        link(tt(out=x[5], in0=x[4], in1=order, op=ALU.mult))
                        most(4, x[5])
                        link(tt(out=x[6], in0=x[5], in1=bc(r[4], NE), op=ALU.is_equal))
                        link(stt(out=x[7], in0=x[6], scalar=-2.0, in1=x[3], op0=ALU.mult, op1=ALU.add))
                    if step == "e11":
                        most(5, x[7])
                        link(tt(out=x[8], in0=x[7], in1=bc(r[5], NE), op=ALU.is_equal))
                        link(tt(out=x[9], in0=x[8], in1=order, op=ALU.mult))
                        most(6, x[9])
                        link(tt(out=x[10], in0=x[9], in1=bc(r[6], NE), op=ALU.is_equal))
                        link(tt(out=x[11], in0=x[6], in1=x[10], op=ALU.add))
                    if step == "e12":
                        link(tt(out=x[12], in0=x[11], in1=x[3], op=ALU.mult))
                        link(stt(out=r[7], in0=r[3], scalar=1e-9, in1=r[5], op0=ALU.add, op1=ALU.add))
                        link(dve.reciprocal(out=r[8], in_=r[7]))
                        link(tt(out=x[13], in0=x[12], in1=bc(r[8], NE), op=ALU.mult))
                        assert done == PER["r_dve"], done
                        if later(n):
                            dve.wait_ge(s["wT"], upto("wT", n - 1))
                        dve.tensor_copy(out=wp[:, :, 0, :], in_=x[13]).then_inc(s["wp"], 1)
                        dve.wait_ge(s["wp"], upto("wp", n, 1))
                        tt(out=x[14], in0=x[13], in1=wp[:, :, 0, :], op=ALU.subtract).then_inc(s["wp"], 1)
                        dve.wait_ge(s["wp"], upto("wp", n, 2))
                        dve.tensor_copy(out=wp[:, :, 1, :], in_=x[14]).then_inc(s["wp"], 1)
                        dve.wait_ge(s["wp"], upto("wp", n, 3))
                        tt(out=wp[:, :, 2, :], in0=x[14], in1=wp[:, :, 1, :], op=ALU.subtract).then_inc(s["wp"], 2)
                    if step == "c0" or (c == "d" and k < 2 * NJ - 1):
                        u = 0 if c == "c" else k + 1
                        w = min(P, F - (u // 2) * P)
                        dve.wait_ge(s["silu"], upto("silu", n, u + 1))
                        dve.wait_ge(s["pe_g"], upto("pe_g", n, u + 1))
                        tt(out=sgt[0:w, u % 2, :], in0=gbank[0:w, :], in1=sl[0:w, u % 2, :],
                           op=ALU.mult).then_inc(s["gated"], 1)
                    if c == "c" and k < 2 * NJ:
                        j, b, u = k // 2, k % 2, k
                        w = min(P, F - j * P)
                        dve.wait_ge(s["gated"], upto("gated", n, u + 1))
                        dve.wait_ge(s["pe_h3"], upto("pe_h3", n, u + 1))
                        if j >= 2:
                            dve.wait_ge(s["pe_down"], upto("pe_down", n, j - 1))
                        tt(out=hh[0:w, j % 2, b, :], in0=h3bank[0:w, :], in1=sgt[0:w, b, :],
                           op=ALU.mult).then_inc(s["hh"], 1)
                    if step == "c23":
                        dve.wait_ge(s["pe_moe"], upto("pe_moe", n, NTH[step]))
                        dve.wait_ge(s["hxc"], upto("hxc", n))
                        tt(out=ot[:, :, :].rearrange("p g d -> p (g d)"), in0=misc[:, :],
                           in1=ot[:, :, :].rearrange("p g d -> p (g d)"), op=ALU.add).then_inc(s["ot"], 1)

            run(program, dve)

        @block.gpsimd
        def _(_e):
            tt = pool.tensor_tensor
            presets = 0
            for ap, v in ((qs[96:P, :, :], 0.0), (ks[96:P, :, :], 0.0), (va[:, :, :, :], 0.0), (wT[:, :, :], 0.0),
                          (wdec[:, :], 1.0), (mext[:, 0:1], 0.0), (half3[:, :], 1.5),
                          (ks[96:96 + PIECES, :, :], 1.0), (va[:, :, :, HD:HD + 1], 1.0)):
                presets += 1
                pool.memset(ap, v).then_inc(cleared, 1)
                pool.wait_ge(cleared, presets)
            pool.wait_ge(loaded, 16 * LOADS)
            pool.wait_ge(rows, ROW_STEPS)

            def program(it, stages):
                for step in [x for x in READERS if x[0] in stages]:
                    n = it - SKEW[step[0]]
                    misc = banks[BANK[step]] if step in BANK else None
                    if step == "f0":
                        if later(n):
                            pool.wait_ge(s["x0"], full("x0", n - 1))
                        pool.tensor_copy(out=idxc[:, :], in_=idx[:, bass.ds(n * G, G)]).then_inc(s["idxc"], 1)
                        pool.wait_ge(s["idxc"], upto("idxc", n))
                        if later(n):
                            pool.wait_ge(s["xm"], upto("xm", n - 1))
                        if later(n):
                            pool.wait_ge(s["xc"], upto("xc", n - 1))
                        tt(out=pad[:, 0:1], in0=nscale[:, 0:1], in1=nscale[:, 0:1], op=ALU.mult)
                        for g in range(G):
                            pool.indirect_dma_start(
                                out=x0[:, g, :], out_offset=None, in_=a["table"],
                                in_offset=bass.IndirectOffsetOnAxis(ap=idxc[:, g:g + 1], axis=0)).then_inc(s["x0"], 16)
                    if step == "g2":
                        newton("g", n, g_tiny)
                    if step == "g15":
                        pool.wait_ge(s["eexp"], upto("eexp", n))
                        pool.wait_ge(s["kT"], upto("kT", n))
                        tt(out=ek[:, :], in0=eexp[:, :], in1=kT[:, :], op=ALU.mult).then_inc(s["ek"], 1)
                        pool.wait_ge(s["qT"], upto("qT", n))
                        tt(out=wqx[:, :], in0=wexp[:, :], in1=qT[:, :], op=ALU.mult).then_inc(s["wqx"], 1)
                        pool.wait_ge(s["so"], upto("so", n))
                        tt(out=hw[:, :], in0=wexp[:, :], in1=ab[:, 2, :], op=ALU.mult).then_inc(s["hw"], 1)
                    if step == "g16":
                        pool.wait_ge(s["wqx"], upto("wqx", n))
                        pool.wait_ge(s["nst"], upto("nst", n))
                        tt(out=prod[:, :], in0=nst[:, :], in1=wqx[:, :], op=ALU.mult).then_inc(s["prod"], 1)
                    if step == "g3":
                        pool.wait_ge(s["g_newton"], full("g_newton", n))
                        pool.wait_ge(s["xsq"], upto("xsq", n))
                        tt(out=xn[:, :, :], in0=xc[:, :, :], in1=bc(g_tiny[4], D), op=ALU.mult).then_inc(s["xn"], 1)
                    if step == "m5":
                        pool.wait_ge(s["dlt"], full("dlt", n))
                        tt(out=dlt[:, 0:NC - 1, :], in0=dlt[:, 0:NC - 1, :], in1=bc(wend[:, 0:NC - 1], P),
                           op=ALU.mult).then_inc(s["dltw"], 1)
                    if step == "m13":
                        newton("mh", n, mh_tiny)
                    if step == "m16":
                        newton("ml", n, ml_tiny)
                    if step == "a38":
                        pool.wait_ge(s["b_newton"], full("b_newton", n))
                        pool.wait_ge(s["x2"], upto("x2", n))
                        if later(n):
                            pool.wait_ge(s["xf"], full("xf", n - 1))
                        for q in range(2):
                            last = tt(out=fl[:, :, q, :], in0=x2[:, :, :], in1=bc(b_tiny[4], D), op=ALU.mult)
                        last.then_inc(s["fl"], 1)
                    if step == "a37":
                        newton("b", n, b_tiny)
                    if step == "m14":
                        pool.wait_ge(s["hf"], upto("hf", n))
                        pool.wait_ge(s["hsq"], upto("hsq", n))
                        tt(out=ho[:, :, :], in0=ht[:, :, :], in1=bc(mt[:, 23, :], D), op=ALU.mult).then_inc(s["ho"], 1)
                        pool.wait_ge(s["ho"], upto("ho", n))
                        tt(out=ho[:, :, :], in0=ho[:, :, :], in1=nscale[:, :].unsqueeze(1).to_broadcast([P, G, D]),
                           op=ALU.mult).then_inc(s["hos"], 1)
                        pool.wait_ge(s["hos"], upto("hos", n))
                        if later(n):
                            pool.wait_ge(s["hy"], upto("hy", n - 1))
                        tt(out=h1[:, :, :], in0=ho[:, :, :], in1=xr[:, :, :], op=ALU.add).then_inc(s["h1"], 1)
                    if step == "m17":
                        if later(n):
                            pool.wait_ge(s["y0b"], upto("y0b", n - 1))
                        pool.wait_ge(s["hc"], upto("hc", n))
                        pool.wait_ge(s["ml_newton"], full("ml_newton", n))
                        tt(out=y0[:, :, :], in0=hc[:, :, :], in1=bc(ml_tiny[4][:, 0:G], D),
                           op=ALU.mult).then_inc(s["y0"], 1)
                    if step == "b42":
                        pool.wait_ge(s["y0"], upto("y0", n))
                        if later(n):
                            pool.wait_ge(s["hx"], upto("hx", n - 1))
                        tt(out=hy[:, :, :], in0=h1[:, :, :], in1=y0[:, :, :], op=ALU.add).then_inc(s["hy"], 1)
                        pool.tensor_copy(out=y0b[:, :, :], in_=y0[:, :, :]).then_inc(s["y0b"], 1)
                    if step in ("q2", "q4"):
                        x, rows = (0, P) if step == "q2" else (1, D)
                        pool.wait_ge(s["t2"], upto("t2", n, x + 1))
                        tt(out=qr[0:rows, x, :], in0=t1[0:rows, x, :], in1=t2[0:rows, x, :],
                           op=ALU.add).then_inc(s["qr"], 1)
                    if step in ("b38", "b39"):
                        x, rows, dst = (0, P, qp) if step == "b38" else (1, D, kp)
                        pool.wait_ge(s["p1"], upto("p1", n, x + 1))
                        tt(out=t1[0:rows, x, :], in0=qr[0:rows, x, :], in1=dst[0:rows, 0, :],
                           op=ALU.subtract).then_inc(s["r1"], 1)
                    if step in ("b40", "b41"):
                        x, rows, dst = (0, P, qp) if step == "b40" else (1, D, kp)
                        pool.wait_ge(s["p2"], upto("p2", n, x + 1))
                        tt(out=dst[0:rows, 2, :], in0=t1[0:rows, x, :], in1=dst[0:rows, 1, :],
                           op=ALU.subtract).then_inc(s["p3"], 1)
                    if step == "e9":
                        if later(n):
                            pool.wait_ge(s["xblo"], full("xblo", n - 1))
                        pool.wait_ge(s["cast1"], upto("cast1", n, 1))
                        tt(out=xres[:, :], in0=xf[0:D, 0, :], in1=xa[0:D, 0, :], op=ALU.subtract).then_inc(s["cres"], 1)
                    if step in ("e5", "e6"):
                        k = int(step[1:]) - 5
                        pool.wait_ge(s["cast2"], upto("cast2", n, k + 1))
                        tt(out=xb[0:D, k, :], in0=xres[:, :], in1=x2p[:, :], op=ALU.subtract).then_inc(s["xblo"], 1)
                        if k == 0:
                            pool.wait_ge(s["xblo"], upto("xblo", n, 1))
                            pool.wait_ge(s["cast1"], upto("cast1", n, 3))
                            tt(out=xres[:, :], in0=xf[0:D, 1, :], in1=xa[0:D, 1, :],
                               op=ALU.subtract).then_inc(s["cres"], 1)

            run(program, pool)
    return nc


def _host(x):
    def bd(w):
        z = np.zeros((2 * w.shape[0], 2 * w.shape[1]), np.float32)
        z[:w.shape[0], :w.shape[1]] = w
        z[w.shape[0]:, w.shape[1]:] = w
        return z

    def twice(v):
        return np.ascontiguousarray(np.tile(np.reshape(v, (-1, 1)), (2, 1)))

    h = {}
    r = np.arange(P)
    h["ident"] = np.eye(P, dtype=np.float32)
    up = np.where(r[None, :] > r[:, None], np.float32(NEG), np.float32(0))
    h["maskf"] = np.concatenate([up, up.T], 1)
    h["chunkmask"] = ((r[:, None] <= r[None, :]) & (r[:, None] // L == r[None, :] // L)).astype(np.float32)
    h["batchmask"] = (r[:, None] // D == r[None, :] // D).astype(np.float32)
    h["restart"] = np.tile((np.arange(T) % L != 0).astype(np.float32), (P, 1))
    h["onesbd"] = (r[:, None] // D == np.arange(2)[None, :]).astype(np.float32)
    h["rev"] = np.tile(NE - np.arange(NE, dtype=np.float32), (P, 1))
    Wg, bg = x["L0_attn_Wg"], x["L0_attn_bg"]
    ws = [x["L0_attn_Wq"], x["L0_attn_Wk"], x["L0_attn_Wv"], Wg[:, :D], Wg[:, D:2 * D], Wg[:, 2 * D:]]
    bs = [x["L0_attn_bq"], x["L0_attn_bk"], x["L0_attn_bv"], bg[:D], bg[D:2 * D], bg[2 * D:]]
    h["proj"] = np.stack([bd(w) for w in ws], 1)
    h["bias"] = np.concatenate([twice(b) for b in bs], 1)
    h["ibias"] = twice(x["L0_attn_input_bias"])
    h["nscale"] = np.tile(x["L0_attn_norm_scale"], (P, 1))
    h["ln1"], h["ln2"] = twice(x["L0_ffn_ln1_w"]), twice(x["L0_ffn_ln2_w"])

    swap = (np.arange(HD) + HD // 2) % HD

    def heads(w, n, order):
        w = np.transpose(np.reshape(w, (n, HD, D))[:, order, :], (2, 1, 0))
        z = np.zeros((2, D, HD, 2, n), np.float32)
        z[0, :, :, 0, :] = w
        z[1, :, :, 1, :] = w
        return np.reshape(z, (P, HD * 2 * n))

    same = np.arange(HD)
    h["wq"] = np.stack([heads(x["L0_ffn_wq"], NH, same), heads(x["L0_ffn_wq"], NH, swap)], 1)
    h["wk"] = np.concatenate([heads(x["L0_ffn_wk"], NKV, same), heads(x["L0_ffn_wk"], NKV, swap)], 1)
    h["wv"] = bd(np.transpose(x["L0_ffn_wv"]))
    h["wo"] = bd(np.transpose(x["L0_ffn_wo"]))
    inv = 1.0 / 10000.0 ** (np.arange(0, HD, 2, dtype=np.float32) / HD)
    ang = np.outer(np.arange(T, dtype=np.float32), inv)
    ang = np.concatenate([ang, ang], -1).T
    sign = np.where(np.arange(HD) < HD // 2, -1.0, 1.0)[:, None]
    cs = np.stack([np.cos(ang), np.sin(ang) * sign], 1).astype(np.float32)
    h["ropeq"] = np.repeat(cs * np.float32(HD ** -0.5), 2 * NH, 0)
    h["ropek"] = np.concatenate([np.repeat(cs[:, 0], 2 * NKV, 0), np.repeat(cs[:, 1], 2 * NKV, 0)], 0)
    h["rw"] = np.concatenate([np.transpose(x["L0_ffn_router_w"]), np.zeros((D, NE), np.float32)], 0)
    for name in ("w1", "w3"):
        w = np.reshape(np.transpose(x["L0_ffn_" + name], (2, 0, 1)), (D, F))
        h[name] = np.concatenate([w, w], 0)
    w = np.zeros((NJ * P, D), np.float32)
    w[:F] = np.reshape(np.transpose(x["L0_ffn_w2"], (0, 2, 1)), (F, D))
    h["w2"] = np.transpose(np.reshape(w, (NJ, P, D)), (1, 0, 2))
    z = np.zeros((P, NJ * P), np.float32)
    for p in range(PIECES):
        for e in range(NE):
            z[p * NE + e, e * HID:(e + 1) * HID] = 1.0
    h["selg"] = z
    h["idx"] = np.reshape(np.transpose(np.reshape(x["x"], (NP, 2, NT, P)), (3, 0, 2, 1)), (P, NP * G))
    h["table"] = np.reshape(x["L0_tok_ple_table"], (VOCAB * HIDDEN // D, D))
    return {k: np.ascontiguousarray(v) for k, v in h.items()}


def kernel(**inputs):
    import concourse.bacc as bacc
    from concourse.bass_utils import run_bass_kernel_spmd

    arrays = _host({k: np.asarray(v) for k, v in inputs.items()})
    nc = bacc.Bacc("TRN2", target_bir_lowering=False, num_devices=1)
    a = {k: nc.dram_tensor("in_" + k, v.shape, mybir.dt.from_np(v.dtype), kind="ExternalInput").ap()
         for k, v in arrays.items()}
    a["out"] = nc.dram_tensor("out", (B, T, D), mybir.dt.float32, kind="ExternalOutput").ap()
    tower(nc, a)
    r = run_bass_kernel_spmd(nc, [{"in_" + k: v for k, v in arrays.items()}], core_ids=[0])
    return r.results[0]["out"]
```
